# Optimizing a Trainium2 kernel written in Bass

```python
import numpy as np
import jax
import jax.numpy as jnp

def _softmax(x, axis=-1):
    return jax.nn.softmax(x, axis=axis)

def _gelu(x):
    return jax.nn.gelu(x, approximate=True)

def _silu(x):
    return jax.nn.silu(x)

def _sigmoid(x):
    return jax.nn.sigmoid(x)

def _layernorm(x, axis=-1, eps=1e-05):
    m = jnp.mean(x, axis=axis, keepdims=True)
    v = jnp.var(x, axis=axis, keepdims=True)
    return (x - m) / jnp.sqrt(v + eps)

def _scatter_add(tgt, idx, src, axis=0):
    return tgt.at[idx].add(src)

def _segment_sum(src, seg, n):
    return jax.ops.segment_sum(src, seg, n)
kernel_name = 'mk_macaron_d1_jaxref_r8_a2d548'

def setup_inputs(seed: int=0):
    np.random.seed(seed)
    _w = jnp.asarray

    def _L0_attn_setup():
        import jax, jax.numpy as jnp
        import numpy as np
        import math
        D_MODEL = 128
        NUM_HEADS = 16
        HEAD = D_MODEL // NUM_HEADS
        EPS = 1e-05

        def _layernorm(x, w, b):
            mean = jnp.mean(x, axis=-1, keepdims=True)
            var = jnp.var(x, axis=-1, keepdims=True)
            return (x - mean) * w / jnp.sqrt(var + EPS) + b
        key = jax.random.key(seed)
        ks = jax.random.split(key, 5)
        x = jax.random.normal(ks[0], (2, 256, D_MODEL), dtype=jnp.float32)
        wq = jax.random.uniform(ks[1], (NUM_HEADS, D_MODEL, HEAD), dtype=jnp.float32) * 0.02
        wk = jax.random.uniform(ks[2], (NUM_HEADS, D_MODEL, HEAD), dtype=jnp.float32) * 0.02
        wv = jax.random.uniform(ks[3], (NUM_HEADS, D_MODEL, HEAD), dtype=jnp.float32) * 0.02
        wo = jax.random.uniform(ks[4], (D_MODEL, D_MODEL), dtype=jnp.float32) * 0.02
        ln_w = jnp.ones((D_MODEL,), dtype=jnp.float32)
        ln_b = jnp.zeros((D_MODEL,), dtype=jnp.float32)
        return {'x': x, 'ln_w': ln_w, 'ln_b': ln_b, 'wq': wq, 'wk': wk, 'wv': wv, 'wo': wo}
    _L0_attn_in = _L0_attn_setup()

    def _L0_ffn_setup():
        import jax, jax.numpy as jnp
        import numpy as np
        S_LEN, BATCH, HIDDEN = (256, 2, 128)
        N_HEADS, N_KV = (16, 8)
        N_EXP, TOP_K, CAP_F = (8, 2, 1.25)
        FFN = 512
        HEAD_DIM = HIDDEN // N_HEADS
        Q_PER_KV = N_HEADS // N_KV
        EPS = 1e-05
        NEG = -1000000000.0

        def _ln(x, w, b):
            mu = jnp.mean(x, -1, keepdims=True)
            var = jnp.var(x, -1, keepdims=True)
            return (x - mu) * jax.lax.rsqrt(var + EPS) * w + b

        def _forward(hidden_states, ln1_weight, ln1_bias, ln2_weight, ln2_bias, qkv_weight, proj_weight, router_weight, moe_w1, moe_w2):
            S, B, H = hidden_states.shape
            ln1 = _ln(hidden_states, ln1_weight, ln1_bias)
            qkv = (ln1 @ qkv_weight.T).reshape(S, B, N_KV, (Q_PER_KV + 2) * HEAD_DIM)
            q_dim = Q_PER_KV * HEAD_DIM
            q = qkv[..., :q_dim].reshape(S, B, N_HEADS, HEAD_DIM)
            k = jnp.repeat(qkv[..., q_dim:q_dim + HEAD_DIM], Q_PER_KV, axis=2)
            v = jnp.repeat(qkv[..., q_dim + HEAD_DIM:], Q_PER_KV, axis=2)
            scores = jnp.einsum('sbhd,tbhd->bhst', q, k) / jnp.sqrt(jnp.float32(HEAD_DIM))
            causal = jnp.tril(jnp.ones((S, S), bool))
            attn = jax.nn.softmax(jnp.where(causal[None, None], scores, NEG), axis=-1)
            attn_out = jnp.einsum('bhst,tbhd->sbhd', attn, v).reshape(S, B, H)
            hidden_after_attn = hidden_states + attn_out @ proj_weight.T
            x = _ln(hidden_after_attn, ln2_weight, ln2_bias).reshape(-1, H)
            N = S * B
            probs = jax.nn.softmax(x.astype(jnp.float32) @ router_weight, axis=-1)
            top_p, top_i = jax.lax.top_k(probs, TOP_K)
            top_p = top_p / jnp.sum(top_p, -1, keepdims=True)
            flat_exp = top_i.reshape(-1)
            order = jnp.argsort(flat_exp)
            sorted_exp = flat_exp[order]
            counts = jnp.bincount(sorted_exp, length=N_EXP)
            offsets = jnp.concatenate([jnp.zeros((1,), counts.dtype), jnp.cumsum(counts)])
            within = jnp.arange(N * TOP_K) - offsets[sorted_exp]
            cap = int(np.ceil(N * TOP_K / N_EXP * CAP_F))
            keep = within < cap
            slot = jnp.where(keep, sorted_exp * cap + within, N_EXP * cap)
            tok_id = order // TOP_K
            padded_tokens = jnp.zeros((N_EXP * cap + 1, H), x.dtype).at[slot].set(x[tok_id])[:-1]
            padded_probs = jnp.zeros((N_EXP * cap + 1,), jnp.float32).at[slot].set(top_p.reshape(-1)[order])[:-1]
            padded_ids = jnp.zeros((N_EXP * cap + 1,), jnp.int32).at[slot].set(tok_id.astype(jnp.int32))[:-1]
            exp_in = padded_tokens.reshape(N_EXP, cap, H)
            act = jax.nn.gelu(jnp.einsum('ech,ehf->ecf', exp_in, moe_w1), approximate=False)
            exp_out = jnp.einsum('ecf,efh->ech', act, moe_w2).reshape(N_EXP * cap, H)
            weighted = exp_out * padded_probs[:, None].astype(exp_out.dtype)
            moe = jnp.zeros((N, H), exp_out.dtype).at[padded_ids].add(weighted)
            return hidden_after_attn + moe.reshape(S, B, H)
        ks = jax.random.split(jax.random.key(seed), 6)
        qkv_out = N_KV * (Q_PER_KV + 2) * HEAD_DIM
        sc = 0.02
        return {'hidden_states': jax.random.normal(ks[0], (S_LEN, BATCH, HIDDEN), jnp.float32), 'ln1_weight': jnp.ones((HIDDEN,), jnp.float32), 'ln1_bias': jnp.zeros((HIDDEN,), jnp.float32), 'ln2_weight': jnp.ones((HIDDEN,), jnp.float32), 'ln2_bias': jnp.zeros((HIDDEN,), jnp.float32), 'qkv_weight': jax.random.normal(ks[1], (qkv_out, HIDDEN), jnp.float32) * sc, 'proj_weight': jax.random.normal(ks[2], (HIDDEN, HIDDEN), jnp.float32) * sc, 'router_weight': jax.random.normal(ks[3], (HIDDEN, N_EXP), jnp.float32) * sc, 'moe_w1': jax.random.normal(ks[4], (N_EXP, HIDDEN, FFN), jnp.float32) * sc, 'moe_w2': jax.random.normal(ks[5], (N_EXP, FFN, HIDDEN), jnp.float32) * sc}
    _L0_ffn_in = _L0_ffn_setup()
    _d = {'L0_attn_x': _L0_attn_in['x'], 'L0_attn_ln_w': _L0_attn_in['ln_w'], 'L0_attn_ln_b': _L0_attn_in['ln_b'], 'L0_attn_wq': _L0_attn_in['wq'], 'L0_attn_wk': _L0_attn_in['wk'], 'L0_attn_wv': _L0_attn_in['wv'], 'L0_attn_wo': _L0_attn_in['wo'], 'L0_ffn_ln1_weight': _L0_ffn_in['ln1_weight'], 'L0_ffn_ln1_bias': _L0_ffn_in['ln1_bias'], 'L0_ffn_ln2_weight': _L0_ffn_in['ln2_weight'], 'L0_ffn_ln2_bias': _L0_ffn_in['ln2_bias'], 'L0_ffn_qkv_weight': _L0_ffn_in['qkv_weight'], 'L0_ffn_proj_weight': _L0_ffn_in['proj_weight'], 'L0_ffn_router_weight': _L0_ffn_in['router_weight'], 'L0_ffn_moe_w1': _L0_ffn_in['moe_w1'], 'L0_ffn_moe_w2': _L0_ffn_in['moe_w2']}
    _x0 = _d['L0_attn_x']
    _d['L0_attn_x'] = jax.random.normal(jax.random.fold_in(jax.random.key(seed), 1), (16, 256, 128), dtype=_x0.dtype)
    del _x0
    return _d

def reference(L0_attn_x, L0_attn_ln_w, L0_attn_ln_b, L0_attn_wq, L0_attn_wk, L0_attn_wv, L0_attn_wo, L0_ffn_ln1_weight, L0_ffn_ln1_bias, L0_ffn_ln2_weight, L0_ffn_ln2_bias, L0_ffn_qkv_weight, L0_ffn_proj_weight, L0_ffn_router_weight, L0_ffn_moe_w1, L0_ffn_moe_w2):

    def _L0_attn_ref(x, ln_w, ln_b, wq, wk, wv, wo):
        import jax, jax.numpy as jnp
        import numpy as np
        import math
        D_MODEL = 128
        NUM_HEADS = 16
        HEAD = D_MODEL // NUM_HEADS
        EPS = 1e-05

        def _layernorm(x, w, b):
            mean = jnp.mean(x, axis=-1, keepdims=True)
            var = jnp.var(x, axis=-1, keepdims=True)
            return (x - mean) * w / jnp.sqrt(var + EPS) + b
        y = _layernorm(x, ln_w, ln_b)
        seq_len = y.shape[-2]
        q = jnp.einsum('bsd,hde->bhse', y, wq)
        k = jnp.einsum('bsd,hde->bhse', y, wk)
        v = jnp.einsum('bsd,hde->bhse', y, wv)
        scores = jnp.einsum('bhse,bhte->bhst', q, k) / math.sqrt(HEAD)
        causal = jnp.triu(jnp.full((seq_len, seq_len), -jnp.inf, dtype=scores.dtype), k=1)
        scores = scores + causal
        weights = jax.nn.softmax(scores, axis=-1)
        attn = jnp.einsum('bhst,bhte->bshe', weights, v)
        attn = attn.reshape(*attn.shape[:-2], -1)
        out = attn @ wo
        return out + x

    def _L0_ffn_ref(hidden_states, ln1_weight, ln1_bias, ln2_weight, ln2_bias, qkv_weight, proj_weight, router_weight, moe_w1, moe_w2):
        import jax, jax.numpy as jnp
        import numpy as np
        S_LEN, BATCH, HIDDEN = (256, 2, 128)
        N_HEADS, N_KV = (16, 8)
        N_EXP, TOP_K, CAP_F = (8, 2, 1.25)
        FFN = 512
        HEAD_DIM = HIDDEN // N_HEADS
        Q_PER_KV = N_HEADS // N_KV
        EPS = 1e-05
        NEG = -1000000000.0

        def _ln(x, w, b):
            mu = jnp.mean(x, -1, keepdims=True)
            var = jnp.var(x, -1, keepdims=True)
            return (x - mu) * jax.lax.rsqrt(var + EPS) * w + b

        def _forward(hidden_states, ln1_weight, ln1_bias, ln2_weight, ln2_bias, qkv_weight, proj_weight, router_weight, moe_w1, moe_w2):
            S, B, H = hidden_states.shape
            ln1 = _ln(hidden_states, ln1_weight, ln1_bias)
            qkv = (ln1 @ qkv_weight.T).reshape(S, B, N_KV, (Q_PER_KV + 2) * HEAD_DIM)
            q_dim = Q_PER_KV * HEAD_DIM
            q = qkv[..., :q_dim].reshape(S, B, N_HEADS, HEAD_DIM)
            k = jnp.repeat(qkv[..., q_dim:q_dim + HEAD_DIM], Q_PER_KV, axis=2)
            v = jnp.repeat(qkv[..., q_dim + HEAD_DIM:], Q_PER_KV, axis=2)
            scores = jnp.einsum('sbhd,tbhd->bhst', q, k) / jnp.sqrt(jnp.float32(HEAD_DIM))
            causal = jnp.tril(jnp.ones((S, S), bool))
            attn = jax.nn.softmax(jnp.where(causal[None, None], scores, NEG), axis=-1)
            attn_out = jnp.einsum('bhst,tbhd->sbhd', attn, v).reshape(S, B, H)
            hidden_after_attn = hidden_states + attn_out @ proj_weight.T
            x = _ln(hidden_after_attn, ln2_weight, ln2_bias).reshape(-1, H)
            N = S * B
            probs = jax.nn.softmax(x.astype(jnp.float32) @ router_weight, axis=-1)
            top_p, top_i = jax.lax.top_k(probs, TOP_K)
            top_p = top_p / jnp.sum(top_p, -1, keepdims=True)
            flat_exp = top_i.reshape(-1)
            order = jnp.argsort(flat_exp)
            sorted_exp = flat_exp[order]
            counts = jnp.bincount(sorted_exp, length=N_EXP)
            offsets = jnp.concatenate([jnp.zeros((1,), counts.dtype), jnp.cumsum(counts)])
            within = jnp.arange(N * TOP_K) - offsets[sorted_exp]
            cap = int(np.ceil(N * TOP_K / N_EXP * CAP_F))
            keep = within < cap
            slot = jnp.where(keep, sorted_exp * cap + within, N_EXP * cap)
            tok_id = order // TOP_K
            padded_tokens = jnp.zeros((N_EXP * cap + 1, H), x.dtype).at[slot].set(x[tok_id])[:-1]
            padded_probs = jnp.zeros((N_EXP * cap + 1,), jnp.float32).at[slot].set(top_p.reshape(-1)[order])[:-1]
            padded_ids = jnp.zeros((N_EXP * cap + 1,), jnp.int32).at[slot].set(tok_id.astype(jnp.int32))[:-1]
            exp_in = padded_tokens.reshape(N_EXP, cap, H)
            act = jax.nn.gelu(jnp.einsum('ech,ehf->ecf', exp_in, moe_w1), approximate=False)
            exp_out = jnp.einsum('ecf,efh->ech', act, moe_w2).reshape(N_EXP * cap, H)
            weighted = exp_out * padded_probs[:, None].astype(exp_out.dtype)
            moe = jnp.zeros((N, H), exp_out.dtype).at[padded_ids].add(weighted)
            return hidden_after_attn + moe.reshape(S, B, H)
        return _forward(hidden_states, ln1_weight, ln1_bias, ln2_weight, ln2_bias, qkv_weight, proj_weight, router_weight, moe_w1, moe_w2)
    x = L0_attn_x
    x = x + 0.5 * _L0_ffn_ref(_layernorm(x, axis=-1), L0_ffn_ln1_weight, L0_ffn_ln1_bias, L0_ffn_ln2_weight, L0_ffn_ln2_bias, L0_ffn_qkv_weight, L0_ffn_proj_weight, L0_ffn_router_weight, L0_ffn_moe_w1, L0_ffn_moe_w2)
    x = x + _L0_attn_ref(_layernorm(x, axis=-1), L0_attn_ln_w, L0_attn_ln_b, L0_attn_wq, L0_attn_wk, L0_attn_wv, L0_attn_wo)
    x = x + 0.5 * _L0_ffn_ref(_layernorm(x, axis=-1), L0_ffn_ln1_weight, L0_ffn_ln1_bias, L0_ffn_ln2_weight, L0_ffn_ln2_bias, L0_ffn_qkv_weight, L0_ffn_proj_weight, L0_ffn_router_weight, L0_ffn_moe_w1, L0_ffn_moe_w2)
    return x

_drawn_inputs = setup_inputs


def setup_inputs(seed=0):
    import zlib

    import numpy as np

    out = dict(_drawn_inputs(seed))
    spreads = {'L0_attn_ln_w': (1.0, 0.6),
     'L0_attn_ln_b': (0.0, 0.8),
     'L0_ffn_ln1_weight': (1.0, 0.6),
     'L0_ffn_ln1_bias': (0.0, 0.8),
     'L0_ffn_ln2_weight': (1.0, 0.6),
     'L0_ffn_ln2_bias': (0.0, 0.8)}
    factors = {'L0_attn_wq': 8.0,
     'L0_attn_wk': 8.0,
     'L0_attn_wv': 8.0,
     'L0_attn_wo': 8.0,
     'L0_ffn_qkv_weight': 4.073,
     'L0_ffn_proj_weight': 3.923,
     'L0_ffn_router_weight': 3.349,
     'L0_ffn_moe_w1': 2.887,
     'L0_ffn_moe_w2': 2.85}
    for name, (base, spread) in spreads.items():
        noise = np.random.default_rng([zlib.crc32(name.encode()), seed]).standard_normal(out[name].shape)
        drawn = base * np.exp(spread * noise) if base else spread * noise
        out[name] = jnp.asarray(drawn.astype(out[name].dtype))
    for name, factor in factors.items():
        out[name] = (out[name] * factor).astype(out[name].dtype)
    return out
```

```python
from contextlib import ExitStack

import numpy as np

import concourse.bass as bass
from concourse import mybir

F32 = mybir.dt.float32
BF16 = mybir.dt.bfloat16
U32 = mybir.dt.uint32
ALU = mybir.AluOpType
ACT = mybir.ActivationFunctionType
AX = mybir.AxisListType

P = 128
EPS = 1e-5
HEADS, HD = 16, 8
SCALE = HD ** -0.5
NEG = -1e30


CREDIT = 32


def done(n):
    return n + (1 + CREDIT)


class Chain:

    def __init__(self, engine, sem):
        self.engine, self.sem, self.n = engine, sem, 0

    def __call__(self, ins):
        self.n += 1
        ins.then_inc(self.sem, 1)
        self.engine.wait_ge(self.sem, self.n)


def bcast(ap, axis, n):
    wide = ap.unsqueeze(axis)
    shape = list(wide.shape)
    shape[axis] = n
    return wide.broadcast_to(shape)


def macaron_kernel(nc, x, at_ln_w, at_ln_b, wq, wk, wv, wo, ln1_w, ln1_b, ln2_w, ln2_b,
                   qkv_w, proj_w, router_w, moe_w1, moe_w2, out, stages=3):
    S, B, D = x.shape
    NT = S * B // P
    HALVES = B // P
    E, _, FF = moe_w1.shape
    FC = FF // P
    CAP = -(-S * B * 2 * 5 // (4 * E))
    CH = 2 * P
    NCH = CAP // CH
    assert CAP % CH == 0 and D == P and NCH % 2 == 1 and E % 2 == 0

    xv = x.rearrange("s (a p) f -> p (s a) f", p=P)
    outv = out.rearrange("s (a p) f -> p (s a) f", p=P)
    queue = nc.dram_tensor("queue", [E * CAP, D], F32).ap()
    answer = nc.dram_tensor("answer", [E * CAP, D], F32).ap()
    q_parts = nc.dram_tensor("q_parts", [S, 3, D, B], BF16).ap()
    k_parts = nc.dram_tensor("k_parts", [S, 3, D, B], BF16).ap()
    zero_rows = nc.dram_tensor("zero_rows", [3, HEADS * B], BF16).ap()

    ctx = ExitStack()
    with ctx:
        def sb(name, shape, dt=F32):
            return ctx.enter_context(nc.sbuf_tensor(name, shape, dt))

        taken = []

        def sem(name):
            taken.append(nc.alloc_semaphore(name))
            return taken[-1]

        def recycle_semaphores():
            nc.clear_and_free_semaphores(taken)
            taken.clear()
            nc.all_engine_barrier()

        banks = [ctx.enter_context(nc.psum_tensor(f"bank{i}", [P, 512], F32)) for i in range(2)]
        st_ps = [ctx.enter_context(nc.psum_tensor(f"pair{i}", [P, 2, 512], F32)) for i in range(2)]
        banks += [ctx.enter_context(nc.psum_tensor(f"bank{i}", [P, 512], F32)) for i in (2, 3)]

        X = sb("X", [P, NT, D])
        H2 = sb("H2", [P, NT, D])
        qT = sb("qT", [P, S, B])
        kT = sb("kT", [P, S, B])
        V = sb("V", [P, NT, D])
        prodQ = [sb(f"prodQ{i}", [P, S, B]) for i in range(2)]
        prodV = [sb(f"prodV{i}", [P, S, D]) for i in range(2)]
        stageZ = [sb(f"stageZ{i}", [P, 4, D]) for i in range(2)]
        stageT = [sb(f"stageT{i}", [P, 4 * P]) for i in range(2)]
        Z2 = qT[:, :, :].rearrange("p s (a f) -> p (s a) f", a=HALVES)

        ident = sb("ident", [P, P])
        ones = sb("ones", [P, P])
        before = sb("before", [P, P])
        select = sb("select", [P, 32])
        causal = sb("causal", [P, 2 * P], BF16)
        identb = sb("identb", [P, P], BF16)
        WqT, WkT, WvT, WpT = (sb(n, [P, P]) for n in ("WqT", "WkT", "WvT", "WpT"))
        Wqa, Wka, Wva, Woa = (sb(n, [P, P]) for n in ("Wqa", "Wka", "Wva", "Woa"))
        Wr = sb("Wr", [P, E])
        lnp = sb("lnp", [P, 6])
        eps = sb("eps", [P, 1])
        expert_base = sb("expert_base", [P, E])
        rank_of = sb("rank_of", [P, E])
        stats = sb("stats", [P, NT, 6])
        mean = sb("mean", [P, NT])
        r0 = sb("r0", [P, NT])
        r01 = sb("r01", [P, NT])
        tiny = [sb(f"tiny{i}", [P, NT]) for i in range(4)]

        loads, consts, wt, wt_ps, wt_done = (sem(n) for n in ("loads", "consts", "wt", "wt_ps", "wt_done"))
        qkv_in = [prodV[0][:, i, :] for i in range(2)]
        proj_in = prodV[0][:, 2, :]
        with nc.Block() as block:
            N_LOADS = 16

            @block.sync
            def _(sp):
                sp.dma_start(X[:, :, :], xv).then_inc(loads, 16)
                sp.dma_start(prodV[0][:, 0:2, :], qkv_w.rearrange("(a p) f -> p a f", p=P)).then_inc(loads, 16)
                sp.dma_start(proj_in, proj_w).then_inc(loads, 16)
                sp.dma_start(Wr[:, :], router_w).then_inc(loads, 16)
                for W, w in ((Wqa, wq), (Wka, wk), (Wva, wv)):
                    sp.dma_start(W[:, :].rearrange("f (h e) -> f h e", e=HD),
                                 w.rearrange("h f e -> f h e")).then_inc(loads, 16)
                sp.dma_start(Woa[:, :], wo).then_inc(loads, 16)
                for i, v in enumerate((ln1_w, ln1_b, ln2_w, ln2_b, at_ln_w, at_ln_b)):
                    sp.dma_start(lnp[:, i:i + 1], v.rearrange("(p a) -> p a", a=1)).then_inc(loads, 16)
                sp.wait_ge(consts, 1)
                for part in range(2):
                    rows = E * CAP // 2
                    sp.dma_start(queue[part * rows:(part + 1) * rows, :].rearrange("(p a) f -> p (a f)", p=P),
                                 prodQ[0][:, :, :].rearrange("p s b -> p (s b)")[:, 0:rows // P * D]
                                 if rows // P * D <= S * B else
                                 bcast(prodQ[0][:, 0, :], 1, rows // P * D // B)).then_inc(loads, 16)
                sp.dma_start(zero_rows[:, :], prodQ[0][0:3, 0:HEADS // 2, :].rearrange("p s b -> p (s b)").bitcast(BF16))\
                  .then_inc(loads, 16)
                sp.wait_ge(loads, 16 * 17)

            @block.gpsimd
            def _(pool):
                pool.memset(prodQ[0][:, :, :], 0.0).then_inc(consts, 1)
                pool.memset(ident[:, :], 0.0)
                pool.memset(ones[:, :], 1.0)
                pool.memset(before[:, :], 1.0)
                pool.memset(select[:, 0:HEADS], 1.0)
                pool.memset(select[:, HEADS:], 0.0)
                pool.memset(identb[:, :], 0.0)
                pool.memset(causal[:, :], 0.0)
                pool.memset(eps[:, :], EPS)
                pool.iota(expert_base[:, :], [[CAP, E]], base=0, channel_multiplier=0,
                          allow_small_or_imprecise_dtypes=True)
                pool.iota(rank_of[:, :], [[-1, E]], base=E, channel_multiplier=0,
                          allow_small_or_imprecise_dtypes=True).then_inc(consts, 1)
                pool.wait_ge(consts, 2)
                for m in (ident, identb):
                    pool.affine_select(out=m[:, :], in_=m[:, :], compare_op=ALU.not_equal, fill=1.0,
                                       base=0, pattern=[[-1, P]], channel_multiplier=1)
                pool.affine_select(out=before[:, :], in_=before[:, :], compare_op=ALU.is_ge, fill=0.0,
                                   base=-1, pattern=[[1, P]], channel_multiplier=-1)
                cv = causal[:, :].rearrange("p (a t) -> p a t", a=2)
                pool.affine_select(out=cv, in_=cv, compare_op=ALU.is_ge, fill=NEG,
                                   base=0, pattern=[[0, 2], [-1, P]], channel_multiplier=1)
                sel = select[:, 0:HEADS]
                pool.affine_select(out=sel, in_=sel, compare_op=ALU.is_ge, fill=0.0,
                                   base=0, pattern=[[-HD, HEADS]], channel_multiplier=1).then_inc(consts, 1)
                pool.wait_ge(consts, 3)
                pool.affine_select(out=sel, in_=sel, compare_op=ALU.is_ge, fill=0.0,
                                   base=HD - 1, pattern=[[HD, HEADS]], channel_multiplier=-1).then_inc(consts, 1)
                pool.wait_ge(consts, 4)

            @block.tensor
            def _(pe):
                pe.wait_ge(loads, 16 * 17)
                pe.wait_ge(consts, 4)
                for i in range(2):
                    pe.transpose(banks[0][:, i * P:(i + 1) * P], qkv_in[i], ident[:, :])
                pe.transpose(banks[0][:, 2 * P:3 * P], proj_in, ident[:, :]).then_inc(wt_ps, 1)

            @block.vector
            def _(dve):
                dve.wait_ge(wt_ps, 1)
                src = banks[0][:, 0:2 * P].rearrange("f (g c) -> f g c", c=4 * HD)
                dve.tensor_copy(WqT[:, :].rearrange("f (g c) -> f g c", c=2 * HD), src[:, :, 0:2 * HD])
                for r in range(2):
                    for W, c in ((WkT, 2), (WvT, 3)):
                        dve.tensor_copy(W[:, :].rearrange("f (g r d) -> f g r d", r=2, d=HD)[:, :, r, :],
                                        src[:, :, c * HD:(c + 1) * HD])
                dve.tensor_copy(WpT[:, :], banks[0][:, 2 * P:3 * P]).then_inc(wt_done, 1)
                dve.wait_ge(wt_done, 1)

        def layer_norm_stats(name, src, double):
            v_ready, s_ready, steps = sem(name + "_var"), sem(name + "_std"), sem(name + "_steps")
            ve, sd, t0, t1 = (t[:, :] for t in tiny)
            rounds = 2 if double else 1
            with nc.Block() as block:
                @block.scalar
                def _(act):
                    for r in range(rounds):
                        act.wait_ge(v_ready, r + 1)
                        act.activation(sd, ve, ACT.Sqrt).then_inc(s_ready, 1)

                @block.vector
                def _(dve):
                    with dve.Fori(0, NT // 4) as i:
                        for k in range(4):
                            ins = dve.bn_stats(stats[:, bass.ds(i * 4 + k, 1), :], src[:, bass.ds(i * 4 + k, 1), :])
                        ins.then_inc(steps, 1)
                    dve.wait_ge(steps, NT // 4)
                    chain = Chain(dve, steps)
                    chain.n = NT // 4
                    me, mo = stats[:, :, 1], stats[:, :, 4]
                    chain(dve.tensor_tensor(t0, me, mo, ALU.add))
                    chain(dve.tensor_scalar(mean[:, :], t0, 0.5, None, ALU.mult))
                    chain(dve.tensor_tensor(t0, me, mo, ALU.subtract))
                    chain(dve.scalar_tensor_tensor(t0, t0, 0.25, t0, ALU.mult, ALU.mult))
                    chain(dve.tensor_tensor(t1, stats[:, :, 2], stats[:, :, 5], ALU.add))
                    chain(dve.scalar_tensor_tensor(t0, t1, 1.0 / D, t0, ALU.mult, ALU.add))
                    for r in range(rounds):
                        if r:
                            chain(dve.tensor_tensor(t0, t0, r0[:, :], ALU.mult))
                            chain(dve.tensor_tensor(t0, t0, r0[:, :], ALU.mult))
                        dve.tensor_scalar(ve, t0, EPS, None, ALU.add).then_inc(v_ready, 1)
                        dve.wait_ge(v_ready, r + 1)
                        dve.wait_ge(s_ready, r + 1)
                        y = r01[:, :] if r else r0[:, :]
                        chain(dve.reciprocal(y, sd))
                        chain(dve.tensor_tensor(t1, y, y, ALU.mult))
                        chain(dve.tensor_tensor(t1, t1, ve, ALU.mult))
                        chain(dve.tensor_scalar(t1, t1, -0.5, 1.5, ALU.mult, ALU.add))
                        chain(dve.tensor_tensor(y, y, t1, ALU.mult))
                    if double:
                        chain(dve.tensor_tensor(r01[:, :], r01[:, :], r0[:, :], ALU.mult))

        sc = [sb(f"sc{i}", [P, HALVES, S, HEADS]) for i in range(3)]
        reduced = [sb(f"reduced{i}", [P, 512]) for i in range(2)]
        attnT = [sb(f"attnT{i}", [P, B]) for i in range(2)]
        mx = sb("mx", [P, HALVES, HEADS])
        den = sb("den", [P, HALVES, HEADS])
        logits = sb("logits", [P, NT, E])
        picks = [sb(f"pick{i}", [P, NT, E]) for i in range(2)]
        work = [sb(f"work{i}", [P, NT, E]) for i in range(2)]
        gate = [sb(f"gate{i}", [P, NT]) for i in range(2)]
        put_at = [sb(f"put_at{i}", [P, NT], U32) for i in range(2)]
        get_at = [sb(f"get_at{i}", [P, NT], U32) for i in range(2)]
        w1s = [prodQ[0][:, 2 * i:2 * i + 2, :].rearrange("p a b -> p (a b)") for i in range(2)]
        w2s = [prodQ[0][:, 4 + 2 * i:6 + 2 * i, :].rearrange("p a (c f) -> p (a c) f", f=D) for i in range(2)]
        hidden = [prodQ[1][:, 4 * i:4 * i + 4, :] for i in range(2)]
        xe = [prodQ[1][:, 8 + i, :].rearrange("p (a f) -> p a f", a=2) for i in range(4)]
        xeT = [prodQ[1][:, 12 + i, :] for i in range(2)]
        ye = [prodQ[1][:, 14 + i, :] for i in range(2)]

        def ffn_half(L, last):
            def sm(name):
                return sem(f"{L}_{name}")

            layer_norm_stats(L + "_ln01", X, True)


            G = NT // 4
            z_ready, zT_ps, zT_ready, qk_ps, q_copied, k_copied, v_ps, v_copied = credited = [
                sm(n) for n in ("z_ready", "zT_ps", "zT_ready", "qk_ps", "q_copied", "k_copied", "v_ps", "v_copied")]
            pz = [banks[0], banks[1]]
            pq, pk, pv = st_ps[0][:, 0, :], st_ps[0][:, 1, :], banks[2]
            with nc.Block() as block:
                @block.sync
                def _(sp):
                    for c in credited:
                        sp.sem_inc(c, CREDIT)

                @block.vector
                def _(dve):
                    with dve.Fori(0, G // 2) as i:
                        for u in range(2):
                            n = i * 2 + u
                            dve.wait_ge(zT_ps, done(n - 2))
                            for k in range(4):
                                j = i * 8 + (4 * u + k)
                                ins = dve.tensor_scalar(stageZ[u][:, k, :], X[:, bass.ds(j, 1), :],
                                                        mean[:, bass.ds(j, 1)], r01[:, bass.ds(j, 1)],
                                                        ALU.subtract, ALU.mult)
                            ins.then_inc(z_ready, 1)
                            for k in range(4):
                                j = i * 8 + (4 * u + k)
                                dve.tensor_scalar(H2[:, bass.ds(j, 1), :], X[:, bass.ds(j, 1), :],
                                                  mean[:, bass.ds(j, 1)], r0[:, bass.ds(j, 1)],
                                                  ALU.subtract, ALU.mult)
                            dve.wait_ge(qk_ps, done(n))
                            dve.tensor_copy(kT[:, bass.ds(i * 4 + 2 * u, 2), :],
                                            pk.rearrange("p (s b) -> p s b", s=2)).then_inc(k_copied, 1)

                @block.tensor
                def _(pe):
                    with pe.Fori(0, G // 2) as i:
                        for u in range(2):
                            n = i * 2 + u
                            pe.wait_ge(z_ready, done(n))
                            pe.wait_ge(zT_ready, done(n - 2))
                            for k in range(4):
                                ins = pe.transpose(pz[u][:, k * P:(k + 1) * P], stageZ[u][:, k, :], ident[:, :])
                            ins.then_inc(zT_ps, 1)
                            pe.wait_ge(zT_ready, done(n))
                            pe.wait_ge(q_copied, done(n - 1))
                            pe.wait_ge(k_copied, done(n - 1))
                            pe.matmul(pq, WqT[:, :], stageT[u][:, :], start=True, stop=True)
                            pe.matmul(pk, WkT[:, :], stageT[u][:, :], start=True, stop=True).then_inc(qk_ps, 1)
                            pe.wait_ge(v_copied, done(n - 1))
                            for k in range(4):
                                ins = pe.matmul(pv[:, k * P:(k + 1) * P], stageT[u][:, k * P:(k + 1) * P],
                                                WvT[:, :], start=True, stop=True)
                            ins.then_inc(v_ps, 1)

                @block.scalar
                def _(act):
                    with act.Fori(0, G // 2) as i:
                        for u in range(2):
                            n = i * 2 + u
                            act.wait_ge(zT_ps, done(n))
                            act.wait_ge(v_ps, done(n - 2))
                            act.activation(stageT[u][:, :], pz[u][:, :], ACT.Identity, bias=lnp[:, 1:2],
                                           scale=lnp[:, 0:1]).then_inc(zT_ready, 1)
                            act.wait_ge(qk_ps, done(n))
                            act.activation(qT[:, bass.ds(i * 4 + 2 * u, 2), :],
                                           pq.rearrange("p (s b) -> p s b", s=2), ACT.Copy).then_inc(q_copied, 1)
                            act.wait_ge(v_ps, done(n))
                            act.activation(V[:, bass.ds(i * 8 + 4 * u, 4), :],
                                           pv[:, :].rearrange("p (k f) -> p k f", k=4), ACT.Copy)\
                               .then_inc(v_copied, 1)

            groups = [(s, g) for s in range(S) for g in range(s // 8 + 1)]
            first = {s: groups.index((s, 0)) for s in range(S)}
            n_groups = {s: s // 8 + 1 for s in range(S)}

            def units(s, g):
                return min(4, s // 2 + 1 - 4 * g)

            prod_ready, red_ps, red_sb, tr_ps, sc_ready, centred, exped = (
                sm(n) for n in ("prod_ready", "red_ps", "red_sb", "tr_ps", "sc_ready", "centred", "exped"))
            probs_ready, pv_ready, pv_used, o_sb, y_ps, added, own = (
                sm(n) for n in ("probs_ready", "pv_ready", "pv_used", "o_sb", "y_ps", "added", "own"))
            pO, pY = st_ps[0], st_ps[1]
            LAGS = S + 3
            with nc.Block() as block:
                @block.vector
                def _(dve):
                    chain = Chain(dve, own)

                    def qk_product(s):
                        n = 2 * (s // 2 + 1)
                        if s >= 2:
                            dve.wait_ge(red_ps, first[s - 2] + n_groups[s - 2])
                        dve.tensor_tensor(prodQ[s % 2][:, 0:n, :], bcast(qT[:, s, :], 1, n), kT[:, 0:n, :],
                                          ALU.mult).then_inc(prod_ready, 1)

                    def centre(s):
                        n = s + 1
                        dve.wait_ge(sc_ready, first[s] + n_groups[s])
                        chain(dve.tensor_reduce(mx[:, :, :], sc[s % 3][:, :, 0:n, :].rearrange("p a t h -> p a h t"),
                                                AX.X, ALU.max))
                        dve.tensor_tensor(sc[s % 3][:, :, 0:n, :], sc[s % 3][:, :, 0:n, :], bcast(mx[:, :, :], 2, n),
                                          ALU.subtract).then_inc(centred, 1)

                    def normalise(s):
                        n = s + 1
                        dve.wait_ge(exped, s + 1)
                        chain(dve.tensor_reduce(den[:, :, :], sc[s % 3][:, :, 0:n, :].rearrange("p a t h -> p a h t"),
                                                AX.X, ALU.add))
                        chain(dve.reciprocal(den[:, :, :], den[:, :, :]))
                        dve.tensor_tensor(sc[s % 3][:, :, 0:n, :], sc[s % 3][:, :, 0:n, :], bcast(den[:, :, :], 2, n),
                                          ALU.mult).then_inc(probs_ready, 1)

                    def pv_product(s, a):
                        n = s + 1
                        dve.wait_ge(probs_ready, s + 1)
                        if s:
                            dve.wait_ge(pv_used, 2 * s + a - 1)
                        dve.tensor_tensor(prodV[a][:, 0:n, :].rearrange("p t (h d) -> p t h d", d=HD),
                                          bcast(sc[s % 3][:, a, 0:n, :], 3, HD),
                                          V[:, a:a + 2 * s + 1:2, :].rearrange("p t (h d) -> p t h d", d=HD),
                                          ALU.mult).then_inc(pv_ready, 1)

                    def add(s):
                        dve.wait_ge(y_ps, s + 1)
                        h = H2[:, 2 * s:2 * s + 2, :]
                        dve.tensor_tensor(h, h, pY[:, s % 2, 0:B].rearrange("p (a f) -> p a f", a=HALVES),
                                          ALU.add).then_inc(added, 1)

                    for i in range(LAGS):
                        if i < S:
                            qk_product(i)
                        if 0 <= i - 1 < S:
                            centre(i - 1)
                        if 0 <= i - 2 < S:
                            pv_product(i - 2, 0)
                        if 0 <= i - 1 < S:
                            normalise(i - 1)
                        if 0 <= i - 2 < S:
                            pv_product(i - 2, 1)
                        if 0 <= i - 3 < S:
                            add(i - 3)

                @block.tensor
                def _(pe):
                    def reduce_heads(s):
                        pe.wait_ge(prod_ready, s + 1)
                        for g in range(n_groups[s]):
                            n = first[s] + g
                            if n >= 2:
                                pe.wait_ge(red_sb, n - 1)
                            for j in range(units(s, g)):
                                u = 4 * g + j
                                ins = pe.matmul(banks[n % 2][32 * j:32 * j + 32, :], select[:, :],
                                                prodQ[s % 2][:, 2 * u:2 * u + 2, :].rearrange("p t b -> p (t b)"),
                                                start=True, stop=True)
                            ins.then_inc(red_ps, 1)

                    def to_columns(s):
                        for g in range(n_groups[s]):
                            n = first[s] + g
                            m = 32 * units(s, g)
                            pe.wait_ge(red_sb, n + 1)
                            if n >= 2:
                                pe.wait_ge(sc_ready, n - 1)
                            for c in range(4):
                                ins = pe.transpose(banks[2 + n % 2][:, c * P:c * P + m],
                                                   reduced[n % 2][0:m, c * P:(c + 1) * P], ident[0:m, 0:m])
                            ins.then_inc(tr_ps, 1)

                    def sum_pv(s, a):
                        pe.wait_ge(pv_ready, 2 * s + a + 1)
                        if a == 0 and s >= 2:
                            pe.wait_ge(o_sb, s - 1)
                        for t in range(s + 1):
                            ins = pe.matmul(pO[:, s % 2, a * P:(a + 1) * P], prodV[a][:, t, :], ident[:, :],
                                            start=(t == 0), stop=(t == s))
                        ins.then_inc(pv_used, 1)

                    def project(s):
                        pe.wait_ge(o_sb, s + 1)
                        if s >= 2:
                            pe.wait_ge(added, s - 1)
                        for a in range(HALVES):
                            ins = pe.matmul(pY[:, s % 2, a * P:(a + 1) * P], attnT[s % 2][:, a * P:(a + 1) * P],
                                            WpT[:, :], start=True, stop=True)
                        ins.then_inc(y_ps, 1)

                    for i in range(LAGS):
                        if i < S:
                            reduce_heads(i)
                        if 0 <= i - 2 < S:
                            sum_pv(i - 2, 0)
                        if i < S:
                            to_columns(i)
                        if 0 <= i - 2 < S:
                            sum_pv(i - 2, 1)
                        if 0 <= i - 3 < S:
                            project(i - 3)

                @block.scalar
                def _(act):
                    for i in range(LAGS):
                        if i < S:
                            for g in range(n_groups[i]):
                                n, m = first[i] + g, 32 * units(i, g)
                                act.wait_ge(red_ps, n + 1)
                                if n >= 2:
                                    act.wait_ge(tr_ps, n - 1)
                                act.activation(reduced[n % 2][0:m, :], banks[n % 2][0:m, :], ACT.Copy)\
                                   .then_inc(red_sb, 1)
                        if 0 <= i - 1 < S:
                            s = i - 1
                            act.wait_ge(centred, s + 1)
                            e = sc[s % 3][:, :, 0:s + 1, :]
                            act.activation(e, e, ACT.Exp, scale=SCALE).then_inc(exped, 1)
                        if i < S:
                            for g in range(n_groups[i]):
                                n, m = first[i] + g, units(i, g)
                                act.wait_ge(tr_ps, n + 1)
                                if i >= 3:
                                    act.wait_ge(pv_ready, 2 * (i - 2))
                                for par in range(2):
                                    src = banks[2 + n % 2][:, 2 * par * P:2 * (par + 1) * P]
                                    src = src.rearrange("p (a j h) -> p a j h", a=HALVES, h=32)[:, :, 0:m, 0:HEADS]
                                    t0 = 8 * g + par
                                    ins = act.activation(sc[i % 3][:, :, t0:t0 + 2 * m - 1:2, :], src, ACT.Copy)
                                ins.then_inc(sc_ready, 1)
                        if 0 <= i - 2 < S:
                            s = i - 2
                            act.wait_ge(pv_used, 2 * s + 2)
                            if s >= 2:
                                act.wait_ge(y_ps, s - 1)
                            act.activation(attnT[s % 2][:, :], pO[:, s % 2, 0:B], ACT.Copy).then_inc(o_sb, 1)

            layer_norm_stats(L + "_ln2", H2, False)

            y_ready, yT_ps, yT_ready, kept, lg_ps, lg_copied = credited = [
                sm(n) for n in ("y_ready", "yT_ps", "yT_ready", "kept", "lg_ps", "lg_copied")]
            pl = [banks[2], banks[3]]
            with nc.Block() as block:
                @block.sync
                def _(sp):
                    for c in credited:
                        sp.sem_inc(c, CREDIT)

                @block.vector
                def _(dve):
                    with dve.Fori(0, G // 2) as i:
                        for u in range(2):
                            n = i * 2 + u
                            dve.wait_ge(yT_ps, done(n - 2))
                            dve.wait_ge(kept, done(n - 2))
                            for k in range(4):
                                j = i * 8 + (4 * u + k)
                                ins = dve.tensor_scalar(stageZ[u][:, k, :], H2[:, bass.ds(j, 1), :],
                                                        mean[:, bass.ds(j, 1)], r0[:, bass.ds(j, 1)],
                                                        ALU.subtract, ALU.mult)
                            ins.then_inc(y_ready, 1)
                            dve.wait_ge(lg_ps, done(n))
                            dve.tensor_copy(logits[:, bass.ds(i * 8 + 4 * u, 4), :],
                                            pl[u][:, 0:4 * E].rearrange("p (k e) -> p k e", e=E)).then_inc(lg_copied, 1)

                @block.tensor
                def _(pe):
                    with pe.Fori(0, G // 2) as i:
                        for u in range(2):
                            n = i * 2 + u
                            pe.wait_ge(y_ready, done(n))
                            pe.wait_ge(yT_ready, done(n - 2))
                            for k in range(4):
                                ins = pe.transpose(pz[u][:, k * P:(k + 1) * P], stageZ[u][:, k, :], ident[:, :])
                            ins.then_inc(yT_ps, 1)
                            pe.wait_ge(yT_ready, done(n))
                            pe.wait_ge(lg_copied, done(n - 2))
                            for k in range(4):
                                ins = pe.matmul(pl[u][:, k * E:(k + 1) * E], stageT[u][:, k * P:(k + 1) * P],
                                                Wr[:, :], start=True, stop=True)
                            ins.then_inc(lg_ps, 1)

                @block.scalar
                def _(act):
                    with act.Fori(0, G // 2) as i:
                        for u in range(2):
                            n = i * 2 + u
                            act.wait_ge(y_ready, done(n))
                            act.activation(Z2[:, bass.ds(i * 8 + 4 * u, 4), :], stageZ[u][:, :, :], ACT.Copy)\
                               .then_inc(kept, 1)
                            act.wait_ge(yT_ps, done(n))
                            act.wait_ge(lg_ps, done(n - 2))
                            act.activation(stageT[u][:, :], pz[u][:, :], ACT.Identity, bias=lnp[:, 3:4],
                                           scale=lnp[:, 2:3]).then_inc(yT_ready, 1)

            steps, gap, gap_exp, ranks_ps, placed, scattered = (
                sm(n) for n in ("steps", "gap", "gap_exp", "ranks_ps", "placed", "scattered"))
            t0, t1, t2, t3 = (t[:, :] for t in tiny)
            with nc.Block() as block:
                @block.vector
                def _(dve):
                    chain = Chain(dve, steps)
                    wk0, wk1 = work[0][:, :, :], work[1][:, :, :]
                    lg = logits[:, :, :]
                    for k, top in ((0, t0), (1, t1)):
                        chain(dve.tensor_reduce(top, lg, AX.X, ALU.max))
                        chain(dve.tensor_tensor(wk0, lg, bcast(top, 2, E), ALU.is_equal))
                        chain(dve.tensor_tensor(wk0, wk0, bcast(rank_of[:, :], 1, NT), ALU.mult))
                        chain(dve.tensor_reduce(t2, wk0, AX.X, ALU.max))
                        chain(dve.tensor_tensor(picks[k][:, :, :], wk0, bcast(t2, 2, E), ALU.is_equal))
                        if k == 0:
                            chain(dve.scalar_tensor_tensor(lg, picks[0][:, :, :], NEG, lg, ALU.mult, ALU.add))
                    dve.tensor_tensor(t2, t1, t0, ALU.subtract).then_inc(gap, 1)
                    dve.tensor_tensor(wk0, picks[0][:, :, :], picks[1][:, :, :], ALU.add).then_inc(gap, 1)
                    dve.wait_ge(gap_exp, 1)
                    chain(dve.tensor_scalar(t0, t3, 1.0, None, ALU.add))
                    chain(dve.reciprocal(gate[0][:, :], t0))
                    chain(dve.tensor_tensor(gate[1][:, :], gate[0][:, :], t3, ALU.mult))
                    dve.wait_ge(ranks_ps, 1)
                    total = banks[1][:, 0:NT * E].rearrange("p (n e) -> p n e", e=E)
                    inside = banks[0][:, 0:NT * E].rearrange("p (n e) -> p n e", e=E)
                    chain(dve.tensor_copy(wk0, total))
                    src, dst = work[0], work[1]
                    w = 1
                    while w < NT:
                        dve.tensor_copy(dst[:, 0:w, :], src[:, 0:w, :])
                        chain(dve.tensor_tensor(dst[:, w:NT, :], src[:, w:NT, :], src[:, 0:NT - w, :], ALU.add))
                        src, dst = dst, src
                        w *= 2
                    run = src[:, :, :]
                    chain(dve.tensor_tensor(run, run, total, ALU.subtract))
                    chain(dve.tensor_tensor(run, run, inside, ALU.add))
                    for k in range(2):
                        tmp = dst[:, :, :]
                        chain(dve.tensor_tensor(tmp, picks[k][:, :, :], run, ALU.mult))
                        chain(dve.tensor_reduce(t0, tmp, AX.X, ALU.add))
                        chain(dve.tensor_tensor(tmp, picks[k][:, :, :], bcast(expert_base[:, :], 1, NT), ALU.mult))
                        chain(dve.tensor_reduce(t1, tmp, AX.X, ALU.add))
                        chain(dve.tensor_scalar(t2, t0, float(CAP), None, ALU.is_lt))
                        chain(dve.tensor_tensor(gate[k][:, :], gate[k][:, :], t2, ALU.mult))
                        chain(dve.tensor_tensor(t0, t0, t1, ALU.add))
                        chain(dve.tensor_tensor(t0, t0, t2, ALU.mult))
                        chain(dve.tensor_copy(get_at[k][:, :], t0))
                        chain(dve.tensor_scalar(t2, t2, -2.0 * E * CAP, 2.0 * E * CAP, ALU.mult, ALU.add))
                        chain(dve.tensor_tensor(t0, t0, t2, ALU.add))
                        dve.tensor_copy(put_at[k][:, :], t0).then_inc(placed, 1)
                        dve.wait_ge(placed, k + 1)

                @block.scalar
                def _(act):
                    act.wait_ge(gap, 1)
                    act.activation(t3, t2, ACT.Exp).then_inc(gap_exp, 1)

                @block.tensor
                def _(pe):
                    pe.wait_ge(gap, 2)
                    m = work[0][:, :, :].rearrange("p n e -> p (n e)")
                    pe.matmul(banks[0][:, 0:NT * E], before[:, :], m, start=True, stop=True)
                    pe.matmul(banks[1][:, 0:NT * E], ones[:, :], m, start=True, stop=True).then_inc(ranks_ps, 1)

                @block.gpsimd
                def _(pool):
                    for k in range(2):
                        pool.wait_ge(placed, k + 1)
                        for j in range(NT):
                            pool.indirect_dma_start(
                                queue, bass.IndirectOffsetOnAxis(ap=put_at[k][:, j:j + 1], axis=0),
                                Z2[:, j, :], None, bounds_check=E * CAP - 1, oob_is_err=False).then_inc(scattered, 16)
                    pool.wait_ge(scattered, 16 * 2 * NT)

            NPAIR, NC2 = E // 2, 2 * NCH
            w_in = [sm(f"w_in{u}") for u in range(2)]
            xe_in = [sm(f"xe_in{u}") for u in range(4)]
            ye_out = sm("ye_out")
            xeT_ps, xeT_ready, h_ps, h_ready, y2_ps, y2_copied, ye_free = credited = [
                sm(n) for n in ("xeT_ps", "xeT_ready", "h_ps", "h_ready", "y2_ps", "y2_copied", "ye_free")]
            px, py = [banks[0], banks[1]], [banks[2], banks[3]]
            with nc.Block() as block:
                @block.sync
                def _(sp):
                    for c in credited:
                        sp.sem_inc(c, CREDIT)
                    with sp.Fori(0, NPAIR) as i:
                        for u in range(2):
                            sp.wait_ge(y2_ps, done(i * NC2 + (u * NCH - NCH - 1)))
                            sp.dma_start(w1s[u], moe_w1[bass.ds(i * 2 + u, 1), :, :].rearrange("e p f -> p (e f)"))\
                              .then_inc(w_in[u], 16)
                            sp.dma_start(w2s[u], moe_w2[bass.ds(i * 2 + u, 1), :, :]
                                         .rearrange("e (c p) f -> p (e c) f", p=P)).then_inc(w_in[u], 16)
                            for c in range(NCH):
                                n = i * NC2 + (u * NCH + c)
                                q = u * NCH + c
                                sp.wait_ge(y2_ps, done(n - 2))
                                sp.dma_start(xe[q % 2], queue[bass.ds(n * CH, CH), :]
                                             .rearrange("(a p) f -> p a f", p=P)).then_inc(xe_in[q % 2], 16)

                @block.tensor
                def _(pe):
                    with pe.Fori(0, NPAIR) as i:
                        for q in range(NC2):
                            u, c = q // NCH, q % NCH
                            n = i * NC2 + q
                            b = q % 2
                            pe.wait_ge(xe_in[b], i * (16 * NCH) + 16 * (q // 2 + 1))
                            pe.wait_ge(xeT_ready, done(n - 2))
                            for a in range(2):
                                ins = pe.transpose(px[b][:, a * P:(a + 1) * P], xe[b][:, a, :], ident[:, :])
                            ins.then_inc(xeT_ps, 1)
                            pe.wait_ge(xeT_ready, done(n))
                            pe.wait_ge(h_ready, done(n - 2))
                            if c == 0:
                                pe.wait_ge(w_in[u], i * 32 + 32)
                            for f in range(FC):
                                ins = pe.matmul(st_ps[b][:, :, :].rearrange("p a c -> p (a c)")[:, f * CH:(f + 1) * CH],
                                                w1s[u][:, f * P:(f + 1) * P], xeT[b], start=True, stop=True)
                            ins.then_inc(h_ps, 1)
                            pe.wait_ge(h_ready, done(n))
                            pe.wait_ge(y2_copied, done(n - 2))
                            for a in range(2):
                                for f in range(FC):
                                    ins = pe.matmul(py[b][:, a * P:(a + 1) * P],
                                                    hidden[b][:, f, a * P:(a + 1) * P],
                                                    w2s[u][:, f, :], start=(f == 0), stop=(f == FC - 1))
                            ins.then_inc(y2_ps, 1)

                @block.scalar
                def _(act):
                    with act.Fori(0, NPAIR) as i:
                        for q in range(NC2):
                            n = i * NC2 + q
                            act.wait_ge(h_ps, done(n))
                            act.wait_ge(y2_ps, done(n - 2))
                            act.activation(hidden[q % 2].rearrange("p a b -> p (a b)"),
                                           st_ps[q % 2][:, :, :].rearrange("p a c -> p (a c)"),
                                           ACT.Gelu).then_inc(h_ready, 1)

                @block.vector
                def _(dve):
                    with dve.Fori(0, NPAIR) as i:
                        for q in range(NC2):
                            n = i * NC2 + q
                            b = q % 2
                            dve.wait_ge(xeT_ps, done(n))
                            dve.wait_ge(h_ps, done(n - 2))
                            dve.tensor_scalar(xeT[b], px[b][:, 0:CH], lnp[:, 2:3], lnp[:, 3:4],
                                              ALU.mult, ALU.add).then_inc(xeT_ready, 1)
                            dve.wait_ge(y2_ps, done(n))
                            dve.wait_ge(ye_free, done(n - 2))
                            dve.tensor_copy(ye[b], py[b][:, 0:CH]).then_inc(y2_copied, 1)

                @block.gpsimd
                def _(pool):
                    with pool.Fori(0, NPAIR) as i:
                        for q in range(NC2):
                            n = i * NC2 + q
                            pool.wait_ge(y2_copied, done(n))
                            pool.dma_start(answer[bass.ds(n * CH, CH), :].rearrange("(a p) f -> p a f", p=P),
                                           ye[q % 2].rearrange("p (a f) -> p a f", f=D)).then_inc(ye_out, 16)
                            pool.wait_ge(ye_out, n * 16 + 16)
                            pool.sem_inc(ye_free, 1)

            SLOTS = 8
            got = [sm(f"got{k}") for k in range(SLOTS)]
            mixed, own2, stored = sm("mixed"), sm("own2"), sm("stored")
            rows = [[prodV[k][:, s_, :] for k in range(2)] for s_ in range(SLOTS)]
            with nc.Block() as block:
                @block.gpsimd
                def _(pool):
                    for j in range(NT):
                        if j >= SLOTS:
                            pool.wait_ge(mixed, j - SLOTS + 1)
                        for k in range(2):
                            pool.indirect_dma_start(rows[j % SLOTS][k], None, answer,
                                                    bass.IndirectOffsetOnAxis(ap=get_at[k][:, j:j + 1], axis=0),
                                                    bounds_check=E * CAP - 1, oob_is_err=False)\
                                .then_inc(got[j % SLOTS], 16)

                @block.vector
                def _(dve):
                    chain = Chain(dve, own2)
                    for j in range(NT):
                        dve.wait_ge(got[j % SLOTS], 32 * (j // SLOTS + 1))
                        h = H2[:, j, :]
                        for k in range(2):
                            chain(dve.scalar_tensor_tensor(h, rows[j % SLOTS][k], gate[k][:, j:j + 1], h,
                                                           ALU.mult, ALU.add))
                        dve.scalar_tensor_tensor(X[:, j, :], h, 0.5, X[:, j, :], ALU.mult, ALU.add)\
                           .then_inc(mixed, 1)
                    dve.wait_ge(mixed, NT)

                if last:
                    @block.sync
                    def _(sp):
                        for j in range(0, NT, 4):
                            sp.wait_ge(mixed, j + 4)
                            sp.dma_start(outv[:, j:j + 4, :], X[:, j:j + 4, :]).then_inc(stored, 16)
                        sp.wait_ge(stored, 16 * (NT // 4))

        PART_Q, PART_K = (0, 0, 1, 1, 0, 2), (0, 1, 0, 1, 2, 0)
        MROW = 64
        KB = B // P
        flat = "p s b -> p (s b)"
        qs = [prodQ[0][:, :, :].rearrange(flat)[:, i * 2048:(i + 1) * 2048].bitcast(BF16)
              .rearrange("p (h t) -> p h t", h=HEADS) for i in range(2)]
        ks = [prodQ[1][:, :, :].rearrange(flat)[:, i * 2048:(i + 1) * 2048].bitcast(BF16)
              .rearrange("p (h t) -> p h t", h=HEADS) for i in range(2)]
        PT = [prodV[i // 2][:, :, :].rearrange(flat)[:, (i % 2) * 1024:(i % 2 + 1) * 1024]
              .rearrange("p (j c) -> p j c", j=2) for i in range(4)]
        Vp = [qT[:, 4 * i:4 * i + 4, :].rearrange(flat).rearrange("p (a h c) -> p a h c", a=KB, c=32)
              for i in range(2)]
        parts = [[kT[:, 3 * (2 * w + i):3 * (2 * w + i) + 3, :].rearrange(flat).bitcast(BF16)
                  .rearrange("p (c n) -> p c n", c=3) for i in range(2)] for w in range(2)]
        rest = [kT[:, 12 + 2 * w:14 + 2 * w, :].rearrange(flat) for w in range(2)]
        sums = [kT[:, i, :] for i in range(2)]
        heads_out = [kT[:, 2 + i, :].rearrange("p (a f) -> p a f", a=KB) for i in range(2)]
        heads_outT = kT[:, 4, :]
        mx3 = kT[:, 5, 0:3 * HEADS].rearrange("p (h c) -> p h c", c=3)
        negm = kT[:, 6, 0:KB * HEADS].rearrange("p (a h) -> p a h", a=KB)
        rec = kT[:, 7, 0:KB * 4].rearrange("p (a j) -> p a j", a=KB)
        m_rest = [kT[0:HEADS, 8 + i, :] for i in range(2)]
        m_parts = kT[0:HEADS, 10:12, :].rearrange(flat).bitcast(BF16)[:, 0:3 * B].rearrange("p (c t) -> p c t", c=3)

        def attention_half():
            def sm(name):
                return sem(f"at_{name}")

            layer_norm_stats("at_ln01", X, True)
            grow, shift = tiny[0], tiny[1]

            G = NT // 4
            z_ready, zT_ps, zT_ready, qk_ps, hi_ready, rest_ready, mid_ready, lo_ready, v_ps, v_copied, \
                parts_out = credited = [sm(n) for n in (
                    "z_ready", "zT_ps", "zT_ready", "qk_ps", "hi_ready", "rest_ready", "mid_ready", "lo_ready",
                    "v_ps", "v_copied", "parts_out")]
            coef, q_out, k_out, counted_groups = sm("coef"), sm("q_out"), sm("k_out"), sm("counted_groups")
            pz = [banks[0], banks[1]]
            pqk, pv = st_ps[0], banks[2]
            with nc.Block() as block:
                @block.sync
                def _(sp):
                    for c in credited:
                        sp.sem_inc(c, CREDIT)
                    with sp.Fori(0, G // 2) as i:
                        for u in range(2):
                            n = i * 2 + u
                            sp.wait_ge(lo_ready, done(n))
                            for w, (dst, s_) in enumerate(((q_parts, q_out), (k_parts, k_out))):
                                for b in range(2):
                                    sp.dma_start(dst[bass.ds(i * 4 + (2 * u + b), 1), :, :, :]
                                                 .rearrange("a c f t -> f (a c) t"),
                                                 parts[w][u][:, :, b * B:(b + 1) * B]).then_inc(s_, 16)
                            sp.wait_ge(q_out, n * 32 + 32)
                            sp.wait_ge(k_out, n * 32 + 32)
                            sp.sem_inc(parts_out, 1)

                @block.vector
                def _(dve):
                    dve.tensor_scalar(grow[:, :], r0[:, :], 1.0, None, ALU.add)
                    dve.tensor_tensor(shift[:, :], mean[:, :], r0[:, :], ALU.mult).then_inc(coef, 1)
                    dve.wait_ge(coef, 1)
                    with dve.Fori(0, G // 2) as i:
                        for u in range(2):
                            n = i * 2 + u
                            dve.wait_ge(zT_ps, done(n - 2))
                            for k in range(4):
                                j = i * 8 + (4 * u + k)
                                ins = dve.tensor_scalar(stageZ[u][:, k, :], X[:, bass.ds(j, 1), :],
                                                        mean[:, bass.ds(j, 1)], r01[:, bass.ds(j, 1)],
                                                        ALU.subtract, ALU.mult)
                            ins.then_inc(z_ready, 1)
                            for k in range(4):
                                j = i * 8 + (4 * u + k)
                                dve.tensor_scalar(X[:, bass.ds(j, 1), :], X[:, bass.ds(j, 1), :],
                                                  grow[:, bass.ds(j, 1)], shift[:, bass.ds(j, 1)],
                                                  ALU.mult, ALU.subtract)
                            dve.wait_ge(hi_ready, done(n))
                            dve.wait_ge(lo_ready, done(n - 1))
                            for w in range(2):
                                ins = dve.tensor_tensor(rest[w], pqk[:, w, :], parts[w][u][:, 0, :], ALU.subtract)
                            ins.then_inc(rest_ready, 1)

                @block.gpsimd
                def _(pool):
                    with pool.Fori(0, G // 2) as i:
                        for u in range(2):
                            n = i * 2 + u
                            pool.wait_ge(rest_ready, done(n))
                            pool.sem_inc(counted_groups, 1)
                            for w in range(2):
                                ins = pool.tensor_copy(parts[w][u][:, 1, :], rest[w])
                            ins.then_inc(mid_ready, 1)
                            pool.wait_ge(mid_ready, done(n))
                            for w in range(2):
                                ins = pool.tensor_tensor(parts[w][u][:, 2, :], rest[w], parts[w][u][:, 1, :],
                                                         ALU.subtract)
                            ins.then_inc(lo_ready, 1)

                @block.tensor
                def _(pe):
                    with pe.Fori(0, G // 2) as i:
                        for u in range(2):
                            n = i * 2 + u
                            pe.wait_ge(z_ready, done(n))
                            pe.wait_ge(zT_ready, done(n - 2))
                            for k in range(4):
                                ins = pe.transpose(pz[u][:, k * P:(k + 1) * P], stageZ[u][:, k, :], ident[:, :])
                            ins.then_inc(zT_ps, 1)
                            pe.wait_ge(zT_ready, done(n))
                            pe.wait_ge(rest_ready, done(n - 1))
                            pe.matmul(pqk[:, 0, :], Wqa[:, :], stageT[u][:, :], start=True, stop=True)
                            pe.matmul(pqk[:, 1, :], Wka[:, :], stageT[u][:, :], start=True, stop=True).then_inc(qk_ps, 1)
                            pe.wait_ge(v_copied, done(n - 1))
                            for k in range(4):
                                ins = pe.matmul(pv[:, k * P:(k + 1) * P], stageT[u][:, k * P:(k + 1) * P],
                                                Wva[:, :], start=True, stop=True)
                            ins.then_inc(v_ps, 1)

                @block.scalar
                def _(act):
                    with act.Fori(0, G // 2) as i:
                        for u in range(2):
                            n = i * 2 + u
                            act.wait_ge(zT_ps, done(n))
                            act.wait_ge(v_ps, done(n - 2))
                            act.activation(stageT[u][:, :], pz[u][:, :], ACT.Identity, bias=lnp[:, 5:6],
                                           scale=lnp[:, 4:5]).then_inc(zT_ready, 1)
                            act.wait_ge(qk_ps, done(n))
                            act.wait_ge(parts_out, done(n - 2))
                            for w in range(2):
                                ins = act.activation(parts[w][u][:, 0, :], pqk[:, w, :], ACT.Copy)
                            ins.then_inc(hi_ready, 1)
                            act.wait_ge(v_ps, done(n))
                            act.activation(V[:, bass.ds(i * 8 + 4 * u, 4), :],
                                           pv[:, :].rearrange("p (k f) -> p k f", k=4), ACT.Copy)\
                               .then_inc(v_copied, 1)

            PAIRS = HEADS // 2
            PERB = 13 * 16
            USES = 7
            cleared, counted = sm("cleared"), sm("counted")
            stack_in = [sm(f"stack_in{u}") for u in range(2)]
            m_in = [sm(f"m_in{u}") for u in range(2)]
            s_ps, s_max, m_ready, mp_ready, st_done, exp_done, masked, pv_done, sums_copied, vp_ready, \
                shared_ps, shared_free, heads_done, outT_ready, dve_own = credited = [sm(n) for n in (
                    "s_ps", "s_max", "m_ready", "mp_ready", "st_done", "exp_done", "masked", "pv_done",
                    "sums_copied", "vp_ready", "shared_ps", "shared_free", "heads_done", "outT_ready", "dve_own")]
            s_bank, pv_bank, shared = [banks[0], banks[1]], banks[2], banks[3]

            def shared_use(b, k):
                return b * USES + (k + 1)

            with nc.Block() as block:
                @block.sync
                def _(sp):
                    for c in credited:
                        sp.sem_inc(c, CREDIT)

                    def load(b, u):
                        for r in range(6):
                            for stack, src, p_ in ((qs, q_parts, PART_Q), (ks, k_parts, PART_K)):
                                sp.dma_start(stack[u][HD * r:HD * (r + 1), :, :],
                                             src[bass.ds(b, 1), p_[r], :, :].rearrange("a (h d) t -> d (a h) t", d=HD))\
                                  .then_inc(stack_in[u], 16)
                        sp.dma_start(qs[u][MROW:MROW + 3, :, :].rearrange("p h t -> p (h t)"), zero_rows)\
                          .then_inc(stack_in[u], 16)

                    def send_maxima(b, u):
                        sp.wait_ge(mp_ready, done(b))
                        for c in range(3):
                            sp.dma_start(qs[u][MROW + c:MROW + c + 1, :, :], m_parts[:, c:c + 1, :])\
                              .then_inc(m_in[u], 16)

                    sp.wait_ge(cleared, 1)
                    load(0, 0)
                    load(1, 1)
                    send_maxima(0, 0)
                    with sp.Fori(0, S // 2 - 1) as i:
                        for u in range(2):
                            b = i * 2 + u
                            send_maxima(b + 1, 1 - u)
                            sp.wait_ge(st_done, done(b * PAIRS + (PAIRS - 1)))
                            load(b + 2, u)
                    send_maxima(S - 1, (S - 1) % 2)

                @block.gpsimd
                def _(pool):
                    for stack in (prodQ[0], prodQ[1]):
                        pool.memset(stack[:, :, :], 0.0)
                    for v in Vp:
                        pool.memset(v, 0.0)
                    pool.drain().then_inc(cleared, 1)
                    pool.wait_ge(cleared, 1)
                    for v in Vp:
                        ins = pool.memset(v[:, :, :, HD:HD + 1], 1.0)
                    ins.then_inc(cleared, 1)
                    pool.wait_ge(cleared, 2)
                    for n, k_ in enumerate(ks):
                        pool.memset(k_[MROW:MROW + 3, :, :], 1.0).then_inc(cleared, 1)
                        pool.wait_ge(cleared, 3 + n)

                    def wait_count(s_, value):
                        pool.wait_ge(s_, value)
                        pool.sem_inc(counted, 1)

                    def spread_v(b, u):
                        for a in range(KB):
                            ins = pool.tensor_copy(Vp[u][:, a, :, 0:HD],
                                                   V[:, bass.ds(b * KB + a, 1), :]
                                                   .rearrange("p a (h d) -> p (a h) d", d=HD))
                        ins.then_inc(vp_ready, 1)

                    def mask(b):
                        for pr in range(PAIRS):
                            n = b * PAIRS + pr
                            wait_count(exp_done, done(n))
                            diag = PT[pr % 4].rearrange("p j (c s) -> p (j c) s", s=P)[:, 0:8:2, :]
                            pool.affine_select(out=diag, in_=diag, compare_op=ALU.is_ge, fill=0.0, base=0,
                                               pattern=[[0, 4], [1, P]], channel_multiplier=-1)\
                                .then_inc(masked, 1)
                            if pr == 2:
                                wait_count(pv_done, done(n - 3))

                    spread_v(0, 0)
                    with pool.Fori(0, S // 2 - 1) as i:
                        for u in range(2):
                            mask(i * 2 + u)
                            spread_v(i * 2 + (u + 1), 1 - u)
                    mask(S - 2)
                    spread_v(S - 1, 1)
                    mask(S - 1)

                @block.tensor
                def _(pe):
                    def scores(b, u, h):
                        n = b * HEADS + h
                        ps, q, k = s_bank[h % 2], qs[u][:, h, :], ks[u][:, h, :]
                        pe.wait_ge(s_max, done(n - 2))
                        pe.matmul(ps[:, 0:2 * P], identb[:, :], causal[:, :], start=True, stop=False,
                                  skip_group_check=True)
                        pe.matmul(ps[:, 0:P], q[:, 0:P], k[:, 0:P], start=False, stop=False, skip_group_check=True)
                        pe.matmul(ps[:, P:2 * P], q[:, P:2 * P], k[:, P:2 * P], start=False, stop=False,
                                  skip_group_check=True)
                        pe.matmul(ps[:, 2 * P:3 * P], q[:, P:2 * P], k[:, 0:P], start=False, stop=True,
                                  skip_group_check=True).then_inc(s_ps, 1)

                    def maxima_rows(b):
                        pe.wait_ge(m_ready, done(b))
                        pe.wait_ge(shared_free, done(shared_use(b - 1, 6) - 1))
                        for a in range(KB):
                            ins = pe.transpose(shared[0:HEADS, a * P:(a + 1) * P], negm[:, a, :], ident[:, :])
                        ins.then_inc(shared_ps, 1)

                    def scores_t(b, u, pr):
                        n = b * PAIRS + pr
                        pe.wait_ge(exp_done, done(n - 2))
                        for j in range(2):
                            h = 2 * pr + j
                            ps, q, k = st_ps[pr % 2][:, j, :], qs[u][:, h, :], ks[u][:, h, :]
                            pe.matmul(ps[:, 0:B], k[:, 0:P], q, start=True, stop=True)
                            ins = pe.matmul(ps[:, B:B + P], k[:, P:2 * P], q[:, P:2 * P], start=True, stop=True)
                        ins.then_inc(st_done, 1)

                    def weighted_sum(b, u, pr):
                        n = b * PAIRS + pr
                        pe.wait_ge(masked, done(n))
                        if pr == 0:
                            pe.wait_ge(vp_ready, done(b))
                        if pr % 2 == 0:
                            pe.wait_ge(sums_copied, done(b * 4 + (pr // 2 - 1)))
                        for j in range(2):
                            h = 2 * pr + j
                            o = pv_bank[32 * (h % 4):32 * (h % 4) + 32, 0:B]
                            pe.matmul(o, Vp[u][:, 0, h, :], PT[pr % 4][:, j, 0:B], start=True, stop=False)
                            ins = pe.matmul(o[:, P:B], Vp[u][:, 1, h, :], PT[pr % 4][:, j, B:B + P],
                                            start=False, stop=True)
                        ins.then_inc(pv_done, 1)

                    def sums_to_tokens(b, g):
                        pe.wait_ge(sums_copied, done(b * 4 + g))
                        pe.wait_ge(shared_free, done(shared_use(b, g) - 1))
                        for a in range(KB):
                            ins = pe.transpose(shared[:, a * P:(a + 1) * P], sums[g % 2][:, a * P:(a + 1) * P],
                                               ident[:, :])
                        ins.then_inc(shared_ps, 1)

                    def project(b, u):
                        pe.wait_ge(heads_done, done(b * 4 + 3))
                        pe.wait_ge(shared_free, done(shared_use(b, 4) - 1))
                        for a in range(KB):
                            ins = pe.transpose(shared[:, a * P:(a + 1) * P], heads_out[u][:, a, :], ident[:, :])
                        ins.then_inc(shared_ps, 1)
                        pe.wait_ge(outT_ready, done(b))
                        pe.wait_ge(shared_free, done(shared_use(b, 5) - 1))
                        for a in range(KB):
                            ins = pe.matmul(shared[:, a * P:(a + 1) * P], heads_outT[:, a * P:(a + 1) * P],
                                            Woa[:, :], start=True, stop=True)
                        ins.then_inc(shared_ps, 1)

                    def sequence(b, u, i, more):
                        for pr in range(PAIRS):
                            if more:
                                if pr == 0:
                                    pe.wait_ge(stack_in[1 - u], (i + (1 + u)) * PERB)
                                scores(b + 1, 1 - u, 2 * pr)
                                scores(b + 1, 1 - u, 2 * pr + 1)
                            if pr == 0:
                                pe.wait_ge(m_in[u], i * 48 + 48)
                            scores_t(b, u, pr)
                            if pr:
                                weighted_sum(b, u, pr - 1)
                            if pr >= 3 and pr % 2:
                                sums_to_tokens(b, (pr - 3) // 2)
                        weighted_sum(b, u, PAIRS - 1)
                        sums_to_tokens(b, 3)
                        project(b, u)
                        if more:
                            maxima_rows(b + 1)

                    pe.wait_ge(cleared, 4)
                    pe.wait_ge(stack_in[0], PERB)
                    for h in range(HEADS):
                        scores(0, 0, h)
                    maxima_rows(0)
                    with pe.Fori(0, S // 2 - 1) as i:
                        for u in range(2):
                            sequence(i * 2 + u, u, i, True)
                    sequence(S - 2, 0, S // 2 - 1, True)
                    sequence(S - 1, 1, S // 2 - 1, False)

                @block.scalar
                def _(act):
                    def sequence(b, u):
                        for pr in range(PAIRS):
                            n = b * PAIRS + pr
                            act.wait_ge(st_done, done(n))
                            act.wait_ge(pv_done, done(n - 4))
                            act.activation(PT[pr % 4][:, :, 0:3 * P], st_ps[pr % 2][:, :, 0:3 * P], ACT.Exp, scale=SCALE)\
                               .then_inc(exp_done, 1)
                            if pr >= 2 and pr % 2 == 0:
                                copy_sums(b, pr // 2 - 1)
                        copy_sums(b, 3)
                        act.wait_ge(shared_ps, done(shared_use(b, 4)))
                        act.activation(heads_outT, shared[:, 0:B], ACT.Copy).then_inc(shared_free, 1)
                        act.wait_ge(shared_free, done(shared_use(b, 4)))
                        act.sem_inc(outT_ready, 1)

                    def copy_sums(b, g):
                        act.wait_ge(pv_done, done(b * PAIRS + (2 * g + 1)))
                        act.wait_ge(shared_ps, done(shared_use(b, g) - (3 if g < 2 else 2)))
                        act.activation(sums[g % 2], pv_bank[:, 0:B], ACT.Copy).then_inc(sums_copied, 1)

                    with act.Fori(0, S // 2) as i:
                        for u in range(2):
                            sequence(i * 2 + u, u)

                @block.vector
                def _(dve):
                    OWN = 6

                    def maxima(b, h):
                        n = b * HEADS + h
                        dve.wait_ge(s_ps, done(n))
                        dve.tensor_reduce(mx3[:, h, :], s_bank[h % 2][:, 0:3 * P].rearrange("p (c t) -> p c t", c=3),
                                          AX.X, ALU.max, negate=True).then_inc(s_max, 1)

                    def combine(b):
                        dve.wait_ge(s_max, done(b * HEADS + (HEADS - 1)))
                        dve.tensor_copy(negm[:, 0, :], mx3[:, :, 0])
                        dve.tensor_tensor(negm[:, 1, :], mx3[:, :, 1], mx3[:, :, 2], ALU.min).then_inc(m_ready, 1)

                    def split_maxima(b, u_prev_count, u_prev):
                        dve.wait_ge(shared_ps, done(shared_use(b - 1, 6)))
                        src = shared[0:HEADS, 0:B]
                        if u_prev is not None:
                            dve.wait_ge(m_in[u_prev], u_prev_count)
                        own = b * OWN
                        dve.tensor_copy(m_parts[:, 0, :], src).then_inc(dve_own, 1)
                        dve.wait_ge(dve_own, done(own))
                        dve.tensor_tensor(m_rest[0], src, m_parts[:, 0, :], ALU.subtract).then_inc(shared_free, 1)
                        dve.wait_ge(shared_free, done(shared_use(b - 1, 6)))
                        dve.tensor_copy(m_parts[:, 1, :], m_rest[0]).then_inc(dve_own, 1)
                        dve.wait_ge(dve_own, done(own + 1))
                        dve.tensor_tensor(m_parts[:, 2, :], m_rest[0], m_parts[:, 1, :], ALU.subtract)\
                           .then_inc(mp_ready, 1)

                    def normalise(b, u, g):
                        dve.wait_ge(shared_ps, done(shared_use(b, g)))
                        src = shared[:, 0:B].rearrange("p (a j c) -> p a j c", a=KB, c=32)
                        own = b * OWN + (2 + g)
                        dve.reciprocal(rec, src[:, :, :, HD]).then_inc(dve_own, 1)
                        dve.wait_ge(dve_own, done(own))
                        out_ = heads_out[u][:, :, 32 * g:32 * g + 32].rearrange("p a (j d) -> p a j d", d=HD)
                        dve.tensor_tensor(out_, src[:, :, :, 0:HD], bcast(rec, 3, HD), ALU.mult)\
                           .then_inc(heads_done, 1)
                        dve.wait_ge(heads_done, done(b * 4 + g))
                        dve.sem_inc(shared_free, 1)

                    def add(b):
                        dve.wait_ge(shared_ps, done(shared_use(b, 5)))
                        xb = X[:, bass.ds(b * KB, KB), :]
                        dve.tensor_tensor(xb, xb, shared[:, 0:B].rearrange("p (a f) -> p a f", a=KB), ALU.add)\
                           .then_inc(shared_free, 1)

                    def sequence(b, u, i, more):
                        for pr in range(PAIRS):
                            if more:
                                maxima(b + 1, 2 * pr)
                                maxima(b + 1, 2 * pr + 1)
                            if pr >= 4 and pr % 2 == 0:
                                normalise(b, u, (pr - 4) // 2)
                        if more:
                            combine(b + 1)
                        normalise(b, u, 2)
                        normalise(b, u, 3)
                        add(b)
                        if more:
                            split_maxima(b + 1, i * 48 + 48, u)

                    for h in range(HEADS):
                        maxima(0, h)
                    combine(0)
                    split_maxima(0, None, None)
                    with dve.Fori(0, S // 2 - 1) as i:
                        for u in range(2):
                            sequence(i * 2 + u, u, i, True)
                    sequence(S - 2, 0, S // 2 - 1, True)
                    sequence(S - 1, 1, S // 2 - 1, False)

            if stages == 2:
                stored = sm("stored")
                with nc.Block() as block:
                    @block.sync
                    def _(sp):
                        sp.dma_start(outv, X[:, :, :]).then_inc(stored, 16)
                        sp.wait_ge(stored, 16)

        ffn_half("f1", stages == 1)
        if stages >= 2:
            recycle_semaphores()
            attention_half()
        if stages >= 3:
            recycle_semaphores()
            ffn_half("f2", True)


_INS = ["L0_attn_x", "L0_attn_ln_w", "L0_attn_ln_b", "L0_attn_wq", "L0_attn_wk", "L0_attn_wv", "L0_attn_wo",
        "L0_ffn_ln1_weight", "L0_ffn_ln1_bias", "L0_ffn_ln2_weight", "L0_ffn_ln2_bias", "L0_ffn_qkv_weight",
        "L0_ffn_proj_weight", "L0_ffn_router_weight", "L0_ffn_moe_w1", "L0_ffn_moe_w2"]
_OUTS = [((16, 256, 128), "float32")]


def kernel(**inputs):
    import numpy as _np
    import concourse.bacc as _bacc
    from concourse import mybir as _mybir
    from concourse.bass_utils import run_bass_kernel_spmd as _run

    nc = _bacc.Bacc("TRN2", target_bir_lowering=False, num_devices=1)
    arrays, args = {}, []
    for name in _INS:
        a = _np.ascontiguousarray(inputs[name])
        arrays[f"in_{name}_dram"] = a
        args.append(nc.dram_tensor(f"in_{name}_dram", a.shape, _mybir.dt.from_np(a.dtype), kind="ExternalInput").ap())
    for i, (shape, dtype) in enumerate(_OUTS):
        dt = _mybir.dt.from_np(_np.dtype(dtype))
        args.append(nc.dram_tensor(f"out_{i}_dram", shape, dt, kind="ExternalOutput").ap())
    macaron_kernel(nc, *args)
    r = _run(nc, [arrays], core_ids=[0])
    got = tuple(r.results[0][f"out_{i}_dram"] for i in range(len(_OUTS)))
    return got[0]
```

```python
from contextlib import ExitStack

import numpy as np

import concourse.bass as bass
from concourse import mybir

F32 = mybir.dt.float32
BF16 = mybir.dt.bfloat16
U32 = mybir.dt.uint32
ALU = mybir.AluOpType
ACT = mybir.ActivationFunctionType
AX = mybir.AxisListType

P = 128
EPS = 1e-5
HEADS, HD = 16, 8
SCALE = HD ** -0.5
NEG = -1e30


CREDIT = 32


def done(n):
    return n + (1 + CREDIT)


class Chain:

    def __init__(self, engine, sem):
        self.engine, self.sem, self.n = engine, sem, 0

    def __call__(self, ins):
        self.n += 1
        ins.then_inc(self.sem, 1)
        self.engine.wait_ge(self.sem, self.n)


def ahead_of(engine, count, ahead, rest):
    ahead(0, 0)
    with engine.Fori(0, count // 2 - 1) as i:
        for u in range(2):
            ahead(i * 2 + (u + 1), 1 - u)
            rest(i * 2 + u, u)
    ahead(count - 1, 1)
    rest(count - 2, 0)
    rest(count - 1, 1)


def bcast(ap, axis, n):
    wide = ap.unsqueeze(axis)
    shape = list(wide.shape)
    shape[axis] = n
    return wide.broadcast_to(shape)


def macaron_kernel(nc, x, at_ln_w, at_ln_b, wq, wk, wv, wo, ln1_w, ln1_b, ln2_w, ln2_b,
                   qkv_w, proj_w, router_w, moe_w1, moe_w2, out, stages=3):
    S, B, D = x.shape
    NT = S * B // P
    HALVES = B // P
    E, _, FF = moe_w1.shape
    FC = FF // P
    CAP = -(-S * B * 2 * 5 // (4 * E))
    CH = 2 * P
    NCH = CAP // CH
    assert CAP % CH == 0 and D == P and NCH % 2 == 1 and E % 2 == 0

    xv = x.rearrange("s (a p) f -> p (s a) f", p=P)
    outv = out.rearrange("s (a p) f -> p (s a) f", p=P)
    queue = nc.dram_tensor("queue", [E * CAP, D], F32).ap()
    answer = nc.dram_tensor("answer", [E * CAP, D], F32).ap()
    q_parts = nc.dram_tensor("q_parts", [S, 3, D, B], BF16).ap()
    k_parts = nc.dram_tensor("k_parts", [S, 3, D, B], BF16).ap()
    zero_rows = nc.dram_tensor("zero_rows", [3, HEADS * B], BF16).ap()

    ctx = ExitStack()
    with ctx:
        def sb(name, shape, dt=F32):
            return ctx.enter_context(nc.sbuf_tensor(name, shape, dt))

        taken = []

        def sem(name):
            taken.append(nc.alloc_semaphore(name))
            return taken[-1]

        def recycle_semaphores():
            nc.clear_and_free_semaphores(taken)
            taken.clear()
            nc.all_engine_barrier()

        banks = [ctx.enter_context(nc.psum_tensor(f"bank{i}", [P, 512], F32)) for i in range(2)]
        st_ps = [ctx.enter_context(nc.psum_tensor(f"pair{i}", [P, 2, 512], F32)) for i in range(2)]
        banks += [ctx.enter_context(nc.psum_tensor(f"bank{i}", [P, 512], F32)) for i in (2, 3)]

        X = sb("X", [P, NT, D])
        H2 = sb("H2", [P, NT, D])
        qT = sb("qT", [P, S, B])
        kT = sb("kT", [P, S, B])
        V = sb("V", [P, NT, D])
        prodQ = [sb(f"prodQ{i}", [P, S, B]) for i in range(2)]
        prodV = [sb(f"prodV{i}", [P, S, D]) for i in range(2)]
        stageZ = [sb(f"stageZ{i}", [P, 4, D]) for i in range(2)]
        stageT = [sb(f"stageT{i}", [P, 4 * P]) for i in range(2)]
        Z2 = qT[:, :, :].rearrange("p s (a f) -> p (s a) f", a=HALVES)

        ident = sb("ident", [P, P])
        ones = sb("ones", [P, P])
        before = sb("before", [P, P])
        select = sb("select", [P, 32])
        causal = sb("causal", [P, 2 * P], BF16)
        identb = sb("identb", [P, P], BF16)
        WqT, WkT, WvT, WpT = (sb(n, [P, P]) for n in ("WqT", "WkT", "WvT", "WpT"))
        Wqa, Wka, Wva, Woa = (sb(n, [P, P]) for n in ("Wqa", "Wka", "Wva", "Woa"))
        Wr = sb("Wr", [P, E])
        lnp = sb("lnp", [P, 6])
        eps = sb("eps", [P, 1])
        expert_base = sb("expert_base", [P, E])
        rank_of = sb("rank_of", [P, E])
        stats = sb("stats", [P, NT, 6])
        mean = sb("mean", [P, NT])
        r0 = sb("r0", [P, NT])
        r01 = sb("r01", [P, NT])
        tiny = [sb(f"tiny{i}", [P, NT]) for i in range(4)]

        loads, consts, wt, wt_ps, wt_done = (sem(n) for n in ("loads", "consts", "wt", "wt_ps", "wt_done"))
        qkv_in = [prodV[0][:, i, :] for i in range(2)]
        proj_in = prodV[0][:, 2, :]
        with nc.Block() as block:
            N_LOADS = 16

            @block.sync
            def _(sp):
                sp.dma_start(X[:, :, :], xv).then_inc(loads, 16)
                sp.dma_start(prodV[0][:, 0:2, :], qkv_w.rearrange("(a p) f -> p a f", p=P)).then_inc(loads, 16)
                sp.dma_start(proj_in, proj_w).then_inc(loads, 16)
                sp.dma_start(Wr[:, :], router_w).then_inc(loads, 16)
                for W, w in ((Wqa, wq), (Wka, wk), (Wva, wv)):
                    sp.dma_start(W[:, :].rearrange("f (h e) -> f h e", e=HD),
                                 w.rearrange("h f e -> f h e")).then_inc(loads, 16)
                sp.dma_start(Woa[:, :], wo).then_inc(loads, 16)
                for i, v in enumerate((ln1_w, ln1_b, ln2_w, ln2_b, at_ln_w, at_ln_b)):
                    sp.dma_start(lnp[:, i:i + 1], v.rearrange("(p a) -> p a", a=1)).then_inc(loads, 16)
                sp.wait_ge(consts, 1)
                for part in range(2):
                    rows = E * CAP // 2
                    sp.dma_start(queue[part * rows:(part + 1) * rows, :].rearrange("(p a) f -> p (a f)", p=P),
                                 prodQ[0][:, :, :].rearrange("p s b -> p (s b)")[:, 0:rows // P * D]
                                 if rows // P * D <= S * B else
                                 bcast(prodQ[0][:, 0, :], 1, rows // P * D // B)).then_inc(loads, 16)
                sp.dma_start(zero_rows[:, :], prodQ[0][0:3, 0:HEADS // 2, :].rearrange("p s b -> p (s b)").bitcast(BF16))\
                  .then_inc(loads, 16)
                sp.wait_ge(loads, 16 * 17)

            @block.gpsimd
            def _(pool):
                pool.memset(prodQ[0][:, :, :], 0.0).then_inc(consts, 1)
                pool.memset(ident[:, :], 0.0)
                pool.memset(ones[:, :], 1.0)
                pool.memset(before[:, :], 1.0)
                pool.memset(select[:, 0:HEADS], 1.0)
                pool.memset(select[:, HEADS:], 0.0)
                pool.memset(identb[:, :], 0.0)
                pool.memset(causal[:, :], 0.0)
                pool.memset(eps[:, :], EPS)
                pool.iota(expert_base[:, :], [[CAP, E]], base=0, channel_multiplier=0,
                          allow_small_or_imprecise_dtypes=True)
                pool.iota(rank_of[:, :], [[-1, E]], base=E, channel_multiplier=0,
                          allow_small_or_imprecise_dtypes=True).then_inc(consts, 1)
                pool.wait_ge(consts, 2)
                for m in (ident, identb):
                    pool.affine_select(out=m[:, :], in_=m[:, :], compare_op=ALU.not_equal, fill=1.0,
                                       base=0, pattern=[[-1, P]], channel_multiplier=1)
                pool.affine_select(out=before[:, :], in_=before[:, :], compare_op=ALU.is_ge, fill=0.0,
                                   base=-1, pattern=[[1, P]], channel_multiplier=-1)
                cv = causal[:, :].rearrange("p (a t) -> p a t", a=2)
                pool.affine_select(out=cv, in_=cv, compare_op=ALU.is_ge, fill=NEG,
                                   base=0, pattern=[[0, 2], [-1, P]], channel_multiplier=1)
                sel = select[:, 0:HEADS]
                pool.affine_select(out=sel, in_=sel, compare_op=ALU.is_ge, fill=0.0,
                                   base=0, pattern=[[-HD, HEADS]], channel_multiplier=1).then_inc(consts, 1)
                pool.wait_ge(consts, 3)
                pool.affine_select(out=sel, in_=sel, compare_op=ALU.is_ge, fill=0.0,
                                   base=HD - 1, pattern=[[HD, HEADS]], channel_multiplier=-1).then_inc(consts, 1)
                pool.wait_ge(consts, 4)

            @block.tensor
            def _(pe):
                pe.wait_ge(loads, 16 * 17)
                pe.wait_ge(consts, 4)
                for i in range(2):
                    pe.transpose(banks[0][:, i * P:(i + 1) * P], qkv_in[i], ident[:, :])
                pe.transpose(banks[0][:, 2 * P:3 * P], proj_in, ident[:, :]).then_inc(wt_ps, 1)

            @block.vector
            def _(dve):
                dve.wait_ge(wt_ps, 1)
                src = banks[0][:, 0:2 * P].rearrange("f (g c) -> f g c", c=4 * HD)
                dve.tensor_copy(WqT[:, :].rearrange("f (g c) -> f g c", c=2 * HD), src[:, :, 0:2 * HD])
                for r in range(2):
                    for W, c in ((WkT, 2), (WvT, 3)):
                        dve.tensor_copy(W[:, :].rearrange("f (g r d) -> f g r d", r=2, d=HD)[:, :, r, :],
                                        src[:, :, c * HD:(c + 1) * HD])
                dve.tensor_copy(WpT[:, :], banks[0][:, 2 * P:3 * P]).then_inc(wt_done, 1)
                dve.wait_ge(wt_done, 1)

        def layer_norm_stats(name, src, double):
            v_ready, s_ready, steps = sem(name + "_var"), sem(name + "_std"), sem(name + "_steps")
            ve, sd, t0, t1 = (t[:, :] for t in tiny)
            rounds = 2 if double else 1
            with nc.Block() as block:
                @block.scalar
                def _(act):
                    for r in range(rounds):
                        act.wait_ge(v_ready, r + 1)
                        act.activation(sd, ve, ACT.Sqrt).then_inc(s_ready, 1)

                @block.vector
                def _(dve):
                    with dve.Fori(0, NT // 4) as i:
                        for k in range(4):
                            ins = dve.bn_stats(stats[:, bass.ds(i * 4 + k, 1), :], src[:, bass.ds(i * 4 + k, 1), :])
                        ins.then_inc(steps, 1)
                    dve.wait_ge(steps, NT // 4)
                    chain = Chain(dve, steps)
                    chain.n = NT // 4
                    me, mo = stats[:, :, 1], stats[:, :, 4]
                    chain(dve.tensor_tensor(t0, me, mo, ALU.add))
                    chain(dve.tensor_scalar(mean[:, :], t0, 0.5, None, ALU.mult))
                    chain(dve.tensor_tensor(t0, me, mo, ALU.subtract))
                    chain(dve.scalar_tensor_tensor(t0, t0, 0.25, t0, ALU.mult, ALU.mult))
                    chain(dve.tensor_tensor(t1, stats[:, :, 2], stats[:, :, 5], ALU.add))
                    chain(dve.scalar_tensor_tensor(t0, t1, 1.0 / D, t0, ALU.mult, ALU.add))
                    for r in range(rounds):
                        if r:
                            chain(dve.tensor_tensor(t0, t0, r0[:, :], ALU.mult))
                            chain(dve.tensor_tensor(t0, t0, r0[:, :], ALU.mult))
                        dve.tensor_scalar(ve, t0, EPS, None, ALU.add).then_inc(v_ready, 1)
                        dve.wait_ge(v_ready, r + 1)
                        dve.wait_ge(s_ready, r + 1)
                        y = r01[:, :] if r else r0[:, :]
                        chain(dve.reciprocal(y, sd))
                        chain(dve.tensor_tensor(t1, y, y, ALU.mult))
                        chain(dve.tensor_tensor(t1, t1, ve, ALU.mult))
                        chain(dve.tensor_scalar(t1, t1, -0.5, 1.5, ALU.mult, ALU.add))
                        chain(dve.tensor_tensor(y, y, t1, ALU.mult))
                    if double:
                        chain(dve.tensor_tensor(r01[:, :], r01[:, :], r0[:, :], ALU.mult))

        sc = [sb(f"sc{i}", [P, HALVES, S, HEADS]) for i in range(3)]
        reduced = [sb(f"reduced{i}", [P, 512]) for i in range(2)]
        attnT = [sb(f"attnT{i}", [P, B]) for i in range(2)]
        mx = sb("mx", [P, HALVES, HEADS])
        den = sb("den", [P, HALVES, HEADS])
        logits = sb("logits", [P, NT, E])
        picks = [sb(f"pick{i}", [P, NT, E]) for i in range(2)]
        work = [sb(f"work{i}", [P, NT, E]) for i in range(2)]
        gate = [sb(f"gate{i}", [P, NT]) for i in range(2)]
        put_at = [sb(f"put_at{i}", [P, NT], U32) for i in range(2)]
        get_at = [sb(f"get_at{i}", [P, NT], U32) for i in range(2)]
        w1s = [prodQ[0][:, 2 * i:2 * i + 2, :].rearrange("p a b -> p (a b)") for i in range(2)]
        w2s = [prodQ[0][:, 4 + 2 * i:6 + 2 * i, :].rearrange("p a (c f) -> p (a c) f", f=D) for i in range(2)]
        hidden = [prodQ[1][:, 4 * i:4 * i + 4, :] for i in range(2)]
        xe = [prodQ[1][:, 8 + i, :].rearrange("p (a f) -> p a f", a=2) for i in range(4)]
        xeT = [prodQ[1][:, 12 + i, :] for i in range(2)]
        ye = [prodQ[1][:, 14 + i, :] for i in range(2)]

        def ffn_half(L, last):
            def sm(name):
                return sem(f"{L}_{name}")

            layer_norm_stats(L + "_ln01", X, True)


            G = NT // 4
            z_ready, zT_ps, zT_ready, qk_ps, q_copied, k_copied, v_ps, v_copied = credited = [
                sm(n) for n in ("z_ready", "zT_ps", "zT_ready", "qk_ps", "q_copied", "k_copied", "v_ps", "v_copied")]
            pz = [banks[0], banks[1]]
            pqk, pv = st_ps, [banks[2], banks[3]]
            with nc.Block() as block:
                @block.sync
                def _(sp):
                    for c in credited:
                        sp.sem_inc(c, CREDIT)

                @block.vector
                def _(dve):
                    def normalise(n, u):
                        dve.wait_ge(zT_ps, done(n - 2))
                        for k in range(4):
                            j = n * 4 + k
                            ins = dve.tensor_scalar(stageZ[u][:, k, :], X[:, bass.ds(j, 1), :],
                                                    mean[:, bass.ds(j, 1)], r01[:, bass.ds(j, 1)],
                                                    ALU.subtract, ALU.mult)
                        ins.then_inc(z_ready, 1)
                        for k in range(4):
                            j = n * 4 + k
                            dve.tensor_scalar(H2[:, bass.ds(j, 1), :], X[:, bass.ds(j, 1), :],
                                              mean[:, bass.ds(j, 1)], r0[:, bass.ds(j, 1)],
                                              ALU.subtract, ALU.mult)

                    def keep_k(n, u):
                        dve.wait_ge(qk_ps, done(n))
                        dve.tensor_copy(kT[:, bass.ds(n * 2, 2), :],
                                        pqk[u][:, 1, :].rearrange("p (s b) -> p s b", s=2)).then_inc(k_copied, 1)

                    ahead_of(dve, G, normalise, keep_k)

                @block.tensor
                def _(pe):
                    def turn(n, u):
                        pe.wait_ge(z_ready, done(n))
                        pe.wait_ge(zT_ready, done(n - 2))
                        for k in range(4):
                            ins = pe.transpose(pz[u][:, k * P:(k + 1) * P], stageZ[u][:, k, :], ident[:, :])
                        ins.then_inc(zT_ps, 1)

                    def project(n, u):
                        pe.wait_ge(zT_ready, done(n))
                        pe.wait_ge(q_copied, done(n - 2))
                        pe.wait_ge(k_copied, done(n - 2))
                        pe.matmul(pqk[u][:, 0, :], WqT[:, :], stageT[u][:, :], start=True, stop=True)
                        pe.matmul(pqk[u][:, 1, :], WkT[:, :], stageT[u][:, :], start=True, stop=True).then_inc(qk_ps, 1)
                        pe.wait_ge(v_copied, done(n - 2))
                        for k in range(4):
                            ins = pe.matmul(pv[u][:, k * P:(k + 1) * P], stageT[u][:, k * P:(k + 1) * P],
                                            WvT[:, :], start=True, stop=True)
                        ins.then_inc(v_ps, 1)

                    ahead_of(pe, G, turn, project)

                @block.scalar
                def _(act):
                    def scale(n, u):
                        act.wait_ge(zT_ps, done(n))
                        act.wait_ge(v_ps, done(n - 2))
                        act.activation(stageT[u][:, :], pz[u][:, :], ACT.Identity, bias=lnp[:, 1:2],
                                       scale=lnp[:, 0:1]).then_inc(zT_ready, 1)

                    def keep_qv(n, u):
                        act.wait_ge(qk_ps, done(n))
                        act.activation(qT[:, bass.ds(n * 2, 2), :],
                                       pqk[u][:, 0, :].rearrange("p (s b) -> p s b", s=2), ACT.Copy).then_inc(q_copied, 1)
                        act.wait_ge(v_ps, done(n))
                        act.activation(V[:, bass.ds(n * 4, 4), :],
                                       pv[u][:, :].rearrange("p (k f) -> p k f", k=4), ACT.Copy)\
                           .then_inc(v_copied, 1)

                    ahead_of(act, G, scale, keep_qv)

            groups = [(s, g) for s in range(S) for g in range(s // 8 + 1)]
            first = {s: groups.index((s, 0)) for s in range(S)}
            n_groups = {s: s // 8 + 1 for s in range(S)}

            def units(s, g):
                return min(4, s // 2 + 1 - 4 * g)

            prod_ready, red_ps, red_sb, tr_ps, sc_ready, centred, exped = (
                sm(n) for n in ("prod_ready", "red_ps", "red_sb", "tr_ps", "sc_ready", "centred", "exped"))
            probs_ready, pv_ready, pv_used, o_sb, y_ps, added, own = (
                sm(n) for n in ("probs_ready", "pv_ready", "pv_used", "o_sb", "y_ps", "added", "own"))
            pO, pY = st_ps[0], st_ps[1]
            LAGS = S + 3
            with nc.Block() as block:
                @block.vector
                def _(dve):
                    chain = Chain(dve, own)

                    def qk_product(s):
                        n = 2 * (s // 2 + 1)
                        if s >= 2:
                            dve.wait_ge(red_ps, first[s - 2] + n_groups[s - 2])
                        dve.tensor_tensor(prodQ[s % 2][:, 0:n, :], bcast(qT[:, s, :], 1, n), kT[:, 0:n, :],
                                          ALU.mult).then_inc(prod_ready, 1)

                    def centre(s):
                        n = s + 1
                        dve.wait_ge(sc_ready, first[s] + n_groups[s])
                        chain(dve.tensor_reduce(mx[:, :, :], sc[s % 3][:, :, 0:n, :].rearrange("p a t h -> p a h t"),
                                                AX.X, ALU.max))
                        dve.tensor_tensor(sc[s % 3][:, :, 0:n, :], sc[s % 3][:, :, 0:n, :], bcast(mx[:, :, :], 2, n),
                                          ALU.subtract).then_inc(centred, 1)

                    def normalise(s):
                        n = s + 1
                        dve.wait_ge(exped, s + 1)
                        chain(dve.tensor_reduce(den[:, :, :], sc[s % 3][:, :, 0:n, :].rearrange("p a t h -> p a h t"),
                                                AX.X, ALU.add))
                        chain(dve.reciprocal(den[:, :, :], den[:, :, :]))
                        dve.tensor_tensor(sc[s % 3][:, :, 0:n, :], sc[s % 3][:, :, 0:n, :], bcast(den[:, :, :], 2, n),
                                          ALU.mult).then_inc(probs_ready, 1)

                    def pv_product(s, a):
                        n = s + 1
                        dve.wait_ge(probs_ready, s + 1)
                        if s:
                            dve.wait_ge(pv_used, 2 * s + a - 1)
                        dve.tensor_tensor(prodV[a][:, 0:n, :].rearrange("p t (h d) -> p t h d", d=HD),
                                          bcast(sc[s % 3][:, a, 0:n, :], 3, HD),
                                          V[:, a:a + 2 * s + 1:2, :].rearrange("p t (h d) -> p t h d", d=HD),
                                          ALU.mult).then_inc(pv_ready, 1)

                    def add(s):
                        dve.wait_ge(y_ps, s + 1)
                        h = H2[:, 2 * s:2 * s + 2, :]
                        dve.tensor_tensor(h, h, pY[:, s % 2, 0:B].rearrange("p (a f) -> p a f", a=HALVES),
                                          ALU.add).then_inc(added, 1)

                    for i in range(LAGS):
                        if i < S:
                            qk_product(i)
                        if 0 <= i - 1 < S:
                            centre(i - 1)
                        if 0 <= i - 2 < S:
                            pv_product(i - 2, 0)
                        if 0 <= i - 1 < S:
                            normalise(i - 1)
                        if 0 <= i - 2 < S:
                            pv_product(i - 2, 1)
                        if 0 <= i - 3 < S:
                            add(i - 3)

                @block.tensor
                def _(pe):
                    def reduce_heads(s):
                        pe.wait_ge(prod_ready, s + 1)
                        for g in range(n_groups[s]):
                            n = first[s] + g
                            if n >= 2:
                                pe.wait_ge(red_sb, n - 1)
                            for j in range(units(s, g)):
                                u = 4 * g + j
                                ins = pe.matmul(banks[n % 2][32 * j:32 * j + 32, :], select[:, :],
                                                prodQ[s % 2][:, 2 * u:2 * u + 2, :].rearrange("p t b -> p (t b)"),
                                                start=True, stop=True)
                            ins.then_inc(red_ps, 1)

                    def to_columns(s):
                        for g in range(n_groups[s]):
                            n = first[s] + g
                            m = 32 * units(s, g)
                            pe.wait_ge(red_sb, n + 1)
                            if n >= 2:
                                pe.wait_ge(sc_ready, n - 1)
                            for c in range(4):
                                ins = pe.transpose(banks[2 + n % 2][:, c * P:c * P + m],
                                                   reduced[n % 2][0:m, c * P:(c + 1) * P], ident[0:m, 0:m])
                            ins.then_inc(tr_ps, 1)

                    def sum_pv(s, a):
                        pe.wait_ge(pv_ready, 2 * s + a + 1)
                        if a == 0 and s >= 2:
                            pe.wait_ge(o_sb, s - 1)
                        for t in range(s + 1):
                            ins = pe.matmul(pO[:, s % 2, a * P:(a + 1) * P], prodV[a][:, t, :], ident[:, :],
                                            start=(t == 0), stop=(t == s))
                        ins.then_inc(pv_used, 1)

                    def project(s):
                        pe.wait_ge(o_sb, s + 1)
                        if s >= 2:
                            pe.wait_ge(added, s - 1)
                        for a in range(HALVES):
                            ins = pe.matmul(pY[:, s % 2, a * P:(a + 1) * P], attnT[s % 2][:, a * P:(a + 1) * P],
                                            WpT[:, :], start=True, stop=True)
                        ins.then_inc(y_ps, 1)

                    for i in range(LAGS):
                        if i < S:
                            reduce_heads(i)
                        if 0 <= i - 2 < S:
                            sum_pv(i - 2, 0)
                        if i < S:
                            to_columns(i)
                        if 0 <= i - 2 < S:
                            sum_pv(i - 2, 1)
                        if 0 <= i - 3 < S:
                            project(i - 3)

                @block.scalar
                def _(act):
                    for i in range(LAGS):
                        if i < S:
                            for g in range(n_groups[i]):
                                n, m = first[i] + g, 32 * units(i, g)
                                act.wait_ge(red_ps, n + 1)
                                if n >= 2:
                                    act.wait_ge(tr_ps, n - 1)
                                act.activation(reduced[n % 2][0:m, :], banks[n % 2][0:m, :], ACT.Copy)\
                                   .then_inc(red_sb, 1)
                        if 0 <= i - 1 < S:
                            s = i - 1
                            act.wait_ge(centred, s + 1)
                            e = sc[s % 3][:, :, 0:s + 1, :]
                            act.activation(e, e, ACT.Exp, scale=SCALE).then_inc(exped, 1)
                        if i < S:
                            for g in range(n_groups[i]):
                                n, m = first[i] + g, units(i, g)
                                act.wait_ge(tr_ps, n + 1)
                                if i >= 3:
                                    act.wait_ge(pv_ready, 2 * (i - 2))
                                for par in range(2):
                                    src = banks[2 + n % 2][:, 2 * par * P:2 * (par + 1) * P]
                                    src = src.rearrange("p (a j h) -> p a j h", a=HALVES, h=32)[:, :, 0:m, 0:HEADS]
                                    t0 = 8 * g + par
                                    ins = act.activation(sc[i % 3][:, :, t0:t0 + 2 * m - 1:2, :], src, ACT.Copy)
                                ins.then_inc(sc_ready, 1)
                        if 0 <= i - 2 < S:
                            s = i - 2
                            act.wait_ge(pv_used, 2 * s + 2)
                            if s >= 2:
                                act.wait_ge(y_ps, s - 1)
                            act.activation(attnT[s % 2][:, :], pO[:, s % 2, 0:B], ACT.Copy).then_inc(o_sb, 1)

            layer_norm_stats(L + "_ln2", H2, False)

            y_ready, yT_ps, yT_ready, kept, lg_ps, lg_copied = credited = [
                sm(n) for n in ("y_ready", "yT_ps", "yT_ready", "kept", "lg_ps", "lg_copied")]
            pl = [banks[2], banks[3]]
            with nc.Block() as block:
                @block.sync
                def _(sp):
                    for c in credited:
                        sp.sem_inc(c, CREDIT)

                @block.vector
                def _(dve):
                    with dve.Fori(0, G // 2) as i:
                        for u in range(2):
                            n = i * 2 + u
                            dve.wait_ge(yT_ps, done(n - 2))
                            dve.wait_ge(kept, done(n - 2))
                            for k in range(4):
                                j = i * 8 + (4 * u + k)
                                ins = dve.tensor_scalar(stageZ[u][:, k, :], H2[:, bass.ds(j, 1), :],
                                                        mean[:, bass.ds(j, 1)], r0[:, bass.ds(j, 1)],
                                                        ALU.subtract, ALU.mult)
                            ins.then_inc(y_ready, 1)
                            dve.wait_ge(lg_ps, done(n))
                            dve.tensor_copy(logits[:, bass.ds(i * 8 + 4 * u, 4), :],
                                            pl[u][:, 0:4 * E].rearrange("p (k e) -> p k e", e=E)).then_inc(lg_copied, 1)

                @block.tensor
                def _(pe):
                    with pe.Fori(0, G // 2) as i:
                        for u in range(2):
                            n = i * 2 + u
                            pe.wait_ge(y_ready, done(n))
                            pe.wait_ge(yT_ready, done(n - 2))
                            for k in range(4):
                                ins = pe.transpose(pz[u][:, k * P:(k + 1) * P], stageZ[u][:, k, :], ident[:, :])
                            ins.then_inc(yT_ps, 1)
                            pe.wait_ge(yT_ready, done(n))
                            pe.wait_ge(lg_copied, done(n - 2))
                            for k in range(4):
                                ins = pe.matmul(pl[u][:, k * E:(k + 1) * E], stageT[u][:, k * P:(k + 1) * P],
                                                Wr[:, :], start=True, stop=True)
                            ins.then_inc(lg_ps, 1)

                @block.scalar
                def _(act):
                    with act.Fori(0, G // 2) as i:
                        for u in range(2):
                            n = i * 2 + u
                            act.wait_ge(y_ready, done(n))
                            act.activation(Z2[:, bass.ds(i * 8 + 4 * u, 4), :], stageZ[u][:, :, :], ACT.Copy)\
                               .then_inc(kept, 1)
                            act.wait_ge(yT_ps, done(n))
                            act.wait_ge(lg_ps, done(n - 2))
                            act.activation(stageT[u][:, :], pz[u][:, :], ACT.Identity, bias=lnp[:, 3:4],
                                           scale=lnp[:, 2:3]).then_inc(yT_ready, 1)

            steps, gap, gap_exp, ranks_ps, placed, scattered = (
                sm(n) for n in ("steps", "gap", "gap_exp", "ranks_ps", "placed", "scattered"))
            t0, t1, t2, t3 = (t[:, :] for t in tiny)
            with nc.Block() as block:
                @block.vector
                def _(dve):
                    chain = Chain(dve, steps)
                    wk0, wk1 = work[0][:, :, :], work[1][:, :, :]
                    lg = logits[:, :, :]
                    for k, top in ((0, t0), (1, t1)):
                        chain(dve.tensor_reduce(top, lg, AX.X, ALU.max))
                        chain(dve.tensor_tensor(wk0, lg, bcast(top, 2, E), ALU.is_equal))
                        chain(dve.tensor_tensor(wk0, wk0, bcast(rank_of[:, :], 1, NT), ALU.mult))
                        chain(dve.tensor_reduce(t2, wk0, AX.X, ALU.max))
                        chain(dve.tensor_tensor(picks[k][:, :, :], wk0, bcast(t2, 2, E), ALU.is_equal))
                        if k == 0:
                            chain(dve.scalar_tensor_tensor(lg, picks[0][:, :, :], NEG, lg, ALU.mult, ALU.add))
                    dve.tensor_tensor(t2, t1, t0, ALU.subtract).then_inc(gap, 1)
                    dve.tensor_tensor(wk0, picks[0][:, :, :], picks[1][:, :, :], ALU.add).then_inc(gap, 1)
                    dve.wait_ge(gap_exp, 1)
                    chain(dve.tensor_scalar(t0, t3, 1.0, None, ALU.add))
                    chain(dve.reciprocal(gate[0][:, :], t0))
                    chain(dve.tensor_tensor(gate[1][:, :], gate[0][:, :], t3, ALU.mult))
                    dve.wait_ge(ranks_ps, 1)
                    total = banks[1][:, 0:NT * E].rearrange("p (n e) -> p n e", e=E)
                    inside = banks[0][:, 0:NT * E].rearrange("p (n e) -> p n e", e=E)
                    chain(dve.tensor_copy(wk0, total))
                    src, dst = work[0], work[1]
                    w = 1
                    while w < NT:
                        dve.tensor_copy(dst[:, 0:w, :], src[:, 0:w, :])
                        chain(dve.tensor_tensor(dst[:, w:NT, :], src[:, w:NT, :], src[:, 0:NT - w, :], ALU.add))
                        src, dst = dst, src
                        w *= 2
                    run = src[:, :, :]
                    chain(dve.tensor_tensor(run, run, total, ALU.subtract))
                    chain(dve.tensor_tensor(run, run, inside, ALU.add))
                    for k in range(2):
                        tmp = dst[:, :, :]
                        chain(dve.tensor_tensor(tmp, picks[k][:, :, :], run, ALU.mult))
                        chain(dve.tensor_reduce(t0, tmp, AX.X, ALU.add))
                        chain(dve.tensor_tensor(tmp, picks[k][:, :, :], bcast(expert_base[:, :], 1, NT), ALU.mult))
                        chain(dve.tensor_reduce(t1, tmp, AX.X, ALU.add))
                        chain(dve.tensor_scalar(t2, t0, float(CAP), None, ALU.is_lt))
                        chain(dve.tensor_tensor(gate[k][:, :], gate[k][:, :], t2, ALU.mult))
                        chain(dve.tensor_tensor(t0, t0, t1, ALU.add))
                        chain(dve.tensor_tensor(t0, t0, t2, ALU.mult))
                        chain(dve.tensor_copy(get_at[k][:, :], t0))
                        chain(dve.tensor_scalar(t2, t2, -2.0 * E * CAP, 2.0 * E * CAP, ALU.mult, ALU.add))
                        chain(dve.tensor_tensor(t0, t0, t2, ALU.add))
                        dve.tensor_copy(put_at[k][:, :], t0).then_inc(placed, 1)
                        dve.wait_ge(placed, k + 1)

                @block.scalar
                def _(act):
                    act.wait_ge(gap, 1)
                    act.activation(t3, t2, ACT.Exp).then_inc(gap_exp, 1)

                @block.tensor
                def _(pe):
                    pe.wait_ge(gap, 2)
                    m = work[0][:, :, :].rearrange("p n e -> p (n e)")
                    pe.matmul(banks[0][:, 0:NT * E], before[:, :], m, start=True, stop=True)
                    pe.matmul(banks[1][:, 0:NT * E], ones[:, :], m, start=True, stop=True).then_inc(ranks_ps, 1)

                @block.gpsimd
                def _(pool):
                    for k in range(2):
                        pool.wait_ge(placed, k + 1)
                        for j in range(NT):
                            pool.indirect_dma_start(
                                queue, bass.IndirectOffsetOnAxis(ap=put_at[k][:, j:j + 1], axis=0),
                                Z2[:, j, :], None, bounds_check=E * CAP - 1, oob_is_err=False).then_inc(scattered, 16)
                    pool.wait_ge(scattered, 16 * 2 * NT)

            NPAIR, NC2 = E // 2, 2 * NCH
            w_in = [sm(f"w_in{u}") for u in range(2)]
            xe_in = [sm(f"xe_in{u}") for u in range(2)]
            ye_out = sm("ye_out")
            xeT_ps, xeT_ready, h_ps, h_ready, y2_ps, y2_copied, ye_free = credited = [
                sm(n) for n in ("xeT_ps", "xeT_ready", "h_ps", "h_ready", "y2_ps", "y2_copied", "ye_free")]
            px, py = [banks[0], banks[1]], [banks[2], banks[3]]
            with nc.Block() as block:
                @block.sync
                def _(sp):
                    for c in credited:
                        sp.sem_inc(c, CREDIT)
                    with sp.Fori(0, NPAIR) as i:
                        for u in range(2):
                            sp.wait_ge(y2_ps, done(i * NC2 + (u * NCH - NCH - 1)))
                            sp.dma_start(w1s[u], moe_w1[bass.ds(i * 2 + u, 1), :, :].rearrange("e p f -> p (e f)"))\
                              .then_inc(w_in[u], 16)
                            sp.dma_start(w2s[u], moe_w2[bass.ds(i * 2 + u, 1), :, :]
                                         .rearrange("e (c p) f -> p (e c) f", p=P)).then_inc(w_in[u], 16)
                            for c in range(NCH):
                                n = i * NC2 + (u * NCH + c)
                                q = u * NCH + c
                                sp.wait_ge(xeT_ps, done(n - 2))
                                sp.dma_start(xe[q % 2], queue[bass.ds(n * CH, CH), :]
                                             .rearrange("(a p) f -> p a f", p=P)).then_inc(xe_in[q % 2], 16)

                @block.tensor
                def _(pe):
                    def turn(i, q):
                        i, q = i + q // NC2, q % NC2
                        n, b = i * NC2 + q, q % 2
                        pe.wait_ge(xe_in[b], i * (16 * NCH) + 16 * (q // 2 + 1))
                        pe.wait_ge(xeT_ready, done(n - 2))
                        for a in range(2):
                            ins = pe.transpose(px[b][:, a * P:(a + 1) * P], xe[b][:, a, :], ident[:, :])
                        ins.then_inc(xeT_ps, 1)

                    def up(i, q):
                        i, q = i + q // NC2, q % NC2
                        n, b, u = i * NC2 + q, q % 2, q // NCH
                        pe.wait_ge(xeT_ready, done(n))
                        pe.wait_ge(h_ready, done(n - 2))
                        if q % NCH == 0:
                            pe.wait_ge(w_in[u], i * 32 + 32)
                        for f in range(FC):
                            ins = pe.matmul(st_ps[b][:, :, :].rearrange("p a c -> p (a c)")[:, f * CH:(f + 1) * CH],
                                            w1s[u][:, f * P:(f + 1) * P], xeT[b], start=True, stop=True)
                        ins.then_inc(h_ps, 1)

                    def down(i, q):
                        n, b, u = i * NC2 + q, q % 2, q // NCH
                        pe.wait_ge(h_ready, done(n))
                        pe.wait_ge(y2_copied, done(n - 2))
                        for a in range(2):
                            for f in range(FC):
                                ins = pe.matmul(py[b][:, a * P:(a + 1) * P],
                                                hidden[b][:, f, a * P:(a + 1) * P],
                                                w2s[u][:, f, :], start=(f == 0), stop=(f == FC - 1))
                        ins.then_inc(y2_ps, 1)

                    turn(0, 0)
                    up(0, 0)
                    turn(0, 1)
                    with pe.Fori(0, NPAIR - 1) as i:
                        for q in range(NC2):
                            up(i, q + 1)
                            turn(i, q + 2)
                            down(i, q)
                    for q in range(NC2):
                        if q + 1 < NC2:
                            up(NPAIR - 1, q + 1)
                        if q + 2 < NC2:
                            turn(NPAIR - 1, q + 2)
                        down(NPAIR - 1, q)

                @block.scalar
                def _(act):
                    with act.Fori(0, NPAIR) as i:
                        for q in range(NC2):
                            n = i * NC2 + q
                            act.wait_ge(h_ps, done(n))
                            act.wait_ge(y2_ps, done(n - 2))
                            act.activation(hidden[q % 2].rearrange("p a b -> p (a b)"),
                                           st_ps[q % 2][:, :, :].rearrange("p a c -> p (a c)"),
                                           ACT.Gelu).then_inc(h_ready, 1)

                @block.vector
                def _(dve):
                    def scale(i, q):
                        n, b = i * NC2 + q, q % 2
                        dve.wait_ge(xeT_ps, done(n))
                        dve.wait_ge(h_ps, done(n - 2))
                        dve.tensor_scalar(xeT[b], px[b][:, 0:CH], lnp[:, 2:3], lnp[:, 3:4],
                                          ALU.mult, ALU.add).then_inc(xeT_ready, 1)

                    def keep(i, q):
                        n, b = i * NC2 + q, q % 2
                        dve.wait_ge(y2_ps, done(n))
                        dve.wait_ge(ye_free, done(n - 2))
                        dve.tensor_copy(ye[b], py[b][:, 0:CH]).then_inc(y2_copied, 1)

                    scale(0, 0)
                    scale(0, 1)
                    with dve.Fori(0, NPAIR - 1) as i:
                        for q in range(NC2):
                            scale(i, q + 2)
                            keep(i, q)
                    for q in range(NC2):
                        if q + 2 < NC2:
                            scale(NPAIR - 1, q + 2)
                        keep(NPAIR - 1, q)

                @block.gpsimd
                def _(pool):
                    with pool.Fori(0, NPAIR) as i:
                        for q in range(NC2):
                            n = i * NC2 + q
                            pool.wait_ge(y2_copied, done(n))
                            pool.dma_start(answer[bass.ds(n * CH, CH), :].rearrange("(a p) f -> p a f", p=P),
                                           ye[q % 2].rearrange("p (a f) -> p a f", f=D)).then_inc(ye_out, 16)
                            pool.wait_ge(ye_out, n * 16 + 16)
                            pool.sem_inc(ye_free, 1)

            SLOTS = 8
            got = [sm(f"got{k}") for k in range(SLOTS)]
            mixed, own2, stored = sm("mixed"), sm("own2"), sm("stored")
            rows = [[prodV[k][:, s_, :] for k in range(2)] for s_ in range(SLOTS)]
            with nc.Block() as block:
                @block.gpsimd
                def _(pool):
                    for j in range(NT):
                        if j >= SLOTS:
                            pool.wait_ge(mixed, j - SLOTS + 1)
                        for k in range(2):
                            pool.indirect_dma_start(rows[j % SLOTS][k], None, answer,
                                                    bass.IndirectOffsetOnAxis(ap=get_at[k][:, j:j + 1], axis=0),
                                                    bounds_check=E * CAP - 1, oob_is_err=False)\
                                .then_inc(got[j % SLOTS], 16)

                @block.vector
                def _(dve):
                    chain = Chain(dve, own2)
                    for j in range(NT):
                        dve.wait_ge(got[j % SLOTS], 32 * (j // SLOTS + 1))
                        h = H2[:, j, :]
                        for k in range(2):
                            chain(dve.scalar_tensor_tensor(h, rows[j % SLOTS][k], gate[k][:, j:j + 1], h,
                                                           ALU.mult, ALU.add))
                        dve.scalar_tensor_tensor(X[:, j, :], h, 0.5, X[:, j, :], ALU.mult, ALU.add)\
                           .then_inc(mixed, 1)
                    dve.wait_ge(mixed, NT)

                if last:
                    @block.sync
                    def _(sp):
                        for j in range(0, NT, 4):
                            sp.wait_ge(mixed, j + 4)
                            sp.dma_start(outv[:, j:j + 4, :], X[:, j:j + 4, :]).then_inc(stored, 16)
                        sp.wait_ge(stored, 16 * (NT // 4))

        PART_Q, PART_K = (0, 0, 1, 1, 0, 2), (0, 1, 0, 1, 2, 0)
        MROW = 64
        KB = B // P
        flat = "p s b -> p (s b)"
        stack_space = [prodQ[0][:, :, :], prodQ[1][:, :, :], H2[:, :, :].rearrange("p n f -> p (n f)")
                       .rearrange("p (s b) -> p s b", s=S)]
        qs, ks = ([m.rearrange(flat)[:, w * 2048:(w + 1) * 2048].bitcast(BF16)
                   .rearrange("p (h t) -> p h t", h=HEADS) for m in stack_space] for w in range(2))
        PT = [prodV[i // 2][:, :, :].rearrange(flat)[:, (i % 2) * 1024:(i % 2 + 1) * 1024]
              .rearrange("p (j c) -> p j c", j=2) for i in range(4)]
        Vp = [qT[:, 4 * i:4 * i + 4, :].rearrange(flat).rearrange("p (a h c) -> p a h c", a=KB, c=32)
              for i in range(3)]
        parts = [[kT[:, 3 * (2 * w + i):3 * (2 * w + i) + 3, :].rearrange(flat).bitcast(BF16)
                  .rearrange("p (c n) -> p c n", c=3) for i in range(2)] for w in range(2)]
        rest = [kT[:, 12 + 2 * w:14 + 2 * w, :].rearrange(flat) for w in range(2)]
        sums = [kT[:, i, :] for i in range(2)]
        heads_out = [kT[:, i, :].rearrange("p (a f) -> p a f", a=KB) for i in (2, 3, 13)]
        heads_outT = kT[:, 4, :]
        mx3 = kT[:, 5, 0:3 * HEADS].rearrange("p (h c) -> p h c", c=3)
        negm = kT[:, 6, 0:KB * HEADS].rearrange("p (a h) -> p a h", a=KB)
        rec = kT[:, 7, 0:KB * 4].rearrange("p (a j) -> p a j", a=KB)
        m_rest = [kT[0:HEADS, 8 + i, :] for i in range(2)]
        m_parts = kT[0:HEADS, 10:12, :].rearrange(flat).bitcast(BF16)[:, 0:3 * B].rearrange("p (c t) -> p c t", c=3)

        def attention_half():
            def sm(name):
                return sem(f"at_{name}")

            layer_norm_stats("at_ln01", X, True)
            grow, shift = tiny[0], tiny[1]

            G = NT // 4
            z_ready, zT_ps, zT_ready, qk_ps, hi_ready, rest_ready, mid_ready, lo_ready, v_ps, v_copied, \
                parts_out = credited = [sm(n) for n in (
                    "z_ready", "zT_ps", "zT_ready", "qk_ps", "hi_ready", "rest_ready", "mid_ready", "lo_ready",
                    "v_ps", "v_copied", "parts_out")]
            coef, q_out, k_out, counted_groups = sm("coef"), sm("q_out"), sm("k_out"), sm("counted_groups")
            pz = [banks[0], banks[1]]
            pqk, pv = st_ps, [banks[2], banks[3]]
            with nc.Block() as block:
                @block.sync
                def _(sp):
                    for c in credited:
                        sp.sem_inc(c, CREDIT)
                    with sp.Fori(0, G // 2) as i:
                        for u in range(2):
                            n = i * 2 + u
                            sp.wait_ge(lo_ready, done(n))
                            for w, (dst, s_) in enumerate(((q_parts, q_out), (k_parts, k_out))):
                                for b in range(2):
                                    sp.dma_start(dst[bass.ds(i * 4 + (2 * u + b), 1), :, :, :]
                                                 .rearrange("a c f t -> f (a c) t"),
                                                 parts[w][u][:, :, b * B:(b + 1) * B]).then_inc(s_, 16)
                            sp.wait_ge(q_out, n * 32 + 32)
                            sp.wait_ge(k_out, n * 32 + 32)
                            sp.sem_inc(parts_out, 1)

                @block.vector
                def _(dve):
                    dve.tensor_scalar(grow[:, :], r0[:, :], 1.0, None, ALU.add)
                    dve.tensor_tensor(shift[:, :], mean[:, :], r0[:, :], ALU.mult).then_inc(coef, 1)
                    dve.wait_ge(coef, 1)

                    def normalise(n, u):
                        dve.wait_ge(zT_ps, done(n - 2))
                        for k in range(4):
                            j = n * 4 + k
                            ins = dve.tensor_scalar(stageZ[u][:, k, :], X[:, bass.ds(j, 1), :],
                                                    mean[:, bass.ds(j, 1)], r01[:, bass.ds(j, 1)],
                                                    ALU.subtract, ALU.mult)
                        ins.then_inc(z_ready, 1)
                        for k in range(4):
                            j = n * 4 + k
                            dve.tensor_scalar(X[:, bass.ds(j, 1), :], X[:, bass.ds(j, 1), :],
                                              grow[:, bass.ds(j, 1)], shift[:, bass.ds(j, 1)],
                                              ALU.mult, ALU.subtract)

                    def leave_rest(n, u):
                        dve.wait_ge(hi_ready, done(n))
                        dve.wait_ge(lo_ready, done(n - 1))
                        for w in range(2):
                            ins = dve.tensor_tensor(rest[w], pqk[u][:, w, :], parts[w][u][:, 0, :], ALU.subtract)
                        ins.then_inc(rest_ready, 1)

                    ahead_of(dve, G, normalise, leave_rest)

                @block.gpsimd
                def _(pool):
                    with pool.Fori(0, G // 2) as i:
                        for u in range(2):
                            n = i * 2 + u
                            pool.wait_ge(rest_ready, done(n))
                            pool.sem_inc(counted_groups, 1)
                            for w in range(2):
                                ins = pool.tensor_copy(parts[w][u][:, 1, :], rest[w])
                            ins.then_inc(mid_ready, 1)
                            pool.wait_ge(mid_ready, done(n))
                            for w in range(2):
                                ins = pool.tensor_tensor(parts[w][u][:, 2, :], rest[w], parts[w][u][:, 1, :],
                                                         ALU.subtract)
                            ins.then_inc(lo_ready, 1)

                @block.tensor
                def _(pe):
                    def turn(n, u):
                        pe.wait_ge(z_ready, done(n))
                        pe.wait_ge(zT_ready, done(n - 2))
                        for k in range(4):
                            ins = pe.transpose(pz[u][:, k * P:(k + 1) * P], stageZ[u][:, k, :], ident[:, :])
                        ins.then_inc(zT_ps, 1)

                    def project(n, u):
                        pe.wait_ge(zT_ready, done(n))
                        pe.wait_ge(rest_ready, done(n - 2))
                        pe.matmul(pqk[u][:, 0, :], Wqa[:, :], stageT[u][:, :], start=True, stop=True)
                        pe.matmul(pqk[u][:, 1, :], Wka[:, :], stageT[u][:, :], start=True, stop=True).then_inc(qk_ps, 1)
                        pe.wait_ge(v_copied, done(n - 2))
                        for k in range(4):
                            ins = pe.matmul(pv[u][:, k * P:(k + 1) * P], stageT[u][:, k * P:(k + 1) * P],
                                            Wva[:, :], start=True, stop=True)
                        ins.then_inc(v_ps, 1)

                    ahead_of(pe, G, turn, project)

                @block.scalar
                def _(act):
                    def scale(n, u):
                        act.wait_ge(zT_ps, done(n))
                        act.wait_ge(v_ps, done(n - 2))
                        act.activation(stageT[u][:, :], pz[u][:, :], ACT.Identity, bias=lnp[:, 5:6],
                                       scale=lnp[:, 4:5]).then_inc(zT_ready, 1)

                    def high_parts(n, u):
                        act.wait_ge(qk_ps, done(n))
                        act.wait_ge(parts_out, done(n - 2))
                        for w in range(2):
                            ins = act.activation(parts[w][u][:, 0, :], pqk[u][:, w, :], ACT.Copy)
                        ins.then_inc(hi_ready, 1)
                        act.wait_ge(v_ps, done(n))
                        act.activation(V[:, bass.ds(n * 4, 4), :],
                                       pv[u][:, :].rearrange("p (k f) -> p k f", k=4), ACT.Copy)\
                           .then_inc(v_copied, 1)

                    ahead_of(act, G, scale, high_parts)

            PAIRS = HEADS // 2
            PERB = 13 * 16
            LAG = 2

            def maxima_at(at, pr):
                of, h = (at.next(), HEADS // 2 + 2 * pr) if pr < PAIRS // 2 else (at.next(2), 2 * pr - HEADS // 2)
                return [(of, h), (of, h + 1)] if exists(of) else []

            cleared, counted = sm("cleared"), sm("counted")
            stack_in = [sm(f"stack_in{u}") for u in range(3)]
            m_in = [sm(f"m_in{u}") for u in range(3)]
            s_ps, s_max, m_ready, mp_ready, st_done, exp_done, masked, pv_done, sums_copied, vp_ready, \
                shared_ps, shared_free, heads_done, outT_ready, rec_ready, dve_own = credited = [sm(n) for n in (
                    "s_ps", "s_max", "m_ready", "mp_ready", "st_done", "exp_done", "masked", "pv_done",
                    "sums_copied", "vp_ready", "shared_ps", "shared_free", "heads_done", "outT_ready", "rec_ready", "dve_own")]
            s_bank, pv_bank, shared = [banks[0], banks[1]], banks[2], banks[3]

            SUM2, SUM3, TURN, OUT, MAXIMA, SUM0, SUM1 = range(7)

            def use(b, k):
                return b * 7 + (k - 3)

            def sum_use(b, g):
                return use(b, SUM0 + g) if g < 2 else use(b + 1, SUM2 + g - 2)

            class At:
                def __init__(self, i, c):
                    self.i, self.c = i, c
                    self.b, self.v, self.turn = i * 3 + c, c % 3, i + c // 3

                def next(self, k=1):
                    return At(self.i, self.c + k)

            def exists(at):
                return not isinstance(at.b, int) or at.b < S

            def all_sequences(engine, sequence):
                sequence(At(0, 0), True, False)
                with engine.Fori(0, (S - 4) // 3) as i:
                    for c in range(1, 4):
                        sequence(At(i, c), False, False)
                for b in range(S - 3, S):
                    sequence(At(0, b), False, b == S - 1)

            with nc.Block() as block:
                @block.sync
                def _(sp):
                    for c in credited:
                        sp.sem_inc(c, CREDIT)

                    def load(at):
                        for r in range(6):
                            for stack, src, p_ in ((qs, q_parts, PART_Q), (ks, k_parts, PART_K)):
                                sp.dma_start(stack[at.v][HD * r:HD * (r + 1), :, :],
                                             src[bass.ds(at.b, 1), p_[r], :, :]
                                             .rearrange("a (h d) t -> d (a h) t", d=HD)).then_inc(stack_in[at.v], 16)
                        sp.dma_start(qs[at.v][MROW:MROW + 3, :, :].rearrange("p h t -> p (h t)"), zero_rows)\
                          .then_inc(stack_in[at.v], 16)

                    def send_maxima(at):
                        sp.wait_ge(mp_ready, done(at.b))
                        for c in range(3):
                            sp.dma_start(qs[at.v][MROW + c:MROW + c + 1, :, :], m_parts[:, c:c + 1, :])\
                              .then_inc(m_in[at.v], 16)

                    def sequence(at, first, last):
                        if exists(at.next(2)):
                            sp.wait_ge(st_done, done(at.b * PAIRS - 1))
                            load(at.next(2))
                        if not last:
                            send_maxima(at.next())

                    sp.wait_ge(cleared, 1)
                    load(At(0, 0))
                    load(At(0, 1))
                    send_maxima(At(0, 0))
                    all_sequences(sp, sequence)

                @block.gpsimd
                def _(pool):
                    for m in stack_space:
                        pool.memset(m, 0.0)
                    for v in Vp:
                        pool.memset(v, 0.0)
                    pool.drain().then_inc(cleared, 1)
                    pool.wait_ge(cleared, 1)
                    for v in Vp:
                        ins = pool.memset(v[:, :, :, HD:HD + 1], 1.0)
                    ins.then_inc(cleared, 1)
                    pool.wait_ge(cleared, 2)
                    for n, k_ in enumerate(ks):
                        pool.memset(k_[MROW:MROW + 3, :, :], 1.0).then_inc(cleared, 1)
                        pool.wait_ge(cleared, 3 + n)

                    def wait_count(s_, value):
                        pool.wait_ge(s_, value)
                        pool.sem_inc(counted, 1)

                    def spread_v(at):
                        wait_count(pv_done, done((at.b - 2) * PAIRS - 1))
                        for a in range(KB):
                            ins = pool.tensor_copy(Vp[at.v][:, a, :, 0:HD],
                                                   V[:, bass.ds(at.b * KB + a, 1), :]
                                                   .rearrange("p a (h d) -> p (a h) d", d=HD))
                        ins.then_inc(vp_ready, 1)

                    def sequence(at, first, last):
                        for pr in range(PAIRS):
                            wait_count(exp_done, done(at.b * PAIRS + pr))
                            diag = PT[pr % 4].rearrange("p j (c s) -> p (j c) s", s=P)[:, 0:8:2, :]
                            pool.affine_select(out=diag, in_=diag, compare_op=ALU.is_ge, fill=0.0, base=0,
                                               pattern=[[0, 4], [1, P]], channel_multiplier=-1)\
                                .then_inc(masked, 1)
                            if pr == 3 and not last:
                                spread_v(at.next())

                    spread_v(At(0, 0))
                    all_sequences(pool, sequence)

                @block.tensor
                def _(pe):
                    def scores(at, h):
                        n = at.b * HEADS + h
                        ps, q, k = s_bank[h % 2], qs[at.v][:, h, :], ks[at.v][:, h, :]
                        if h == 0:
                            pe.wait_ge(stack_in[at.v], (at.turn + 1) * PERB)
                        pe.wait_ge(s_max, done(n - 2))
                        pe.matmul(ps[:, 0:2 * P], identb[:, :], causal[:, :], start=True, stop=False,
                                  skip_group_check=True)
                        pe.matmul(ps[:, 0:P], q[:, 0:P], k[:, 0:P], start=False, stop=False, skip_group_check=True)
                        pe.matmul(ps[:, P:2 * P], q[:, P:2 * P], k[:, P:2 * P], start=False, stop=False,
                                  skip_group_check=True)
                        pe.matmul(ps[:, 2 * P:3 * P], q[:, P:2 * P], k[:, 0:P], start=False, stop=True,
                                  skip_group_check=True).then_inc(s_ps, 1)

                    def maxima_rows(b, n):
                        pe.wait_ge(m_ready, done(b))
                        pe.wait_ge(shared_free, done(n - 1))
                        for a in range(KB):
                            ins = pe.transpose(shared[0:HEADS, a * P:(a + 1) * P], negm[:, a, :], ident[:, :])
                        ins.then_inc(shared_ps, 1)

                    def scores_t(at, pr):
                        n = at.b * PAIRS + pr
                        if pr == 0:
                            pe.wait_ge(m_in[at.v], at.turn * 48 + 48)
                        pe.wait_ge(exp_done, done(n - 2))
                        for j in range(2):
                            h = 2 * pr + j
                            ps, q, k = st_ps[pr % 2][:, j, :], qs[at.v][:, h, :], ks[at.v][:, h, :]
                            pe.matmul(ps[:, 0:B], k[:, 0:P], q, start=True, stop=True)
                            ins = pe.matmul(ps[:, B:B + P], k[:, P:2 * P], q[:, P:2 * P], start=True, stop=True)
                        ins.then_inc(st_done, 1)

                    def weighted_sum(at, pr):
                        n = at.b * PAIRS + pr
                        pe.wait_ge(masked, done(n))
                        if pr == 0:
                            pe.wait_ge(vp_ready, done(at.b))
                        if pr % 2 == 0:
                            pe.wait_ge(sums_copied, done(at.b * 4 + (pr // 2 - 1)))
                        for j in range(2):
                            h = 2 * pr + j
                            o = pv_bank[32 * (h % 4):32 * (h % 4) + 32, 0:B]
                            pe.matmul(o, Vp[at.v][:, 0, h, :], PT[pr % 4][:, j, 0:B], start=True, stop=False)
                            ins = pe.matmul(o[:, P:B], Vp[at.v][:, 1, h, :], PT[pr % 4][:, j, B:B + P],
                                            start=False, stop=True)
                        ins.then_inc(pv_done, 1)

                    def sums_to_tokens(at, g, skipped=0):
                        pe.wait_ge(sums_copied, done(at.b * 4 + g))
                        pe.wait_ge(shared_free, done(sum_use(at.b, g) - 1 - skipped))
                        for a in range(KB):
                            ins = pe.transpose(shared[:, a * P:(a + 1) * P], sums[g % 2][:, a * P:(a + 1) * P],
                                               ident[:, :])
                        ins.then_inc(shared_ps, 1)

                    def turn_heads(at, skipped=0):
                        pe.wait_ge(heads_done, done(at.b * 4 + 3))
                        pe.wait_ge(shared_free, done(use(at.b + 1, TURN) - 1 - skipped))
                        for a in range(KB):
                            ins = pe.transpose(shared[:, a * P:(a + 1) * P], heads_out[at.v][:, a, :], ident[:, :])
                        ins.then_inc(shared_ps, 1)

                    def project(at, skipped=0):
                        pe.wait_ge(outT_ready, done(at.b))
                        pe.wait_ge(shared_free, done(use(at.b + 1, OUT) - 1 - skipped))
                        for a in range(KB):
                            ins = pe.matmul(shared[:, a * P:(a + 1) * P], heads_outT[:, a * P:(a + 1) * P],
                                            Woa[:, :], start=True, stop=True)
                        ins.then_inc(shared_ps, 1)

                    def sequence(at, first, last):
                        before_, next_ = at.next(-1), at.next()
                        for pr in range(PAIRS):
                            todo = maxima_at(at, pr)
                            if todo:
                                scores(*todo.pop(0))
                            scores_t(at, pr)
                            if pr >= LAG:
                                weighted_sum(at, pr - LAG)
                            elif not first:
                                weighted_sum(before_, PAIRS + pr - LAG)
                            if todo:
                                scores(*todo.pop(0))
                            if not first:
                                if pr == 0:
                                    sums_to_tokens(before_, 2)
                                if pr == 2:
                                    sums_to_tokens(before_, 3)
                                if pr == 3:
                                    turn_heads(before_)
                                if pr == 4:
                                    project(before_)
                            if pr == 4 and not last:
                                maxima_rows(next_.b, use(at.b, MAXIMA))
                            if pr == 5:
                                sums_to_tokens(at, 0, last)
                            if pr == 6:
                                sums_to_tokens(at, 1, last)

                    pe.wait_ge(cleared, 5)
                    for h in range(HEADS):
                        scores(At(0, 0), h)
                    for h in range(HEADS // 2):
                        scores(At(0, 1), h)
                    maxima_rows(0, 0)
                    all_sequences(pe, sequence)
                    at = At(0, S - 1)
                    weighted_sum(at, PAIRS - 2)
                    sums_to_tokens(at, 2, 1)
                    weighted_sum(at, PAIRS - 1)
                    sums_to_tokens(at, 3, 1)
                    turn_heads(at, 1)
                    project(at, 1)

                @block.scalar
                def _(act):
                    def copy_sums(at, g, skipped=0):
                        act.wait_ge(pv_done, done(at.b * PAIRS + (2 * g + 1)))
                        act.wait_ge(shared_ps, done(sum_use(at.b, g - 2) - skipped if g >= 2
                                                 else sum_use(at.b - 1, g + 2)))
                        act.activation(sums[g % 2], pv_bank[:, 0:B], ACT.Copy).then_inc(sums_copied, 1)

                    def copy_heads(at, skipped=0):
                        act.wait_ge(shared_ps, done(use(at.b + 1, TURN) - skipped))
                        act.activation(heads_outT, shared[:, 0:B], ACT.Copy).then_inc(shared_free, 1)
                        act.wait_ge(shared_free, done(use(at.b + 1, TURN) - skipped))
                        act.sem_inc(outT_ready, 1)

                    def sequence(at, first, last):
                        for pr in range(PAIRS):
                            n = at.b * PAIRS + pr
                            act.wait_ge(st_done, done(n))
                            act.wait_ge(pv_done, done(n - 4))
                            act.activation(PT[pr % 4][:, :, 0:3 * P], st_ps[pr % 2][:, :, 0:3 * P], ACT.Exp,
                                           scale=SCALE).then_inc(exp_done, 1)
                            if pr == 1 and not first:
                                copy_sums(at.next(-1), 3)
                            if pr == 3 and not first:
                                copy_heads(at.next(-1))
                            if pr in (3, 5, 7):
                                copy_sums(at, (pr - 3) // 2, last)

                    all_sequences(act, sequence)
                    copy_sums(At(0, S - 1), 3, 1)
                    copy_heads(At(0, S - 1), 1)

                @block.vector
                def _(dve):
                    def maxima(b, h):
                        n = b * HEADS + h
                        if h == 0:
                            dve.wait_ge(m_ready, done(b - 1))
                        dve.wait_ge(s_ps, done(n))
                        dve.tensor_reduce(mx3[:, h, :], s_bank[h % 2][:, 0:3 * P].rearrange("p (c t) -> p c t", c=3),
                                          AX.X, ALU.max, negate=True).then_inc(s_max, 1)

                    def combine(b):
                        dve.wait_ge(s_max, done(b * HEADS + (HEADS - 1)))
                        dve.tensor_copy(negm[:, 0, :], mx3[:, :, 0])
                        dve.tensor_tensor(negm[:, 1, :], mx3[:, :, 1], mx3[:, :, 2], ALU.min).then_inc(m_ready, 1)

                    def split_maxima(at, n):
                        dve.wait_ge(shared_ps, done(n))
                        src = shared[0:HEADS, 0:B]
                        if at.c:
                            last_ = at.next(-1)
                            dve.wait_ge(m_in[last_.v], last_.turn * 48 + 48)
                        own = at.b * 2
                        dve.tensor_copy(m_parts[:, 0, :], src).then_inc(dve_own, 1)
                        dve.wait_ge(dve_own, done(own))
                        dve.tensor_tensor(m_rest[0], src, m_parts[:, 0, :], ALU.subtract).then_inc(shared_free, 1)
                        dve.wait_ge(shared_free, done(n))
                        dve.tensor_copy(m_parts[:, 1, :], m_rest[0]).then_inc(dve_own, 1)
                        dve.wait_ge(dve_own, done(own + 1))
                        dve.tensor_tensor(m_parts[:, 2, :], m_rest[0], m_parts[:, 1, :], ALU.subtract)\
                           .then_inc(mp_ready, 1)

                    def normalise(at, g, skipped=0):
                        dve.wait_ge(shared_ps, done(sum_use(at.b, g) - skipped))
                        src = shared[:, 0:B].rearrange("p (a j c) -> p a j c", a=KB, c=32)
                        dve.reciprocal(rec, src[:, :, :, HD]).then_inc(rec_ready, 1)
                        dve.wait_ge(rec_ready, done(at.b * 4 + g))
                        out_ = heads_out[at.v][:, :, 32 * g:32 * g + 32].rearrange("p a (j d) -> p a j d", d=HD)
                        dve.tensor_tensor(out_, src[:, :, :, 0:HD], bcast(rec, 3, HD), ALU.mult)\
                           .then_inc(heads_done, 1)
                        dve.wait_ge(heads_done, done(at.b * 4 + g))
                        dve.sem_inc(shared_free, 1)

                    def add(at, skipped=0):
                        dve.wait_ge(shared_ps, done(use(at.b + 1, OUT) - skipped))
                        xb = X[:, bass.ds(at.b * KB, KB), :]
                        dve.tensor_tensor(xb, xb, shared[:, 0:B].rearrange("p (a f) -> p a f", a=KB), ALU.add)\
                           .then_inc(shared_free, 1)

                    def sequence(at, first, last):
                        before_, next_ = at.next(-1), at.next()
                        for pr in range(PAIRS):
                            for of, h in maxima_at(at, pr):
                                maxima(of.b, h)
                            if not first:
                                if pr == 0:
                                    normalise(before_, 2)
                                if pr == 2:
                                    normalise(before_, 3)
                                if pr == 4:
                                    add(before_)
                            if pr == 3 and not last:
                                combine(next_.b)
                            if pr == 4 and not last:
                                split_maxima(next_, use(at.b, MAXIMA))
                            if pr == 5:
                                normalise(at, 0, last)
                            if pr == 6:
                                normalise(at, 1, last)

                    for h in range(HEADS):
                        maxima(0, h)
                    combine(0)
                    for h in range(HEADS // 2):
                        maxima(1, h)
                    split_maxima(At(0, 0), 0)
                    all_sequences(dve, sequence)
                    at = At(0, S - 1)
                    normalise(at, 2, 1)
                    normalise(at, 3, 1)
                    add(at, 1)

            if stages == 2:
                stored = sm("stored")
                with nc.Block() as block:
                    @block.sync
                    def _(sp):
                        sp.dma_start(outv, X[:, :, :]).then_inc(stored, 16)
                        sp.wait_ge(stored, 16)

        ffn_half("f1", stages == 1)
        if stages >= 2:
            recycle_semaphores()
            attention_half()
        if stages >= 3:
            recycle_semaphores()
            ffn_half("f2", True)


_INS = ["L0_attn_x", "L0_attn_ln_w", "L0_attn_ln_b", "L0_attn_wq", "L0_attn_wk", "L0_attn_wv", "L0_attn_wo",
        "L0_ffn_ln1_weight", "L0_ffn_ln1_bias", "L0_ffn_ln2_weight", "L0_ffn_ln2_bias", "L0_ffn_qkv_weight",
        "L0_ffn_proj_weight", "L0_ffn_router_weight", "L0_ffn_moe_w1", "L0_ffn_moe_w2"]
_OUTS = [((16, 256, 128), "float32")]


def kernel(**inputs):
    import numpy as _np
    import concourse.bacc as _bacc
    from concourse import mybir as _mybir
    from concourse.bass_utils import run_bass_kernel_spmd as _run

    nc = _bacc.Bacc("TRN2", target_bir_lowering=False, num_devices=1)
    arrays, args = {}, []
    for name in _INS:
        a = _np.ascontiguousarray(inputs[name])
        arrays[f"in_{name}_dram"] = a
        args.append(nc.dram_tensor(f"in_{name}_dram", a.shape, _mybir.dt.from_np(a.dtype), kind="ExternalInput").ap())
    for i, (shape, dtype) in enumerate(_OUTS):
        dt = _mybir.dt.from_np(_np.dtype(dtype))
        args.append(nc.dram_tensor(f"out_{i}_dram", shape, dt, kind="ExternalOutput").ap())
    macaron_kernel(nc, *args)
    r = _run(nc, [arrays], core_ids=[0])
    got = tuple(r.results[0][f"out_{i}_dram"] for i in range(len(_OUTS)))
    return got[0]
```

```python
from contextlib import ExitStack

import numpy as np

import concourse.bass as bass
from concourse import mybir

F32 = mybir.dt.float32
BF16 = mybir.dt.bfloat16
U32 = mybir.dt.uint32
I32 = mybir.dt.int32
ALU = mybir.AluOpType
ACT = mybir.ActivationFunctionType
AX = mybir.AxisListType

P = 128
EPS = 1e-5
HEADS, HD = 16, 8
SCALE = HD ** -0.5
NEG = -1e30


CREDIT = 32


def done(n):
    return n + (1 + CREDIT)


class Chain:

    def __init__(self, engine, sem):
        self.engine, self.sem, self.n = engine, sem, 0

    def __call__(self, *step):
        self.n += len(step)
        for ins in step:
            ins.then_inc(self.sem, 1)
        self.engine.wait_ge(self.sem, self.n)


def ahead_of(engine, count, ahead, rest, by=1):
    for n in range(by):
        ahead(n, n % 2)
    with engine.Fori(0, count // 2 - 1) as i:
        for u in range(2):
            ahead(i * 2 + (u + by), (u + by) % 2)
            rest(i * 2 + u, u)
    for n in range(count - 2, count):
        if n + by < count:
            ahead(n + by, (n + by) % 2)
        rest(n, n % 2)


def bcast(ap, axis, n):
    wide = ap.unsqueeze(axis)
    shape = list(wide.shape)
    shape[axis] = n
    return wide.broadcast_to(shape)


def macaron_kernel(nc, x, at_ln_w, at_ln_b, wq, wk, wv, wo, ln1_w, ln1_b, ln2_w, ln2_b,
                   qkv_w, proj_w, router_w, moe_w1, moe_w2, out, stages=3):
    S, B, D = x.shape
    NT = S * B // P
    HALVES = B // P
    E, _, FF = moe_w1.shape
    FC = FF // P
    CAP = -(-S * B * 2 * 5 // (4 * E))
    CH = 2 * P
    NCH = CAP // CH
    assert CAP % CH == 0 and D == P and NCH % 2 == 1 and E % 2 == 0

    xv = x.rearrange("s (a p) f -> p (s a) f", p=P)
    outv = out.rearrange("s (a p) f -> p (s a) f", p=P)
    ROW = D + 4
    TOKEN, FIRST, RATIO = D, D + 1, D + 2
    N = S * B
    queues = [nc.dram_tensor(f"queue{i}", [E * CAP, ROW], F32).ap() for i in range(2)]
    answers_of = [nc.dram_tensor(f"answers{i}", [2 * N, D], F32).ap() for i in range(2)]
    q_parts = nc.dram_tensor("q_parts", [S, 3, D, B], BF16).ap()
    k_parts = nc.dram_tensor("k_parts", [S, 3, D, B], BF16).ap()
    zero_rows = nc.dram_tensor("zero_rows", [3, HEADS * B], BF16).ap()

    ctx = ExitStack()
    with ctx:
        def sb(name, shape, dt=F32):
            return ctx.enter_context(nc.sbuf_tensor(name, shape, dt))

        taken = []

        def sem(name):
            taken.append(nc.alloc_semaphore(name))
            return taken[-1]

        def recycle_semaphores():
            nc.clear_and_free_semaphores(taken)
            taken.clear()
            nc.all_engine_barrier()

        banks = [ctx.enter_context(nc.psum_tensor(f"bank{i}", [P, 512], F32)) for i in range(2)]
        st_ps = [ctx.enter_context(nc.psum_tensor(f"pair{i}", [P, 2, 512], F32)) for i in range(2)]
        banks += [ctx.enter_context(nc.psum_tensor(f"bank{i}", [P, 512], F32)) for i in (2, 3)]

        X = sb("X", [P, NT, D])
        H2 = sb("H2", [P, NT, D])
        qT = sb("qT", [P, S, B])
        kT = sb("kT", [P, S, B])
        V = sb("V", [P, NT, D])
        prodQ = [sb(f"prodQ{i}", [P, S, B]) for i in range(2)]
        prodV = [sb(f"prodV{i}", [P, S, D]) for i in range(2)]
        stageZ = [sb(f"stageZ{i}", [P, 4, D]) for i in range(2)]
        stageT = [sb(f"stageT{i}", [P, 4 * P]) for i in range(2)]
        Z2 = sb("Z2", [P, NT, ROW])

        ident = sb("ident", [P, P])
        onesb = sb("onesb", [P, P], BF16)
        beforeb = sb("beforeb", [P, P], BF16)
        blank = sb("blank", [P, ROW])
        before = sb("before", [P, P])
        select = sb("select", [P, 32])
        causal = sb("causal", [P, 2 * P], BF16)
        identb = sb("identb", [P, P], BF16)
        WqT, WkT, WvT, WpT = (sb(n, [P, P]) for n in ("WqT", "WkT", "WvT", "WpT"))
        Wqa, Wka, Wva, Woa = (sb(n, [P, P]) for n in ("Wqa", "Wka", "Wva", "Woa"))
        Wr = sb("Wr", [P, E])
        lnp = sb("lnp", [P, 6])
        eps = sb("eps", [P, 1])
        expert_base = sb("expert_base", [P, E])
        rank_of = sb("rank_of", [P, E])
        stats = sb("stats", [P, NT, 6])
        mean = sb("mean", [P, NT])
        factors = sb("factors", [P, 2, NT])
        r0, r01 = factors[:, 0, :], factors[:, 1, :]
        variances = sb("variances", [P, 2, NT])
        newton = sb("newton", [P, 2, NT])
        tiny = [sb(f"tiny{i}", [P, NT]) for i in range(4)]

        def inverse_sqrt(chain, y, ve, t):
            dve = chain.engine
            chain(dve.tensor_scalar(y.bitcast(I32), ve.bitcast(I32), -0.5, float(0x5F3759DF), ALU.mult, ALU.add))
            for _ in range(3):
                chain(dve.scalar_tensor_tensor(t, y, -0.5, y, ALU.mult, ALU.mult))
                chain(dve.tensor_tensor(t, t, ve, ALU.mult))
                chain(dve.scalar_tensor_tensor(y, t, 1.5, y, ALU.add, ALU.mult))

        def norm_factors(chain, a, b, double):
            dve, n = chain.engine, 2 if double else 1
            var, t, both = tiny[0][:, a:b], tiny[1][:, a:b], tiny[2][:, a:b]
            me, mo = stats[:, a:b, 1], stats[:, a:b, 4]
            chain(dve.tensor_tensor(t, me, mo, ALU.subtract),
                  dve.tensor_tensor(var, stats[:, a:b, 2], stats[:, a:b, 5], ALU.add),
                  dve.tensor_tensor(both, me, mo, ALU.add))
            chain(dve.scalar_tensor_tensor(t, t, 0.25, t, ALU.mult, ALU.mult),
                  dve.tensor_scalar(mean[:, a:b], both, 0.5, None, ALU.mult))
            chain(dve.scalar_tensor_tensor(var, var, 1.0 / D, t, ALU.mult, ALU.add))
            step = [dve.tensor_scalar(variances[:, 0, a:b], var, EPS, None, ALU.add)]
            if double:
                step.append(dve.tensor_scalar(variances[:, 1, a:b], var, 1.0 + EPS, EPS * EPS, ALU.mult, ALU.add))
            chain(*step)
            inverse_sqrt(chain, factors[:, 0:n, a:b], variances[:, 0:n, a:b], newton[:, 0:n, a:b])

        def input_norm(dve, own):
            norm_factors(Chain(dve, own), 0, NT, True)

        filled = nc.alloc_semaphore("filled")
        loads, consts, wt_ps, wt_done = (sem(n) for n in ("loads", "consts", "wt_ps", "wt_done"))
        x_in = [sem(f"x_in{i}") for i in range(4)]
        x_stats, ln_own = sem("x_stats"), sem("ln_own")
        qkv_in = [prodV[0][:, i, :] for i in range(2)]
        proj_in = prodV[0][:, 2, :]
        with nc.Block() as block:
            @block.sync
            def _(sp):
                for i in range(4):
                    sp.dma_start(X[:, 8 * i:8 * i + 8, :], xv[:, 8 * i:8 * i + 8, :]).then_inc(x_in[i], 16)
                for i, v in enumerate((ln1_w, ln1_b, ln2_w, ln2_b, at_ln_w, at_ln_b)):
                    sp.dma_start(lnp[:, i:i + 1], v.rearrange("(p a) -> p a", a=1)).then_inc(loads, 16)
                sp.wait_ge(consts, 1)
                sp.dma_start(zero_rows[:, :], prodQ[0][0:3, 0:HEADS // 2, :].rearrange("p s b -> p (s b)")
                             .bitcast(BF16)).then_inc(loads, 16)
                sp.wait_ge(loads, 16 * 14)
                sp.wait_ge(consts, 5)
                for q in queues:
                    sp.dma_start(q.rearrange("(p a) f -> p a f", p=P), bcast(blank[:, :], 1, E * CAP // P))\
                      .then_inc(filled, 16)
                for m in answers_of:
                    sp.dma_start(m.rearrange("(p a) f -> p a f", p=P), bcast(blank[:, 0:D], 1, 2 * N // P))\
                      .then_inc(filled, 16)

            @block.scalar
            def _(act):
                act.dma_start(prodV[0][:, 0:2, :], qkv_w.rearrange("(a p) f -> p a f", p=P)).then_inc(loads, 16)
                act.dma_start(proj_in, proj_w).then_inc(loads, 16)
                act.dma_start(Wr[:, :], router_w).then_inc(loads, 16)
                for W, w in ((Wqa, wq), (Wka, wk), (Wva, wv)):
                    act.dma_start(W[:, :].rearrange("f (h e) -> f h e", e=HD),
                                  w.rearrange("h f e -> f h e")).then_inc(loads, 16)
                act.dma_start(Woa[:, :], wo).then_inc(loads, 16)

            @block.gpsimd
            def _(pool):
                pool.memset(prodQ[0][:, 0:HEADS // 2, :], 0.0).then_inc(consts, 1)
                pool.memset(blank[:, 0:D], 0.0)
                pool.memset(blank[:, D:ROW], 16.0 * N)
                pool.memset(Z2[:, :, D:ROW], 0.0)
                pool.memset(ident[:, :], 0.0)
                pool.memset(before[:, :], 1.0)
                pool.memset(select[:, 0:HEADS], 1.0)
                pool.memset(select[:, HEADS:], 0.0)
                pool.memset(identb[:, :], 0.0)
                pool.memset(causal[:, :], 0.0)
                pool.memset(eps[:, :], EPS)
                pool.iota(expert_base[:, :], [[CAP, E]], base=0, channel_multiplier=0,
                          allow_small_or_imprecise_dtypes=True)
                pool.iota(rank_of[:, :], [[-1, E]], base=E, channel_multiplier=0,
                          allow_small_or_imprecise_dtypes=True).then_inc(consts, 1)
                pool.wait_ge(consts, 2)
                for m in (ident, identb):
                    pool.affine_select(out=m[:, :], in_=m[:, :], compare_op=ALU.not_equal, fill=1.0,
                                       base=0, pattern=[[-1, P]], channel_multiplier=1)
                pool.affine_select(out=before[:, :], in_=before[:, :], compare_op=ALU.is_ge, fill=0.0,
                                   base=-1, pattern=[[1, P]], channel_multiplier=-1)
                cv = causal[:, :].rearrange("p (a t) -> p a t", a=2)
                pool.affine_select(out=cv, in_=cv, compare_op=ALU.is_ge, fill=NEG,
                                   base=0, pattern=[[0, 2], [-1, P]], channel_multiplier=1)
                sel = select[:, 0:HEADS]
                pool.affine_select(out=sel, in_=sel, compare_op=ALU.is_ge, fill=0.0,
                                   base=0, pattern=[[-HD, HEADS]], channel_multiplier=1).then_inc(consts, 1)
                pool.wait_ge(consts, 3)
                pool.affine_select(out=sel, in_=sel, compare_op=ALU.is_ge, fill=0.0,
                                   base=HD - 1, pattern=[[HD, HEADS]], channel_multiplier=-1).then_inc(consts, 1)
                pool.wait_ge(consts, 4)
                pool.iota(Z2[:, :, TOKEN], [[P, NT]], base=0, channel_multiplier=1,
                          allow_small_or_imprecise_dtypes=True)
                pool.tensor_copy(beforeb[:, :], before[:, :])
                pool.memset(onesb[:, :], 1.0).then_inc(consts, 1)
                pool.wait_ge(consts, 5)

            @block.tensor
            def _(pe):
                pe.wait_ge(loads, 16 * 14)
                pe.wait_ge(consts, 4)
                for i in range(2):
                    pe.transpose(banks[0][:, i * P:(i + 1) * P], qkv_in[i], ident[:, :])
                pe.transpose(banks[0][:, 2 * P:3 * P], proj_in, ident[:, :]).then_inc(wt_ps, 1)

            @block.vector
            def _(dve):
                for i in range(4):
                    dve.wait_ge(x_in[i], 16)
                    for j in range(8 * i, 8 * i + 8):
                        ins = dve.bn_stats(stats[:, j, :], X[:, j, :])
                ins.then_inc(x_stats, 1)
                dve.wait_ge(x_stats, 1)
                input_norm(dve, ln_own)
                dve.wait_ge(wt_ps, 1)
                src = banks[0][:, 0:2 * P].rearrange("f (g c) -> f g c", c=4 * HD)
                dve.tensor_copy(WqT[:, :].rearrange("f (g c) -> f g c", c=2 * HD), src[:, :, 0:2 * HD])
                for r in range(2):
                    for W, c in ((WkT, 2), (WvT, 3)):
                        dve.tensor_copy(W[:, :].rearrange("f (g r d) -> f g r d", r=2, d=HD)[:, :, r, :],
                                        src[:, :, c * HD:(c + 1) * HD])
                dve.tensor_copy(WpT[:, :], banks[0][:, 2 * P:3 * P]).then_inc(wt_done, 1)
                dve.wait_ge(wt_done, 1)

        sc = [sb(f"sc{i}", [P, HALVES, S, HEADS]) for i in range(4)]
        reduced = [sb(f"reduced{i}", [P, 512]) for i in range(2)]
        attnT = [sb(f"attnT{i}", [P, B]) for i in range(2)]
        mx = sb("mx", [P, HALVES, HEADS])
        den = sb("den", [P, HALVES, HEADS])
        logits = sb("logits", [P, NT, E])
        picks = [sb(f"pick{i}", [P, NT, E]) for i in range(2)]
        ranks = sb("ranks", [P, NT, E])
        tops = [sb(f"top{i}", [P, NT]) for i in range(2)]
        second = sb("second", [P, NT])
        gaps = sb("gaps", [P, NT])
        place = [sb(f"place{i}", [P, NT]) for i in range(2)]
        work = [sb(f"work{i}", [P, NT, E]) for i in range(2)]
        gates = [sb(f"gates{i}", [P, 2]) for i in range(NCH)]
        put_at = [sb(f"put_at{i}", [P, NT], U32) for i in range(2)]
        picked = sb("picked", [P, NT, E], BF16)
        picked_before = sb("picked_before", [P, E], BF16)
        answer_at = [sb(f"answer_at{i}", [P, 2], U32) for i in range(NCH)]
        is_first, is_second, denom, numer = ([sb(f"{n}{i}", [P, 2]) for i in range(2)]
                                             for n in ("is_first", "is_second", "denom", "numer"))
        w1s = [prodQ[0][:, 2 * i:2 * i + 2, :].rearrange("p a b -> p (a b)") for i in range(2)]
        w2s = [prodQ[0][:, 4 + 2 * i:6 + 2 * i, :].rearrange("p a (c f) -> p (a c) f", f=D) for i in range(2)]
        hidden = [prodQ[1][:, 4 * i:4 * i + 4, :] for i in range(2)]
        xe = [prodQ[1][:, 8 + 2 * i:10 + 2 * i, :].rearrange("p a b -> p (a b)")[:, 0:2 * ROW]
              .rearrange("p (a f) -> p a f", a=2) for i in range(2)]
        xeT = [prodQ[1][:, 12 + i, :] for i in range(2)]
        ye = [prodQ[1][:, 14 + i, :] for i in range(2)]

        def ffn_half(half, last):
            L = f"f{half}"

            def sm(name):
                return sem(f"{L}_{name}")

            queue, answers = queues[half], answers_of[half]

            G = NT // 4
            z_ready, zT_ps, zT_ready, qk_ps, q_copied, k_copied, v_ps, v_copied = credited = [
                sm(n) for n in ("z_ready", "zT_ps", "zT_ready", "qk_ps", "q_copied", "k_copied", "v_ps", "v_copied")]
            ln_own, coef = sm("ln_own"), sm("coef")
            shift = tiny[1]
            pz = [banks[0], banks[1]]
            pqk, pv = st_ps, [banks[2], banks[3]]
            with nc.Block() as block:
                @block.sync
                def _(sp):
                    for c in credited:
                        sp.sem_inc(c, CREDIT)

                @block.vector
                def _(dve):
                    def normalise(n, u):
                        dve.wait_ge(zT_ps, done(n - 2))
                        for k in range(4):
                            j = n * 4 + k
                            ins = dve.tensor_scalar(stageZ[u][:, k, :], X[:, bass.ds(j, 1), :],
                                                    mean[:, bass.ds(j, 1)], r01[:, bass.ds(j, 1)],
                                                    ALU.subtract, ALU.mult)
                        ins.then_inc(z_ready, 1)

                    def keep_k(n, u):
                        dve.wait_ge(qk_ps, done(n))
                        dve.tensor_copy(kT[:, bass.ds(n * 2, 2), :],
                                        pqk[u][:, 1, :].rearrange("p (s b) -> p s b", s=2)).then_inc(k_copied, 1)

                    if half:
                        input_norm(dve, ln_own)
                    dve.scalar_tensor_tensor(shift[:, :], mean[:, :], -1.0, r0[:, :], ALU.mult, ALU.mult)\
                       .then_inc(coef, 1)
                    ahead_of(dve, G, normalise, keep_k, by=2)

                @block.tensor
                def _(pe):
                    def turn(n, u):
                        pe.wait_ge(z_ready, done(n))
                        pe.wait_ge(zT_ready, done(n - 2))
                        for k in range(4):
                            ins = pe.transpose(pz[u][:, k * P:(k + 1) * P], stageZ[u][:, k, :], ident[:, :])
                        ins.then_inc(zT_ps, 1)

                    def project(n, u):
                        pe.wait_ge(zT_ready, done(n))
                        pe.wait_ge(q_copied, done(n - 2))
                        pe.wait_ge(k_copied, done(n - 2))
                        pe.matmul(pqk[u][:, 0, :], WqT[:, :], stageT[u][:, :], start=True, stop=True)
                        pe.matmul(pqk[u][:, 1, :], WkT[:, :], stageT[u][:, :], start=True, stop=True).then_inc(qk_ps, 1)
                        pe.wait_ge(v_copied, done(n - 2))
                        for k in range(4):
                            ins = pe.matmul(pv[u][:, k * P:(k + 1) * P], stageT[u][:, k * P:(k + 1) * P],
                                            WvT[:, :], start=True, stop=True)
                        ins.then_inc(v_ps, 1)

                    ahead_of(pe, G, turn, project)

                @block.scalar
                def _(act):
                    def scale(n, u):
                        act.wait_ge(zT_ps, done(n))
                        act.wait_ge(v_ps, done(n - 2))
                        act.activation(stageT[u][:, :], pz[u][:, :], ACT.Identity, bias=lnp[:, 1:2],
                                       scale=lnp[:, 0:1]).then_inc(zT_ready, 1)

                    def keep_qv(n, u):
                        for k in range(4):
                            j = n * 4 + k
                            act.activation(H2[:, bass.ds(j, 1), :], X[:, bass.ds(j, 1), :], ACT.Identity,
                                           bias=shift[:, bass.ds(j, 1)], scale=r0[:, bass.ds(j, 1)])
                        act.wait_ge(qk_ps, done(n))
                        act.activation(qT[:, bass.ds(n * 2, 2), :],
                                       pqk[u][:, 0, :].rearrange("p (s b) -> p s b", s=2), ACT.Copy)\
                           .then_inc(q_copied, 1)
                        act.wait_ge(v_ps, done(n))
                        act.activation(V[:, bass.ds(n * 4, 4), :],
                                       pv[u][:, :].rearrange("p (k f) -> p k f", k=4), ACT.Copy)\
                           .then_inc(v_copied, 1)

                    act.wait_ge(coef, 1)
                    ahead_of(act, G, scale, keep_qv)

            groups = [(s, g) for s in range(S) for g in range(s // 8 + 1)]
            first = {s: groups.index((s, 0)) for s in range(S)}
            n_groups = {s: s // 8 + 1 for s in range(S)}

            def units(s, g):
                return min(4, s // 2 + 1 - 4 * g)

            prod_ready, red_ps, red_sb, tr_ps, sc_ready, centred, exped = (
                sm(n) for n in ("prod_ready", "red_ps", "red_sb", "tr_ps", "sc_ready", "centred", "exped"))
            probs_ready, pv_ready, pv_used, o_sb, y_ps, added, own = (
                sm(n) for n in ("probs_ready", "pv_ready", "pv_used", "o_sb", "y_ps", "added", "own"))
            pO, pY = st_ps[0][:, 0, :], st_ps[0][:, 1, :]

            BATCH = [(0, 12), (12, 20), (20, 28), (28, 32)]
            BATCHES = len(BATCH)
            ln2_own, queue_own, choice_own, placed = sm("ln2_own"), sm("queue_own"), sm("choice_own"), sm("placed")
            z2_ready, z2T_ps, z2T_ready, lg_ps, lg_copied, picked_ready, ranks_ps, ranks_copied, \
                counted_before, scattered, gap, gap_exp = (sm(n) for n in (
                    "z2_ready", "z2T_ps", "z2T_ready", "lg_ps", "lg_copied", "picked_ready", "ranks_ps",
                    "ranks_copied", "counted_before", "scattered", "gap", "gap_exp"))
            pz2, plog = st_ps[1][:, 0, :], st_ps[1][:, 1, :]
            NORM = ROUTE = (11, 15, 19, 21)
            RANK = (13, 17, 20, 22)
            CHOOSE = (12, 16, 20, 22)
            PLACE = (20, 22)
            LAGS = RANK[-1] + 1
            assert all(n == b // HALVES - 1 + 6 for n, (_, b) in zip(NORM, BATCH))

            def due(steps, i, do):
                if i in steps:
                    do(steps.index(i))

            POOLED = 2

            def over_experts(chain, out_, values):
                engine = chain.engine
                if engine is nc.vector:
                    chain(engine.tensor_reduce(out_, values, AX.X, ALU.add))
                    return
                n = E // 2
                while n > 1:
                    chain(engine.tensor_tensor(values[:, :, 0:n], values[:, :, 0:n], values[:, :, n:2 * n], ALU.add))
                    n //= 2
                chain(engine.tensor_tensor(out_, values[:, :, 0], values[:, :, 1], ALU.add))

            def choose(chain, m):
                dve, (a, b) = chain.engine, BATCH[m]
                dve.wait_ge(lg_copied, m + 1)
                lg, marked = logits[:, a:b, :], work[0][:, a:b, :]
                for k in range(2):
                    top, r = tops[k][:, a:b], Z2[:, a:b, FIRST] if k == 0 else second[:, a:b]
                    chain(dve.tensor_reduce(top, lg, AX.X, ALU.max))
                    chain(dve.tensor_tensor(marked, lg, bcast(top, 2, E), ALU.is_equal))
                    chain(dve.tensor_tensor(marked, marked, bcast(rank_of[:, :], 1, b - a), ALU.mult))
                    chain(dve.tensor_reduce(r, marked, AX.X, ALU.max))
                    chain(dve.tensor_tensor(picks[k][:, a:b, :], marked, bcast(r, 2, E), ALU.is_equal))
                    if k == 0:
                        chain(dve.scalar_tensor_tensor(lg, picks[0][:, a:b, :], NEG, lg, ALU.mult, ALU.add))
                dve.tensor_tensor(picked[:, a:b, :], picks[0][:, a:b, :], picks[1][:, a:b, :], ALU.add)\
                   .then_inc(picked_ready, 1)
                dve.tensor_tensor(gaps[:, a:b], tops[1][:, a:b], tops[0][:, a:b], ALU.subtract).then_inc(gap, 1)
                dve.wait_ge(picked_ready, m + 1)
                dve.wait_ge(gap, m + 1)

            def find_places(chain, m):
                engine, (a, b) = chain.engine, BATCH[m]
                places, spare, rk = work[0][:, a:b, :], work[1][:, a:b, :], ranks[:, a:b, :]
                engine.wait_ge(counted_before, m + 1)
                engine.wait_ge(ranks_copied, m + 1)
                chain(engine.tensor_scalar(spare, rk, float(CAP), 4.0 * E * CAP, ALU.is_ge, ALU.mult))
                chain(engine.tensor_tensor(places, rk, spare, ALU.add))
                chain(engine.tensor_tensor(places, places, bcast(expert_base[:, :], 1, b - a), ALU.add))
                for k in range(2):
                    chain(engine.tensor_tensor(spare, picks[k][:, a:b, :], places, ALU.mult))
                    over_experts(chain, place[k][:, a:b], spare)
                    chain(engine.tensor_copy(put_at[k][:, a:b], place[k][:, a:b]))
                engine.sem_inc(placed, 1)
                if m + 1 < BATCHES:
                    n = (b - a) // 2
                    chain(engine.tensor_tensor(spare[:, 0:n, :], picked[:, a:a + n, :], picked[:, a + n:b, :], ALU.add))
                    while n > 1:
                        folded = n // 2
                        chain(engine.tensor_tensor(spare[:, 0:folded, :], spare[:, 0:folded, :], spare[:, n - folded:n, :],
                                                   ALU.add))
                        n -= folded
                    engine.tensor_tensor(picked_before[:, :], picked_before[:, :], spare[:, 0, :], ALU.add)\
                        .then_inc(counted_before, 1)
                    engine.wait_ge(counted_before, m + 2)

            with nc.Block() as block:
                @block.vector
                def _(dve):
                    chain = Chain(dve, own)

                    def qk_product(s):
                        n = 2 * (s // 2 + 1)
                        if s >= 2:
                            dve.wait_ge(red_ps, first[s - 2] + n_groups[s - 2])
                        dve.tensor_tensor(prodQ[s % 2][:, 0:n, :], bcast(qT[:, s, :], 1, n), kT[:, 0:n, :],
                                          ALU.mult).then_inc(prod_ready, 1)

                    def centre(s):
                        n = s + 1
                        dve.wait_ge(sc_ready, first[s] + n_groups[s])
                        chain(dve.tensor_reduce(mx[:, :, :], sc[s % 4][:, :, 0:n, :].rearrange("p a t h -> p a h t"),
                                                AX.X, ALU.max))
                        dve.tensor_tensor(sc[s % 4][:, :, 0:n, :], sc[s % 4][:, :, 0:n, :], bcast(mx[:, :, :], 2, n),
                                          ALU.subtract).then_inc(centred, 1)

                    def normalise(s):
                        n = s + 1
                        dve.wait_ge(exped, s + 1)
                        chain(dve.tensor_reduce(den[:, :, :], sc[s % 4][:, :, 0:n, :].rearrange("p a t h -> p a h t"),
                                                AX.X, ALU.add))
                        chain(dve.reciprocal(den[:, :, :], den[:, :, :]))
                        dve.tensor_tensor(sc[s % 4][:, :, 0:n, :], sc[s % 4][:, :, 0:n, :], bcast(den[:, :, :], 2, n),
                                          ALU.mult).then_inc(probs_ready, 1)

                    def pv_product(s, a):
                        n = s + 1
                        dve.wait_ge(probs_ready, s + 1)
                        if s:
                            dve.wait_ge(pv_used, 2 * s + a - 1)
                        dve.tensor_tensor(prodV[a][:, 0:n, :].rearrange("p t (h d) -> p t h d", d=HD),
                                          bcast(sc[s % 4][:, a, 0:n, :], 3, HD),
                                          V[:, a:a + 2 * s + 1:2, :].rearrange("p t (h d) -> p t h d", d=HD),
                                          ALU.mult).then_inc(pv_ready, 1)

                    ln2_chain, queue_chain = Chain(dve, ln2_own), Chain(dve, choice_own)

                    def statistics(m):
                        a, b = BATCH[m]
                        dve.wait_ge(added, b // HALVES)
                        for j in range(a, b):
                            ins = dve.bn_stats(stats[:, j, :], H2[:, j, :])
                        ln2_chain(ins)

                    def factors(m):
                        norm_factors(ln2_chain, *BATCH[m], False)

                    def normalised(m):
                        for j in range(*BATCH[m]):
                            ins = dve.tensor_scalar(Z2[:, j, 0:D], H2[:, j, :], mean[:, j:j + 1], r0[:, j:j + 1],
                                                    ALU.subtract, ALU.mult)
                            if j % 4 == 3:
                                ins.then_inc(z2_ready, 1)

                    for i in range(LAGS):
                        if i < S:
                            qk_product(i)
                        due(NORM, i, statistics)
                        if 0 <= i - 3 < S:
                            pv_product(i - 3, 0)
                        due(NORM, i, factors)
                        if 0 <= i - 1 < S:
                            centre(i - 1)
                        if 0 <= i - 3 < S:
                            pv_product(i - 3, 1)
                        due(NORM, i, normalised)
                        if 0 <= i - 2 < S:
                            normalise(i - 2)
                        due(CHOOSE, i, lambda k: choose(queue_chain, k))
                        due(PLACE, i, lambda k: find_places(queue_chain, POOLED + k))

                @block.tensor
                def _(pe):
                    def reduce_heads(s):
                        pe.wait_ge(prod_ready, s + 1)
                        for g in range(n_groups[s]):
                            n = first[s] + g
                            if n >= 2:
                                pe.wait_ge(red_sb, n - 1)
                            for j in range(units(s, g)):
                                u = 4 * g + j
                                ins = pe.matmul(banks[n % 2][32 * j:32 * j + 32, :], select[:, :],
                                                prodQ[s % 2][:, 2 * u:2 * u + 2, :].rearrange("p t b -> p (t b)"),
                                                start=True, stop=True)
                            ins.then_inc(red_ps, 1)

                    def to_columns(s):
                        for g in range(n_groups[s]):
                            n = first[s] + g
                            m = 32 * units(s, g)
                            pe.wait_ge(red_sb, n + 1)
                            if n >= 2:
                                pe.wait_ge(sc_ready, n - 1)
                            for c in range(4):
                                ins = pe.transpose(banks[2 + n % 2][:, c * P:c * P + m],
                                                   reduced[n % 2][0:m, c * P:(c + 1) * P], ident[0:m, 0:m])
                            ins.then_inc(tr_ps, 1)

                    def sum_pv(s, a):
                        pe.wait_ge(pv_ready, 2 * s + a + 1)
                        if a == 0 and s:
                            pe.wait_ge(o_sb, s)
                        for t in range(s + 1):
                            ins = pe.matmul(pO[:, a * P:(a + 1) * P], prodV[a][:, t, :], ident[:, :],
                                            start=(t == 0), stop=(t == s))
                        ins.then_inc(pv_used, 1)

                    def project(s):
                        pe.wait_ge(o_sb, s + 1)
                        if s:
                            pe.wait_ge(added, s)
                        for a in range(HALVES):
                            pe.matmul(pY[:, a * P:(a + 1) * P], attnT[s % 2][:, a * P:(a + 1) * P],
                                      WpT[:, :], start=True, stop=False)
                            ins = pe.matmul(pY[:, a * P:(a + 1) * P], ident[:, :], H2[:, HALVES * s + a, :],
                                            start=False, stop=True)
                        ins.then_inc(y_ps, 1)

                    def route(m):
                        for g in range(BATCH[m][0] // 4, BATCH[m][1] // 4):
                            pe.wait_ge(z2_ready, g + 1)
                            if g:
                                pe.wait_ge(z2T_ready, g)
                            for k in range(4):
                                ins = pe.transpose(pz2[:, k * P:(k + 1) * P], Z2[:, 4 * g + k, 0:D], ident[:, :])
                            ins.then_inc(z2T_ps, 1)
                            pe.wait_ge(z2T_ready, g + 1)
                            at = 4 * g - BATCH[m][0]
                            if at == 0 and m:
                                pe.wait_ge(lg_copied, m)
                                pe.wait_ge(ranks_copied, m)
                            for k in range(4):
                                ins = pe.matmul(plog[:, (at + k) * E:(at + k + 1) * E],
                                                stageT[g % 2][:, k * P:(k + 1) * P],
                                                Wr[:, :], start=True, stop=True)
                            ins.then_inc(lg_ps, 1)

                    def rank(m):
                        pe.wait_ge(picked_ready, m + 1)
                        pe.wait_ge(counted_before, m + 1)
                        a, b = BATCH[m]
                        mine = picked[:, a:b, :].rearrange("p n e -> p (n e)")
                        out_ = plog[:, P:P + (b - a) * E]
                        pe.matmul(out_, beforeb[:, :], mine, start=True, stop=False, skip_group_check=True)
                        for d in range(1, b - a):
                            pe.matmul(out_[:, d * E:], onesb[:, :], mine[:, 0:(b - a - d) * E], start=False, stop=False,
                                      skip_group_check=True)
                        pe.matmul(out_, onesb[:, :], bcast(picked_before[:, :], 1, b - a), start=False, stop=True,
                                  skip_group_check=True).then_inc(ranks_ps, 1)

                    for i in range(LAGS):
                        if i < S:
                            reduce_heads(i)
                        if 0 <= i - 3 < S:
                            sum_pv(i - 3, 0)
                        if i < S:
                            to_columns(i)
                        due(RANK, i, rank)
                        if 0 <= i - 3 < S:
                            sum_pv(i - 3, 1)
                        due(ROUTE, i, route)
                        if 0 <= i - 4 < S:
                            project(i - 4)

                @block.gpsimd
                def _(pool):
                    chain = Chain(pool, queue_own)

                    pool.memset(picked_before[:, :], 0.0).then_inc(counted_before, 1)
                    pool.wait_ge(counted_before, 1)
                    for m in range(BATCHES):
                        if m < POOLED:
                            find_places(chain, m)
                        else:
                            pool.wait_ge(placed, m + 1)
                        pool.wait_ge(gap_exp, m + 1)
                        if m == 0:
                            pool.wait_ge(filled, 16 * 4)
                        for k in range(2):
                            for j in range(*BATCH[m]):
                                pool.indirect_dma_start(
                                    queue, bass.IndirectOffsetOnAxis(ap=put_at[k][:, j:j + 1], axis=0),
                                    Z2[:, j, :], None, bounds_check=E * CAP - 1, oob_is_err=False)\
                                    .then_inc(scattered, 16)
                    pool.wait_ge(scattered, 16 * 2 * NT)

                @block.scalar
                def _(act):
                    def scale_z2(m):
                        for g in range(BATCH[m][0] // 4, BATCH[m][1] // 4):
                            act.wait_ge(z2T_ps, g + 1)
                            if g >= 2:
                                act.wait_ge(lg_ps, g - 1)
                            act.activation(stageT[g % 2][:, :], pz2, ACT.Identity, bias=lnp[:, 3:4],
                                           scale=lnp[:, 2:3]).then_inc(z2T_ready, 1)

                    def keep_logits(m):
                        a, b = BATCH[m]
                        act.wait_ge(lg_ps, b // 4)
                        act.activation(logits[:, a:b, :], plog[:, 0:(b - a) * E].rearrange("p (k e) -> p k e", e=E),
                                       ACT.Copy).then_inc(lg_copied, 1)

                    def exp_gap(m):
                        a, b = BATCH[m]
                        act.wait_ge(gap, m + 1)
                        act.activation(Z2[:, a:b, RATIO], gaps[:, a:b], ACT.Exp).then_inc(gap_exp, 1)

                    def keep_ranks(m):
                        a, b = BATCH[m]
                        act.wait_ge(ranks_ps, m + 1)
                        act.activation(ranks[:, a:b, :], plog[:, P:P + (b - a) * E]
                                       .rearrange("p (n e) -> p n e", e=E), ACT.Copy).then_inc(ranks_copied, 1)

                    for i in range(LAGS):
                        if i < S:
                            for g in range(n_groups[i]):
                                n, m = first[i] + g, 32 * units(i, g)
                                act.wait_ge(red_ps, n + 1)
                                if n >= 2:
                                    act.wait_ge(tr_ps, n - 1)
                                act.activation(reduced[n % 2][0:m, :], banks[n % 2][0:m, :], ACT.Copy)\
                                   .then_inc(red_sb, 1)
                        if 0 <= i - 5 < S:
                            s = i - 5
                            act.wait_ge(y_ps, s + 1)
                            act.activation(H2[:, 2 * s:2 * s + 2, :], pY[:, 0:B]
                                           .rearrange("p (a f) -> p a f", a=HALVES), ACT.Copy).then_inc(added, 1)
                        if 0 <= i - 1 < S:
                            s = i - 1
                            act.wait_ge(centred, s + 1)
                            e = sc[s % 4][:, :, 0:s + 1, :]
                            act.activation(e, e, ACT.Exp, scale=SCALE).then_inc(exped, 1)
                        if i < S:
                            for g in range(n_groups[i]):
                                n, m = first[i] + g, units(i, g)
                                act.wait_ge(tr_ps, n + 1)
                                if i >= 4:
                                    act.wait_ge(pv_ready, 2 * (i - 3))
                                for par in range(2):
                                    src = banks[2 + n % 2][:, 2 * par * P:2 * (par + 1) * P]
                                    src = src.rearrange("p (a j h) -> p a j h", a=HALVES, h=32)[:, :, 0:m, 0:HEADS]
                                    t0 = 8 * g + par
                                    ins = act.activation(sc[i % 4][:, :, t0:t0 + 2 * m - 1:2, :], src, ACT.Copy)
                                ins.then_inc(sc_ready, 1)
                        due(ROUTE, i, scale_z2)
                        if 0 <= i - 3 < S:
                            s = i - 3
                            act.wait_ge(pv_used, 2 * s + 2)
                            if s >= 2:
                                act.wait_ge(y_ps, s - 1)
                            act.activation(attnT[s % 2][:, :], pO[:, 0:B], ACT.Copy).then_inc(o_sb, 1)
                        due(RANK, i, exp_gap)
                        due(RANK, i, keep_ranks)
                        due(ROUTE, i, keep_logits)

            NPAIR, NC2 = E // 2, 2 * NCH
            w_in = [sm(f"w_in{u}") for u in range(2)]
            xe_in = [sm(f"xe_in{u}") for u in range(2)]
            ye_out = [sm(f"ye_out{u}") for u in range(2)]
            counted, gate_own = sm("counted"), sm("gate_own")
            xeT_ps, xeT_ready, h_ps, h_ready, y2_ps, y2_copied, ye_free, at_ready = credited = [sm(n) for n in (
                "xeT_ps", "xeT_ready", "h_ps", "h_ready", "y2_ps", "y2_copied", "ye_free", "at_ready")]
            px, py = [banks[0], banks[1]], [banks[2], banks[3]]
            with nc.Block() as block:
                @block.sync
                def _(sp):
                    for c in credited:
                        sp.sem_inc(c, CREDIT)
                    with sp.Fori(0, NPAIR) as i:
                        for u in range(2):
                            sp.wait_ge(y2_ps, done(i * NC2 + (u * NCH - NCH - 1)))
                            sp.dma_start(w1s[u], moe_w1[bass.ds(i * 2 + u, 1), :, :].rearrange("e p f -> p (e f)"))\
                              .then_inc(w_in[u], 16)
                            sp.dma_start(w2s[u], moe_w2[bass.ds(i * 2 + u, 1), :, :]
                                         .rearrange("e (c p) f -> p (e c) f", p=P)).then_inc(w_in[u], 16)
                            for c in range(NCH):
                                n = i * NC2 + (u * NCH + c)
                                q = u * NCH + c
                                sp.wait_ge(xeT_ps, done(n - 2))
                                sp.wait_ge(at_ready, done(n - 2))
                                sp.dma_start(xe[q % 2], queue[bass.ds(n * CH, CH), :]
                                             .rearrange("(a p) f -> p a f", p=P)).then_inc(xe_in[q % 2], 16)

                @block.tensor
                def _(pe):
                    def turn(i, q):
                        i, q = i + q // NC2, q % NC2
                        n, b = i * NC2 + q, q % 2
                        pe.wait_ge(xe_in[b], i * (16 * NCH) + 16 * (q // 2 + 1))
                        pe.wait_ge(xeT_ready, done(n - 2))
                        for a in range(2):
                            ins = pe.transpose(px[b][:, a * P:(a + 1) * P], xe[b][:, a, 0:D], ident[:, :])
                        ins.then_inc(xeT_ps, 1)

                    def up(i, q):
                        i, q = i + q // NC2, q % NC2
                        n, b, u = i * NC2 + q, q % 2, q // NCH
                        pe.wait_ge(xeT_ready, done(n))
                        pe.wait_ge(h_ready, done(n - 2))
                        if q % NCH == 0:
                            pe.wait_ge(w_in[u], i * 32 + 32)
                        for f in range(FC):
                            ins = pe.matmul(st_ps[b][:, :, :].rearrange("p a c -> p (a c)")[:, f * CH:(f + 1) * CH],
                                            w1s[u][:, f * P:(f + 1) * P], xeT[b], start=True, stop=True)
                        ins.then_inc(h_ps, 1)

                    def down(i, q):
                        n, b, u = i * NC2 + q, q % 2, q // NCH
                        pe.wait_ge(h_ready, done(n))
                        pe.wait_ge(y2_copied, done(n - 2))
                        for a in range(2):
                            for f in range(FC):
                                ins = pe.matmul(py[b][:, a * P:(a + 1) * P],
                                                hidden[b][:, f, a * P:(a + 1) * P],
                                                w2s[u][:, f, :], start=(f == 0), stop=(f == FC - 1))
                        ins.then_inc(y2_ps, 1)

                    turn(0, 0)
                    up(0, 0)
                    turn(0, 1)
                    with pe.Fori(0, NPAIR - 1) as i:
                        for q in range(NC2):
                            up(i, q + 1)
                            turn(i, q + 2)
                            down(i, q)
                    for q in range(NC2):
                        if q + 1 < NC2:
                            up(NPAIR - 1, q + 1)
                        if q + 2 < NC2:
                            turn(NPAIR - 1, q + 2)
                        down(NPAIR - 1, q)

                @block.scalar
                def _(act):
                    with act.Fori(0, NPAIR) as i:
                        for q in range(NC2):
                            n = i * NC2 + q
                            act.wait_ge(h_ps, done(n))
                            act.wait_ge(y2_ps, done(n - 2))
                            act.activation(hidden[q % 2].rearrange("p a b -> p (a b)"),
                                           st_ps[q % 2][:, :, :].rearrange("p a c -> p (a c)"),
                                           ACT.Gelu).then_inc(h_ready, 1)

                @block.vector
                def _(dve):
                    def scale(i, q):
                        n, b = i * NC2 + q, q % 2
                        dve.wait_ge(xeT_ps, done(n))
                        dve.wait_ge(h_ps, done(n - 2))
                        dve.tensor_scalar(xeT[b], px[b][:, 0:CH], lnp[:, 2:3], lnp[:, 3:4],
                                          ALU.mult, ALU.add).then_inc(xeT_ready, 1)
                        i, q = i + q // NC2, q % NC2
                        own, expert = n * 6, rank_of[:, bass.ds(i * 2 + q // NCH, 1)]
                        dve.wait_ge(ye_free, done(n - NCH))
                        dve.tensor_scalar(is_second[b][:, :], xe[b][:, :, FIRST], expert, None, ALU.not_equal)\
                           .then_inc(gate_own, 1)
                        dve.tensor_scalar(is_first[b][:, :], xe[b][:, :, FIRST], expert, None, ALU.is_equal)\
                           .then_inc(gate_own, 1)
                        dve.tensor_scalar(denom[b][:, :], xe[b][:, :, RATIO], 1.0, None, ALU.add)\
                           .then_inc(gate_own, 1)
                        dve.wait_ge(gate_own, own + 3)
                        dve.scalar_tensor_tensor(answer_at[q % NCH][:, :], is_second[b][:, :], float(N),
                                                 xe[b][:, :, TOKEN], ALU.mult, ALU.add)
                        dve.tensor_tensor(numer[b][:, :], is_second[b][:, :], xe[b][:, :, RATIO], ALU.mult)\
                           .then_inc(gate_own, 1)
                        dve.reciprocal(denom[b][:, :], denom[b][:, :]).then_inc(gate_own, 1)
                        dve.wait_ge(gate_own, own + 5)
                        dve.tensor_tensor(numer[b][:, :], numer[b][:, :], is_first[b][:, :], ALU.add)\
                           .then_inc(gate_own, 1)
                        dve.wait_ge(gate_own, own + 6)
                        dve.scalar_tensor_tensor(gates[q % NCH][:, :], numer[b][:, :], 0.5, denom[b][:, :],
                                                 ALU.mult, ALU.mult).then_inc(at_ready, 1)
                        dve.wait_ge(at_ready, done(n))

                    def keep(i, q):
                        n, b = i * NC2 + q, q % 2
                        dve.wait_ge(y2_ps, done(n))
                        dve.wait_ge(ye_free, done(n - 2))
                        for a in range(2):
                            ins = dve.tensor_scalar(ye[b][:, a * D:(a + 1) * D], py[b][:, a * P:(a + 1) * P],
                                                    gates[q % NCH][:, a:a + 1], None, ALU.mult)
                        ins.then_inc(y2_copied, 1)

                    dve.scalar_tensor_tensor(X[:, :, :], H2[:, :, :], 0.5, X[:, :, :], ALU.mult, ALU.add)
                    scale(0, 0)
                    scale(0, 1)
                    with dve.Fori(0, NPAIR - 1) as i:
                        for q in range(NC2):
                            scale(i, q + 2)
                            keep(i, q)
                    for q in range(NC2):
                        if q + 2 < NC2:
                            scale(NPAIR - 1, q + 2)
                        keep(NPAIR - 1, q)

                @block.gpsimd
                def _(pool):
                    with pool.Fori(0, NPAIR) as i:
                        for q in range(NC2):
                            n = i * NC2 + q
                            pool.wait_ge(y2_copied, done(n))
                            pool.sem_inc(counted, 1)
                            for a in range(2):
                                pool.indirect_dma_start(
                                    answers, bass.IndirectOffsetOnAxis(ap=answer_at[q % NCH][:, a:a + 1], axis=0),
                                    ye[q % 2][:, a * D:(a + 1) * D], None, bounds_check=2 * N - 1, oob_is_err=False)\
                                    .then_inc(ye_out[q % 2], 16)
                            if q:
                                pool.wait_ge(ye_out[(q - 1) % 2], i * (32 * NCH) + 32 * ((q - 1) // 2 + 1))
                                pool.sem_inc(ye_free, 1)
                        pool.wait_ge(ye_out[(NC2 - 1) % 2], i * (32 * NCH) + 32 * NCH)
                        pool.sem_inc(ye_free, 1)

            PIECE = 4
            got = [sm(f"got{k}") for k in range(NT // PIECE)]
            mixed, own2, stored, cleared = sm("mixed"), sm("own2"), sm("stored"), sm("cleared")
            rows = [V, kT[:, :, :].rearrange("p s (a f) -> p (s a) f", f=D)]
            by_choice = answers.rearrange("(k n p) f -> k p n f", k=2, p=P)
            with nc.Block() as block:
                @block.vector
                def _(dve):
                    chain = Chain(dve, own2)
                    if not last:
                        dve.memset(stack_space[2], 0.0).then_inc(cleared, 1)
                    for g in range(NT // PIECE):
                        a, b = g * PIECE, (g + 1) * PIECE
                        dve.wait_ge(got[g], 32)
                        chain(dve.tensor_tensor(X[:, a:b, :], X[:, a:b, :], rows[0][:, a:b, :], ALU.add))
                        dve.tensor_tensor(X[:, a:b, :], X[:, a:b, :], rows[1][:, a:b, :], ALU.add).then_inc(mixed, 1)
                        if not last:
                            dve.wait_ge(mixed, g + 1)
                            for j in range(a, b):
                                ins = dve.bn_stats(stats[:, j, :], X[:, j, :])
                    dve.wait_ge(mixed, NT // PIECE)

                @block.gpsimd
                def _(pool):
                    if not last:
                        for m in stack_space[0:2]:
                            pool.memset(m, 0.0)
                        for v in Vp:
                            pool.memset(v, 0.0)
                        pool.drain().then_inc(cleared, 1)
                        pool.wait_ge(cleared, 2)
                        for k_ in ks:
                            ins = pool.memset(k_[MROW:MROW + 3, :, :], 1.0)
                        ins.then_inc(cleared, 1)
                        pool.wait_ge(cleared, 3)
                        for v in Vp:
                            ins = pool.memset(v[:, :, :, HD:HD + 1], 1.0)
                        ins.then_inc(cleared, 1)
                        pool.wait_ge(cleared, 4)

                @block.scalar
                def _(act):
                    for j in range(0, NT, PIECE):
                        act.dma_start(rows[1][:, j:j + PIECE, :], by_choice[1][:, j:j + PIECE, :])\
                           .then_inc(got[j // PIECE], 16)

                @block.sync
                def _(sp):
                    for j in range(0, NT, PIECE):
                        sp.dma_start(rows[0][:, j:j + PIECE, :], by_choice[0][:, j:j + PIECE, :])\
                          .then_inc(got[j // PIECE], 16)
                    if last:
                        for g in range(NT // PIECE):
                            sp.wait_ge(mixed, g + 1)
                            sp.dma_start(outv[:, g * PIECE:(g + 1) * PIECE, :], X[:, g * PIECE:(g + 1) * PIECE, :])\
                              .then_inc(stored, 16)
                        sp.wait_ge(stored, 16 * (NT // PIECE))

        PART_Q, PART_K = (0, 0, 1, 1, 0, 2), (0, 1, 0, 1, 2, 0)
        MROW = 64
        KB = B // P
        flat = "p s b -> p (s b)"
        stack_space = [prodQ[0][:, :, :], prodQ[1][:, :, :], H2[:, :, :].rearrange("p n f -> p (n f)")
                       .rearrange("p (s b) -> p s b", s=S)]
        qs, ks = ([m.rearrange(flat)[:, w * 2048:(w + 1) * 2048].bitcast(BF16)
                   .rearrange("p (h t) -> p h t", h=HEADS) for m in stack_space] for w in range(2))
        PT = [prodV[i // 2][:, :, :].rearrange(flat)[:, (i % 2) * 1024:(i % 2 + 1) * 1024]
              .rearrange("p (j c) -> p j c", j=2) for i in range(4)]
        Vp = [qT[:, 4 * i:4 * i + 4, :].rearrange(flat).rearrange("p (a h c) -> p a h c", a=KB, c=32)
              for i in range(3)]
        parts = [[kT[:, 3 * (2 * w + i):3 * (2 * w + i) + 3, :].rearrange(flat).bitcast(BF16)
                  .rearrange("p (c n) -> p c n", c=3) for i in range(2)] for w in range(2)]
        rest = [[m[:, 4 * w:4 * w + 4, :].rearrange(flat) for m in prodV] for w in range(2)]
        sums = [kT[:, i, :] for i in range(2)]
        heads_out = [kT[:, i, :].rearrange("p (a f) -> p a f", a=KB) for i in (2, 6, 13)]
        heads_outT = kT[:, 14, :]
        mx3 = kT[:, 12, 0:3 * HEADS].rearrange("p (h c) -> p h c", c=3)
        negm = kT[:, 15, 0:KB * HEADS].rearrange("p (a h) -> p a h", a=KB)
        rec = kT[:, 7, 0:KB * 4].rearrange("p (a j) -> p a j", a=KB)
        m_rest = [qT[0:HEADS, 12 + i, :] for i in range(2)]
        m_parts = qT[0:HEADS, 14:16, :].rearrange(flat).bitcast(BF16)[:, 0:3 * B].rearrange("p (c t) -> p c t", c=3)

        def attention_half():
            def sm(name):
                return sem(f"at_{name}")

            grow, shift = tiny[0], tiny[1]
            class At:
                def __init__(self, i, c):
                    self.i, self.c = i, c
                    self.b, self.v, self.turn = i * 3 + c, c % 3, i + c // 3

                def next(self, k=1):
                    return At(self.i, self.c + k)

            PERB = 13 * 16
            stack_in = [sm(f"stack_in{u}") for u in range(3)]

            def load(sp, at, rows=range(6), zero=True):
                for r in rows:
                    for stack, src, p_ in ((qs, q_parts, PART_Q), (ks, k_parts, PART_K)):
                        sp.dma_start(stack[at.v][HD * r:HD * (r + 1), :, :],
                                     src[bass.ds(at.b, 1), p_[r], :, :]
                                     .rearrange("a (h d) t -> d (a h) t", d=HD)).then_inc(stack_in[at.v], 16)
                if zero:
                    sp.dma_start(qs[at.v][MROW:MROW + 3, :, :].rearrange("p h t -> p (h t)"), zero_rows)\
                      .then_inc(stack_in[at.v], 16)

            s_ps, s_max, m_ready = begun = [sm(n) for n in ("s_ps", "s_max", "m_ready")]
            s_bank = [banks[0], banks[1]]

            def scores(pe, at, h):
                n = at.b * HEADS + h
                ps, q, k = s_bank[h % 2], qs[at.v][:, h, :], ks[at.v][:, h, :]
                if h == 0:
                    pe.wait_ge(stack_in[at.v], (at.turn + 1) * PERB)
                pe.wait_ge(s_max, done(n - 2))
                pe.matmul(ps[:, 0:2 * P], identb[:, :], causal[:, :], start=True, stop=False,
                          skip_group_check=True)
                pe.matmul(ps[:, 0:P], q[:, 0:P], k[:, 0:P], start=False, stop=False, skip_group_check=True)
                pe.matmul(ps[:, P:2 * P], q[:, P:2 * P], k[:, P:2 * P], start=False, stop=False,
                          skip_group_check=True)
                pe.matmul(ps[:, 2 * P:3 * P], q[:, P:2 * P], k[:, 0:P], start=False, stop=True,
                          skip_group_check=True).then_inc(s_ps, 1)

            def maxima(dve, b, h):
                n = b * HEADS + h
                if h == 0:
                    dve.wait_ge(m_ready, done(b - 1))
                dve.wait_ge(s_ps, done(n))
                dve.tensor_reduce(mx3[:, h, :], s_bank[h % 2][:, 0:3 * P].rearrange("p (c t) -> p c t", c=3),
                                  AX.X, ALU.max, negate=True).then_inc(s_max, 1)

            def combine(dve, b):
                dve.wait_ge(s_max, done(b * HEADS + (HEADS - 1)))
                dve.tensor_copy(negm[:, 0, :], mx3[:, :, 0])
                dve.tensor_tensor(negm[:, 1, :], mx3[:, :, 1], mx3[:, :, 2], ALU.min).then_inc(m_ready, 1)

            G = NT // 4
            z_ready, zT_ps, zT_ready, qk_ps, hi_ready, rest_ready, mid_ready, lo_ready, v_ps, v_copied, \
                parts_out = credited = [sm(n) for n in (
                    "z_ready", "zT_ps", "zT_ready", "qk_ps", "hi_ready", "rest_ready", "mid_ready", "lo_ready",
                    "v_ps", "v_copied", "parts_out")]
            coef, q_out, k_out, counted_groups = sm("coef"), sm("q_out"), sm("k_out"), sm("counted_groups")
            ln_own = sm("ln_own")
            pz = [banks[0], banks[1]]
            pqk, pv = st_ps, [banks[2], banks[3]]
            with nc.Block() as block:
                @block.sync
                def _(sp):
                    for c in credited + begun:
                        sp.sem_inc(c, CREDIT)

                    def send(i, u, wait=True):
                        n = i * 2 + u
                        sp.wait_ge(lo_ready, done(n))
                        for w, (dst, s_) in enumerate(((q_parts, q_out), (k_parts, k_out))):
                            for b in range(2):
                                sp.dma_start(dst[bass.ds(i * 4 + (2 * u + b), 1), :, :, :]
                                             .rearrange("a c f t -> f (a c) t"),
                                             parts[w][u][:, :, b * B:(b + 1) * B]).then_inc(s_, 16)
                        if wait:
                            sp.wait_ge(q_out, n * 32 + 32)
                            sp.wait_ge(k_out, n * 32 + 32)
                            sp.sem_inc(parts_out, 1)

                    send(0, 0)
                    assert G == 8
                    for n in range(1, G - 1):
                        send(n // 2, n % 2)
                        at, third = At(0, (n - 1) // 3), (n - 1) % 3
                        load(sp, at, (2 * third, 2 * third + 1), zero=third == 2)
                    send(G // 2 - 1, 1, wait=False)

                @block.vector
                def _(dve):
                    input_norm(dve, ln_own)
                    dve.tensor_scalar(grow[:, :], r0[:, :], 1.0, None, ALU.add)
                    dve.scalar_tensor_tensor(shift[:, :], mean[:, :], -1.0, r0[:, :], ALU.mult, ALU.mult)\
                       .then_inc(coef, 1)
                    dve.wait_ge(coef, 1)

                    def normalise(n, u):
                        dve.wait_ge(zT_ps, done(n - 2))
                        for k in range(4):
                            j = n * 4 + k
                            ins = dve.tensor_scalar(stageZ[u][:, k, :], X[:, bass.ds(j, 1), :],
                                                    mean[:, bass.ds(j, 1)], r01[:, bass.ds(j, 1)],
                                                    ALU.subtract, ALU.mult)
                        ins.then_inc(z_ready, 1)
                        for k in range(4):
                            j = n * 4 + k
                            dve.tensor_scalar(X[:, bass.ds(j, 1), :], X[:, bass.ds(j, 1), :],
                                              grow[:, bass.ds(j, 1)], shift[:, bass.ds(j, 1)],
                                              ALU.mult, ALU.add)

                    def leave_rest(n, u):
                        dve.wait_ge(hi_ready, done(n))
                        dve.wait_ge(lo_ready, done(n - 2))
                        for w in range(2):
                            ins = dve.tensor_tensor(rest[w][u], pqk[u][:, w, :], parts[w][u][:, 0, :], ALU.subtract)
                        ins.then_inc(rest_ready, 1)

                    ahead_of(dve, G, normalise, leave_rest, by=2)
                    for h in range(HEADS):
                        maxima(dve, 0, h)
                    combine(dve, 0)

                @block.gpsimd
                def _(pool):
                    with pool.Fori(0, G // 2) as i:
                        for u in range(2):
                            n = i * 2 + u
                            pool.wait_ge(mid_ready, done(n))
                            pool.sem_inc(counted_groups, 1)
                            for w in range(2):
                                ins = pool.tensor_tensor(parts[w][u][:, 2, :], rest[w][u], parts[w][u][:, 1, :],
                                                         ALU.subtract)
                            ins.then_inc(lo_ready, 1)

                @block.tensor
                def _(pe):
                    def turn(n, u):
                        pe.wait_ge(z_ready, done(n))
                        pe.wait_ge(zT_ready, done(n - 2))
                        for k in range(4):
                            ins = pe.transpose(pz[u][:, k * P:(k + 1) * P], stageZ[u][:, k, :], ident[:, :])
                        ins.then_inc(zT_ps, 1)

                    def project(n, u):
                        pe.wait_ge(zT_ready, done(n))
                        pe.wait_ge(rest_ready, done(n - 2))
                        pe.matmul(pqk[u][:, 0, :], Wqa[:, :], stageT[u][:, :], start=True, stop=True)
                        pe.matmul(pqk[u][:, 1, :], Wka[:, :], stageT[u][:, :], start=True, stop=True).then_inc(qk_ps, 1)
                        pe.wait_ge(v_copied, done(n - 2))
                        for k in range(4):
                            ins = pe.matmul(pv[u][:, k * P:(k + 1) * P], stageT[u][:, k * P:(k + 1) * P],
                                            Wva[:, :], start=True, stop=True)
                        ins.then_inc(v_ps, 1)

                    ahead_of(pe, G, turn, project)
                    for h in range(HEADS):
                        scores(pe, At(0, 0), h)

                @block.scalar
                def _(act):
                    def scale(n, u):
                        act.wait_ge(zT_ps, done(n))
                        act.wait_ge(v_ps, done(n - 2))
                        act.activation(stageT[u][:, :], pz[u][:, :], ACT.Identity, bias=lnp[:, 5:6],
                                       scale=lnp[:, 4:5]).then_inc(zT_ready, 1)

                    def high_parts(n, u):
                        act.wait_ge(qk_ps, done(n))
                        act.wait_ge(parts_out, done(n - 2))
                        for w in range(2):
                            ins = act.activation(parts[w][u][:, 0, :], pqk[u][:, w, :], ACT.Copy)
                        ins.then_inc(hi_ready, 1)
                        act.wait_ge(v_ps, done(n))
                        act.activation(V[:, bass.ds(n * 4, 4), :],
                                       pv[u][:, :].rearrange("p (k f) -> p k f", k=4), ACT.Copy)\
                           .then_inc(v_copied, 1)
                        act.wait_ge(rest_ready, done(n))
                        for w in range(2):
                            ins = act.activation(parts[w][u][:, 1, :], rest[w][u], ACT.Copy)
                        ins.then_inc(mid_ready, 1)

                    ahead_of(act, G, scale, high_parts)

            PAIRS = HEADS // 2
            LAG = 2

            def maxima_at(at, pr):
                of, h = (at.next(), HEADS // 2 + 2 * pr) if pr < PAIRS // 2 else (at.next(2), 2 * pr - HEADS // 2)
                return [(of, h), (of, h + 1)] if exists(of) else []

            counted = sm("counted")
            m_in = [sm(f"m_in{u}") for u in range(3)]
            mp_ready, st_done, exp_done, masked, pv_done, sums_copied, vp_ready, \
                shared_ps, shared_free, heads_done, outT_ready, rec_ready, dve_own = credited = [sm(n) for n in (
                    "mp_ready", "st_done", "exp_done", "masked", "pv_done",
                    "sums_copied", "vp_ready", "shared_ps", "shared_free", "heads_done", "outT_ready",
                    "rec_ready", "dve_own")]
            pv_bank, shared = banks[2], banks[3]

            SUM2, SUM3, TURN, MAXIMA, OUT, SUM0, SUM1 = range(7)

            def use(b, k):
                if k == MAXIMA and isinstance(b, int) and b == 0:
                    return 1
                return b * 7 + (k - 3)

            def sum_use(b, g):
                return use(b, SUM0 + g) if g < 2 else use(b + 1, SUM2 + g - 2)

            def exists(at):
                return not isinstance(at.b, int) or at.b < S

            def all_sequences(engine, sequence):
                sequence(At(0, 0), True, False)
                with engine.Fori(0, (S - 4) // 3) as i:
                    for c in range(1, 4):
                        sequence(At(i, c), False, False)
                for b in range(S - 3, S):
                    sequence(At(0, b), False, b == S - 1)

            with nc.Block() as block:
                @block.sync
                def _(sp):
                    for c in credited:
                        sp.sem_inc(c, CREDIT)

                    def send_maxima(at):
                        sp.wait_ge(mp_ready, done(at.b))
                        for c in range(3):
                            sp.dma_start(qs[at.v][MROW + c:MROW + c + 1, :, :], m_parts[:, c:c + 1, :])\
                              .then_inc(m_in[at.v], 16)

                    def sequence(at, first, last):
                        if exists(at.next(2)):
                            sp.wait_ge(st_done, done(at.b * PAIRS - 1))
                            load(sp, at.next(2))
                        if not last:
                            send_maxima(at.next())

                    sp.wait_ge(q_out, G * 32)
                    sp.wait_ge(k_out, G * 32)
                    send_maxima(At(0, 0))
                    all_sequences(sp, sequence)

                @block.gpsimd
                def _(pool):
                    def wait_count(s_, value):
                        pool.wait_ge(s_, value)
                        pool.sem_inc(counted, 1)

                    def spread_v(at):
                        wait_count(pv_done, done((at.b - 2) * PAIRS - 1))
                        for a in range(KB):
                            ins = pool.tensor_copy(Vp[at.v][:, a, :, 0:HD],
                                                   V[:, bass.ds(at.b * KB + a, 1), :]
                                                   .rearrange("p a (h d) -> p (a h) d", d=HD))
                        ins.then_inc(vp_ready, 1)

                    def sequence(at, first, last):
                        for pr in range(PAIRS):
                            wait_count(exp_done, done(at.b * PAIRS + pr))
                            diag = PT[pr % 4].rearrange("p j (c s) -> p (j c) s", s=P)[:, 0:8:2, :]
                            pool.affine_select(out=diag, in_=diag, compare_op=ALU.is_ge, fill=0.0, base=0,
                                               pattern=[[0, 4], [1, P]], channel_multiplier=-1)\
                                .then_inc(masked, 1)
                            if pr == 3 and not last:
                                spread_v(at.next())

                    spread_v(At(0, 0))
                    all_sequences(pool, sequence)

                @block.tensor
                def _(pe):
                    def maxima_rows(b, n):
                        pe.wait_ge(m_ready, done(b))
                        pe.wait_ge(shared_free, done(n - 1))
                        for a in range(KB):
                            ins = pe.transpose(shared[0:HEADS, a * P:(a + 1) * P], negm[:, a, :], ident[:, :])
                        ins.then_inc(shared_ps, 1)

                    def scores_t(at, pr):
                        n = at.b * PAIRS + pr
                        if pr == 0:
                            pe.wait_ge(m_in[at.v], at.turn * 48 + 48)
                        pe.wait_ge(exp_done, done(n - 2))
                        for j in range(2):
                            h = 2 * pr + j
                            ps, q, k = st_ps[pr % 2][:, j, :], qs[at.v][:, h, :], ks[at.v][:, h, :]
                            pe.matmul(ps[:, 0:B], k[:, 0:P], q, start=True, stop=True)
                            ins = pe.matmul(ps[:, B:B + P], k[:, P:2 * P], q[:, P:2 * P], start=True, stop=True)
                        ins.then_inc(st_done, 1)

                    def weighted_sum(at, pr):
                        n = at.b * PAIRS + pr
                        pe.wait_ge(masked, done(n))
                        if pr == 0:
                            pe.wait_ge(vp_ready, done(at.b))
                        if pr % 2 == 0:
                            pe.wait_ge(sums_copied, done(at.b * 4 + (pr // 2 - 1)))
                        for j in range(2):
                            h = 2 * pr + j
                            o = pv_bank[32 * (h % 4):32 * (h % 4) + 32, 0:B]
                            pe.matmul(o, Vp[at.v][:, 0, h, :], PT[pr % 4][:, j, 0:B], start=True, stop=False)
                            ins = pe.matmul(o[:, P:B], Vp[at.v][:, 1, h, :], PT[pr % 4][:, j, B:B + P],
                                            start=False, stop=True)
                        ins.then_inc(pv_done, 1)

                    def sums_to_tokens(at, g, skipped=0):
                        pe.wait_ge(sums_copied, done(at.b * 4 + g))
                        pe.wait_ge(shared_free, done(sum_use(at.b, g) - 1 - skipped))
                        for a in range(KB):
                            ins = pe.transpose(shared[:, a * P:(a + 1) * P], sums[g % 2][:, a * P:(a + 1) * P],
                                               ident[:, :])
                        ins.then_inc(shared_ps, 1)

                    def turn_heads(at, skipped=0):
                        pe.wait_ge(heads_done, done(at.b * 4 + 3))
                        pe.wait_ge(shared_free, done(use(at.b + 1, TURN) - 1 - skipped))
                        for a in range(KB):
                            ins = pe.transpose(shared[:, a * P:(a + 1) * P], heads_out[at.v][:, a, :], ident[:, :])
                        ins.then_inc(shared_ps, 1)

                    def project(at, skipped=0):
                        pe.wait_ge(outT_ready, done(at.b))
                        pe.wait_ge(shared_free, done(use(at.b + 1, OUT) - 1 - skipped))
                        for a in range(KB):
                            ins = pe.matmul(shared[:, a * P:(a + 1) * P], heads_outT[:, a * P:(a + 1) * P],
                                            Woa[:, :], start=True, stop=True)
                        ins.then_inc(shared_ps, 1)

                    def sequence(at, first, last):
                        before_, next_ = at.next(-1), at.next()
                        for pr in range(PAIRS):
                            todo = maxima_at(at, pr)
                            scores_t(at, pr)
                            if todo:
                                scores(pe, *todo.pop(0))
                            if not first:
                                if pr == 0:
                                    sums_to_tokens(before_, 2)
                                if pr == 2:
                                    sums_to_tokens(before_, 3)
                                if pr == 3:
                                    turn_heads(before_)
                            if pr == 4 and not last:
                                maxima_rows(next_.b, use(at.b, MAXIMA))
                            if pr == 5 and not first:
                                project(before_, last)
                            if pr == 6:
                                sums_to_tokens(at, 0, last)
                            if pr == 7:
                                sums_to_tokens(at, 1, last)
                            if pr >= LAG:
                                weighted_sum(at, pr - LAG)
                            elif not first:
                                weighted_sum(before_, PAIRS + pr - LAG)
                            if todo:
                                scores(pe, *todo.pop(0))

                    maxima_rows(0, 0)
                    for h in range(HEADS // 2):
                        scores(pe, At(0, 1), h)
                    all_sequences(pe, sequence)
                    at = At(0, S - 1)
                    weighted_sum(at, PAIRS - 2)
                    sums_to_tokens(at, 2, 1)
                    weighted_sum(at, PAIRS - 1)
                    sums_to_tokens(at, 3, 1)
                    turn_heads(at, 1)
                    project(at, 2)

                @block.scalar
                def _(act):
                    def copy_sums(at, g, skipped=0):
                        act.wait_ge(pv_done, done(at.b * PAIRS + (2 * g + 1)))
                        act.wait_ge(shared_ps, done(sum_use(at.b, g - 2) - skipped if g >= 2
                                                 else sum_use(at.b - 1, g + 2)))
                        act.activation(sums[g % 2], pv_bank[:, 0:B], ACT.Copy).then_inc(sums_copied, 1)

                    def copy_heads(at, skipped=0):
                        act.wait_ge(shared_ps, done(use(at.b + 1, TURN) - skipped))
                        act.activation(heads_outT, shared[:, 0:B], ACT.Copy).then_inc(shared_free, 1)
                        act.wait_ge(shared_free, done(use(at.b + 1, TURN) - skipped))
                        act.sem_inc(outT_ready, 1)

                    def sequence(at, first, last):
                        for pr in range(PAIRS):
                            n = at.b * PAIRS + pr
                            act.wait_ge(st_done, done(n))
                            act.wait_ge(pv_done, done(n - 4))
                            act.activation(PT[pr % 4][:, :, 0:3 * P], st_ps[pr % 2][:, :, 0:3 * P], ACT.Exp,
                                           scale=SCALE).then_inc(exp_done, 1)
                            if pr == 1 and not first:
                                copy_sums(at.next(-1), 3)
                            if pr == 3 and not first:
                                copy_heads(at.next(-1))
                            if pr in (3, 5, 7):
                                copy_sums(at, (pr - 3) // 2, last)

                    all_sequences(act, sequence)
                    copy_sums(At(0, S - 1), 3, 1)
                    copy_heads(At(0, S - 1), 1)

                @block.vector
                def _(dve):
                    def split_maxima(at, n):
                        dve.wait_ge(shared_ps, done(n))
                        src = shared[0:HEADS, 0:B]
                        if at.c:
                            last_ = at.next(-1)
                            dve.wait_ge(m_in[last_.v], last_.turn * 48 + 48)
                        own = at.b * 2
                        dve.tensor_copy(m_parts[:, 0, :], src).then_inc(dve_own, 1)
                        dve.wait_ge(dve_own, done(own))
                        dve.tensor_tensor(m_rest[0], src, m_parts[:, 0, :], ALU.subtract).then_inc(shared_free, 1)
                        dve.wait_ge(shared_free, done(n))
                        dve.tensor_copy(m_parts[:, 1, :], m_rest[0]).then_inc(dve_own, 1)
                        dve.wait_ge(dve_own, done(own + 1))
                        dve.tensor_tensor(m_parts[:, 2, :], m_rest[0], m_parts[:, 1, :], ALU.subtract)\
                           .then_inc(mp_ready, 1)

                    def normalise(at, g, skipped=0):
                        dve.wait_ge(shared_ps, done(sum_use(at.b, g) - skipped))
                        src = shared[:, 0:B].rearrange("p (a j c) -> p a j c", a=KB, c=32)
                        dve.reciprocal(rec, src[:, :, :, HD]).then_inc(rec_ready, 1)
                        dve.wait_ge(rec_ready, done(at.b * 4 + g))
                        out_ = heads_out[at.v][:, :, 32 * g:32 * g + 32].rearrange("p a (j d) -> p a j d", d=HD)
                        dve.tensor_tensor(out_, src[:, :, :, 0:HD], bcast(rec, 3, HD), ALU.mult)\
                           .then_inc(heads_done, 1)
                        dve.wait_ge(heads_done, done(at.b * 4 + g))
                        dve.sem_inc(shared_free, 1)

                    def add(at, skipped=0):
                        dve.wait_ge(shared_ps, done(use(at.b + 1, OUT) - skipped))
                        xb = X[:, bass.ds(at.b * KB, KB), :]
                        dve.tensor_tensor(xb, xb, shared[:, 0:B].rearrange("p (a f) -> p a f", a=KB), ALU.add)\
                           .then_inc(shared_free, 1)
                        dve.wait_ge(shared_free, done(use(at.b + 1, OUT) - skipped))
                        for a in range(KB):
                            dve.bn_stats(stats[:, bass.ds(at.b * KB + a, 1), :], X[:, bass.ds(at.b * KB + a, 1), :])

                    def sequence(at, first, last):
                        before_, next_ = at.next(-1), at.next()
                        for pr in range(PAIRS):
                            todo = maxima_at(at, pr)
                            if todo:
                                maxima(dve, todo[0][0].b, todo[0][1])
                            if not first:
                                if pr == 0:
                                    normalise(before_, 2)
                                if pr == 2:
                                    normalise(before_, 3)
                            if pr == 4 and not last:
                                split_maxima(next_, use(at.b, MAXIMA))
                            if pr == 5 and not first:
                                add(before_, last)
                            if pr == 6:
                                normalise(at, 0, last)
                            if pr == 7:
                                normalise(at, 1, last)
                            if todo:
                                maxima(dve, todo[1][0].b, todo[1][1])
                            if pr == 3 and not last:
                                combine(dve, next_.b)

                    split_maxima(At(0, 0), 0)
                    for h in range(HEADS // 2):
                        maxima(dve, 1, h)
                    all_sequences(dve, sequence)
                    at = At(0, S - 1)
                    normalise(at, 2, 1)
                    normalise(at, 3, 1)
                    add(at, 2)

            if stages == 2:
                stored = sm("stored")
                with nc.Block() as block:
                    @block.sync
                    def _(sp):
                        sp.dma_start(outv, X[:, :, :]).then_inc(stored, 16)
                        sp.wait_ge(stored, 16)

        ffn_half(0, stages == 1)
        if stages >= 2:
            recycle_semaphores()
            attention_half()
        if stages >= 3:
            recycle_semaphores()
            ffn_half(1, True)


_INS = ["L0_attn_x", "L0_attn_ln_w", "L0_attn_ln_b", "L0_attn_wq", "L0_attn_wk", "L0_attn_wv", "L0_attn_wo",
        "L0_ffn_ln1_weight", "L0_ffn_ln1_bias", "L0_ffn_ln2_weight", "L0_ffn_ln2_bias", "L0_ffn_qkv_weight",
        "L0_ffn_proj_weight", "L0_ffn_router_weight", "L0_ffn_moe_w1", "L0_ffn_moe_w2"]
_OUTS = [((16, 256, 128), "float32")]


def kernel(**inputs):
    import numpy as _np
    import concourse.bacc as _bacc
    from concourse import mybir as _mybir
    from concourse.bass_utils import run_bass_kernel_spmd as _run

    nc = _bacc.Bacc("TRN2", target_bir_lowering=False, num_devices=1)
    arrays, args = {}, []
    for name in _INS:
        a = _np.ascontiguousarray(inputs[name])
        arrays[f"in_{name}_dram"] = a
        args.append(nc.dram_tensor(f"in_{name}_dram", a.shape, _mybir.dt.from_np(a.dtype), kind="ExternalInput").ap())
    for i, (shape, dtype) in enumerate(_OUTS):
        dt = _mybir.dt.from_np(_np.dtype(dtype))
        args.append(nc.dram_tensor(f"out_{i}_dram", shape, dt, kind="ExternalOutput").ap())
    macaron_kernel(nc, *args)
    r = _run(nc, [arrays], core_ids=[0])
    got = tuple(r.results[0][f"out_{i}_dram"] for i in range(len(_OUTS)))
    return got[0]
```
